# Optimizing a Trainium2 kernel written in Bass

```python
import numpy as np
import jax
import jax.numpy as jnp

def _softmax(x, axis=-1):
    return jax.nn.softmax(x, axis=axis)

def _gelu(x):
    return jax.nn.gelu(x, approximate=True)

def _silu(x):
    return jax.nn.silu(x)

def _sigmoid(x):
    return jax.nn.sigmoid(x)

def _layernorm(x, axis=-1, eps=1e-05):
    m = jnp.mean(x, axis=axis, keepdims=True)
    v = jnp.var(x, axis=axis, keepdims=True)
    return (x - m) / jnp.sqrt(v + eps)

def _scatter_add(tgt, idx, src, axis=0):
    return tgt.at[idx].add(src)

def _segment_sum(src, seg, n):
    return jax.ops.segment_sum(src, seg, n)
kernel_name = 'mk_flamingo_gated_d1_seqx_r2_72094f'

def setup_inputs(seed: int=0):
    np.random.seed(seed)
    _w = jnp.asarray

    def _rec_inputs():
        import jax
        import jax.numpy as jnp
        _rk = jax.random.key(seed)
        x = -0.0002928 + 1 * jax.random.normal(jax.random.fold_in(_rk, 1), (8, 512, 512), jnp.float32)
        _lenS = 512 - jax.random.randint(jax.random.fold_in(_rk, 7), (8,), 0, max(1, 512 // 4) + 1, jnp.int32)
        _lenS2 = 120 - jax.random.randint(jax.random.fold_in(_rk, 8), (8,), 0, max(1, 120 // 4) + 1, jnp.int32)
        _ctx_1024P = jax.random.normal(jax.random.fold_in(_rk, 11), (8, 16, 512), jnp.float32)
        _ctx_1024c = jax.random.dirichlet(jax.random.fold_in(_rk, 511), 0.3 * jnp.ones((16,), jnp.float32), (8, 120))
        _ctx_1024t = jnp.einsum('bsk,bkd->bsd', _ctx_1024c, _ctx_1024P)
        _ctx_1024t = _ctx_1024t * jax.lax.rsqrt(jnp.mean(jnp.square(_ctx_1024t)) + 1e-12) * 0.953939
        ctx_1024 = -1.39393e-06 + 0.999914 * (_ctx_1024t + 0.3 * jax.random.normal(jax.random.fold_in(_rk, 611), (8, 120, 512), jnp.float32))
        _g = jax.random.normal(jax.random.fold_in(_rk, 9001), (2, 1), jnp.float32)
        _g = jnp.sign(_g) * jnp.maximum(jnp.abs(_g), 1.0) + (_g == 0) * 1.0
        g_xattn = _g[0]
        g_ffn = _g[1]
        return (x, ctx_1024, g_xattn, g_ffn)
    x, ctx_1024, g_xattn, g_ffn = _rec_inputs()

    def _L0_xattn_setup():
        import jax, jax.numpy as jnp
        import numpy as np
        D = 512
        H = 16
        E = 8
        DK = D // H
        B, S = (2, 1024)
        key = jax.random.key(seed)
        ks = jax.random.split(key, 16)
        sc = 1.0 / np.sqrt(D)
        inp = {'query': jax.random.normal(ks[0], (B, S, D), jnp.float32), 'key': jax.random.normal(ks[1], (B, S, D), jnp.float32), 'value': jax.random.normal(ks[2], (B, S, D), jnp.float32), 'Wq': jax.random.normal(ks[3], (D, D), jnp.float32) * sc, 'bq': jax.random.normal(ks[4], (D,), jnp.float32) * sc, 'Wk': jax.random.normal(ks[5], (D, D), jnp.float32) * sc, 'bk': jax.random.normal(ks[6], (D,), jnp.float32) * sc, 'Wv': jax.random.normal(ks[7], (D, D), jnp.float32) * sc, 'bv': jax.random.normal(ks[8], (D,), jnp.float32) * sc, 'We': jax.random.normal(ks[9], (E, D, D), jnp.float32) * sc, 'be': jax.random.normal(ks[10], (E, D), jnp.float32) * sc, 'Wo': jax.random.normal(ks[11], (D, D), jnp.float32) * sc, 'bo': jax.random.normal(ks[12], (D,), jnp.float32) * sc}
        return inp
    _L0_xattn_all = _L0_xattn_setup()
    _L0_xattn_in = {k: v for k, v in _L0_xattn_all.items() if k in ('Wq', 'bq', 'Wk', 'bk', 'Wv', 'bv', 'We', 'be', 'Wo', 'bo')}
    del _L0_xattn_all

    def _L0_ffn_setup():
        import jax, jax.numpy as jnp
        import numpy as np
        EXPERT_NUM = 8
        CAPACITY = 100
        key = jax.random.key(seed)
        k1, k2, k3 = jax.random.split(key, 3)
        B, S, H, E = (8, 1024, 512, EXPERT_NUM)
        x = jax.random.normal(k1, (B, S, H), dtype=jnp.float32)
        w_gate = jax.random.normal(k2, (H, E), dtype=jnp.float32) * 0.02
        w_expert = jax.random.normal(k3, (H, H), dtype=jnp.float32) * 0.02
        b_expert = jnp.zeros((H,), dtype=jnp.float32)
        return {'x': x, 'w_gate': w_gate, 'w_expert': w_expert, 'b_expert': b_expert}
    _L0_ffn_all = _L0_ffn_setup()
    _L0_ffn_in = {k: v for k, v in _L0_ffn_all.items() if k in ('w_gate', 'w_expert', 'b_expert')}
    del _L0_ffn_all
    return {'x': x, 'ctx_1024': ctx_1024, 'g_xattn': g_xattn, 'g_ffn': g_ffn, 'L0_xattn_Wq': _L0_xattn_in['Wq'], 'L0_xattn_bq': _L0_xattn_in['bq'], 'L0_xattn_Wk': _L0_xattn_in['Wk'], 'L0_xattn_bk': _L0_xattn_in['bk'], 'L0_xattn_Wv': _L0_xattn_in['Wv'], 'L0_xattn_bv': _L0_xattn_in['bv'], 'L0_xattn_We': _L0_xattn_in['We'], 'L0_xattn_be': _L0_xattn_in['be'], 'L0_xattn_Wo': _L0_xattn_in['Wo'], 'L0_xattn_bo': _L0_xattn_in['bo'], 'L0_ffn_w_gate': _L0_ffn_in['w_gate'], 'L0_ffn_w_expert': _L0_ffn_in['w_expert'], 'L0_ffn_b_expert': _L0_ffn_in['b_expert']}

def reference(x, ctx_1024, g_xattn, g_ffn, L0_xattn_Wq, L0_xattn_bq, L0_xattn_Wk, L0_xattn_bk, L0_xattn_Wv, L0_xattn_bv, L0_xattn_We, L0_xattn_be, L0_xattn_Wo, L0_xattn_bo, L0_ffn_w_gate, L0_ffn_w_expert, L0_ffn_b_expert):
    import jax
    import jax.numpy as jnp

    def _L0_xattn_ref(query, key, value, Wq, bq, Wk, bk, Wv, bv, We, be, Wo, bo):
        import jax, jax.numpy as jnp
        import numpy as np
        D = 512
        H = 16
        E = 8
        DK = D // H
        B, S = (2, 1024)
        b = query.shape[0]
        Q = (query @ Wq.T + bq).reshape(b, -1, H, DK).transpose(0, 2, 1, 3)
        K = (key @ Wk.T + bk).reshape(b, -1, H, DK).transpose(0, 2, 1, 3)
        V = (value @ Wv.T + bv).reshape(b, -1, H, DK).transpose(0, 2, 1, 3)
        scores = jnp.einsum('bhqd,bhkd->bhqk', Q, K) / jnp.sqrt(jnp.asarray(DK, Q.dtype))
        attn = jax.nn.softmax(scores, axis=-1)
        out = jnp.einsum('bhqk,bhkd->bhqd', attn, V)
        out = out.transpose(0, 2, 1, 3).reshape(b, -1, D)
        expert = jnp.einsum('bsd,eod->ebso', out, We) + be[:, None, None, :]
        expert = expert.mean(axis=0)
        return expert @ Wo.T + bo

    def _L0_ffn_ref(x, w_gate, w_expert, b_expert):
        import jax, jax.numpy as jnp
        import numpy as np
        EXPERT_NUM = 8
        CAPACITY = 100
        B, S, H = x.shape
        E, C = (EXPERT_NUM, CAPACITY)
        hs = x.reshape(-1, H)
        logits = hs @ w_gate
        probs = jax.nn.softmax(logits, axis=1)
        best = jnp.argmax(probs, axis=1)
        mask = jax.nn.one_hot(best, E, dtype=jnp.int32)
        gate = jnp.sum(probs * mask.astype(probs.dtype), axis=1)
        locations = jnp.cumsum(mask, axis=0) - 1
        mask = mask * (locations < C).astype(jnp.int32)
        loc_sum = jnp.sum(locations * mask, axis=1)
        new_gates = gate[:, None] * mask.astype(probs.dtype)
        loc_oh = jax.nn.one_hot(loc_sum, C, dtype=probs.dtype)
        combine = new_gates[:, :, None] * loc_oh[:, None, :]
        dispatch = (combine != 0).astype(hs.dtype)
        dispatched = jnp.einsum('tec,th->ech', dispatch, hs).reshape(E * C, H)
        expert_out = dispatched @ w_expert + b_expert
        combined = combine.reshape(-1, E * C) @ expert_out
        return combined.reshape(B, S, H)
    x = x + jnp.tanh(g_xattn[0]) * _L0_xattn_ref(_layernorm(x, axis=-1), ctx_1024, ctx_1024, L0_xattn_Wq, L0_xattn_bq, L0_xattn_Wk, L0_xattn_bk, L0_xattn_Wv, L0_xattn_bv, L0_xattn_We, L0_xattn_be, L0_xattn_Wo, L0_xattn_bo)
    x = x + jnp.tanh(g_ffn[0]) * _L0_ffn_ref(_layernorm(x, axis=-1), L0_ffn_w_gate, L0_ffn_w_expert, L0_ffn_b_expert)
    return x

_drawn_inputs = setup_inputs


def setup_inputs(seed=0):
    import zlib

    import numpy as np

    out = dict(_drawn_inputs(seed))
    spreads = {'L0_ffn_b_expert': (0.0, 0.8)}
    factors = {'L0_xattn_bq': 8.0,
     'L0_xattn_bk': 8.0,
     'L0_xattn_bv': 4.709,
     'L0_xattn_be': 4.279,
     'L0_ffn_w_gate': 3.606}
    for name, (base, spread) in spreads.items():
        noise = np.random.default_rng([zlib.crc32(name.encode()), seed]).standard_normal(out[name].shape)
        drawn = base * np.exp(spread * noise) if base else spread * noise
        out[name] = jnp.asarray(drawn.astype(out[name].dtype))
    for name, factor in factors.items():
        out[name] = (out[name] * factor).astype(out[name].dtype)
    return out
```

```python
from contextlib import ExitStack

import concourse.bass as bass
from concourse import mybir

F32 = mybir.dt.float32
F32R = mybir.dt.float32r
F16 = mybir.dt.float16
BF16 = mybir.dt.bfloat16
U32 = mybir.dt.uint32
ALU = mybir.AluOpType
ACT = mybir.ActivationFunctionType
AX = mybir.AxisListType

P = 128
B, S, D = 8, 512, 512
SK = 120
H, DK = 16, 32
NE = 8
CAP = 100
NT = S // P
NK = D // P
HJ = P // DK
HALF = B // 2
QK_SCALE = 16.0
SHIFT_UNIT = 1024.0
EPS = 1e-5
NX = 4
STACK = 3 * DK + 1
FAR = 1.0e6


def build(nc, x, ctx, g_xattn, g_ffn, Wq, bq, Wk, bk, Wv, bv, We, be, Wo, bo, w_gate, w_expert, b_expert, out):
    assert x.shape == (B, S, D) and ctx.shape == (B, SK, D) and H * DK == D
    x_rows = x.rearrange("b (t p) d -> b p t d", p=P)
    out_rows = out.rearrange("b (t p) d -> b p t d", p=P)
    out_flat = out.rearrange("b s d -> (b s) d")
    k_scratch = nc.dram_tensor("k_scratch", (B, 3 * DK, HJ, NK * SK), F16, kind="Internal").ap()

    with ExitStack() as st:
        def sb(name, shape, dt):
            return st.enter_context(nc.sbuf_tensor(name, shape, dt))

        def sem(name):
            return st.enter_context(nc.semaphore(name))

        xb = sb("xb", [P, NX, NT, D], F32)
        wqT_hi = sb("wqT_hi", [P, NK, D], F32R)
        wqT_lo = sb("wqT_lo", [P, NK, D], F32R)
        mixT_hi = sb("mixT_hi", [P, NK, D], F32R)
        mixT_lo = sb("mixT_lo", [P, NK, D], F32R)
        v_all = sb("v_all", [SK, B, D], F32)
        mix_bias = sb("mix_bias", [P, D], F32)
        ident = sb("ident", [P, P], F32)
        tri = sb("tri", [P, P], BF16)
        ones_bf = sb("ones_bf", [P, P], BF16)
        den_sel = sb("den_sel", [SK, NK, DK], F32)
        head_sel = sb("head_sel", [P, NK, P], F32R)
        gate_sum = sb("gate_sum", [P, NE], F32)
        wg = sb("wg", [P, NK, DK], F32)
        bias_rows = sb("bias_rows", [2 * NK, P], F32)
        bias_cols = sb("bias_cols", [P, 2 * NK], F32)
        gates = sb("gates", [P, 2], F32)
        tanh_g = sb("tanh_g", [P, 2], F32)
        mix_scale = sb("mix_scale", [P, 1], F32)
        neg_half = sb("neg_half", [P, NT], F32)
        t_half = sb("t_half", [CAP, NE], F32)
        ones_col = sb("ones_col", [P, 1], F32)
        place_iota = sb("place_iota", [P, CAP], F32)
        token_iota = sb("token_iota", [P, NT], F32)
        rank8 = sb("rank8", [P, NT, NE], F32)
        table = sb("table", [CAP, 2, NE], F32)
        base_cnt = sb("base_cnt", [P, 2, NT, NE], BF16)

        bn_raw = sb("bn_raw", [P, 2, NT, 6], F32)
        mv = sb("mv", [P, 3, NT, 2], F32)
        veps = sb("veps", [P, 3, NT], F32)
        rstd = sb("rstd", [P, 3, NT], F32)

        with ExitStack() as pro:
            def pb(name, shape, dt):
                return pro.enter_context(nc.sbuf_tensor(name, shape, dt))
            raw = [pb(f"raw{i}", [P, NK, D], F32) for i in range(4)]
            ctx_raw = pb("ctx_raw", [SK, B, D], F32)
            ctxT = pb("ctxT", [P, NK, B * SK], F32)
            wkT = pb("wkT", [P, NK, D], F32)
            wvT = pb("wvT", [P, NK, D], F32)
            woT = pb("woT", [P, NK, D], F32)
            w_sum = pb("w_sum", [P, NK, D], F32)
            k_hi = pb("k_hi", [P, B, NK, SK], F16)
            k_lo = pb("k_lo", [P, B, NK, SK], F16)
            be_sb = pb("be_sb", [NE, D], F32)
            bv_bc = pb("bv_bc", [SK, D], F32)
            bo_bc = pb("bo_bc", [P, D], F32)
            be_col = pb("be_col", [P, NK], F32)
        k_stack = sb("k_stack", [P, 2, HJ, NK * SK], F16)
        k_diag = sb("k_diag", [P, NK, HJ * SK], F16)
        xn = sb("xn", [P, 2, D], F32)
        xnT_hi = sb("xnT_hi", [P, NK, S], F32R)
        xnT_lo = sb("xnT_lo", [P, NK, S], F32R)
        q_hi = sb("q_hi", [P, NK, S], F16)
        q_lo = sb("q_lo", [P, NK, S], F16)
        q_stack = sb("q_stack", [P, HJ, NK, S], F16)
        probs = sb("probs", [SK, HJ, S], F32)
        attn = sb("attn", [P, NK, S], F32)
        rden = sb("rden", [P, S], F32)
        rden_hi = sb("rden_hi", [P, S], F32R)
        rden_lo = sb("rden_lo", [P, S], F32R)
        attn_hi = sb("attn_hi", [P, NK, S], F32R)
        attn_lo = sb("attn_lo", [P, NK, S], F32R)
        x2n = sb("x2n", [P, 2, D], F32)
        x2nT = sb("x2nT", [P, NK, S], F32)
        partT = sb("partT", [P, S], F32)
        neg_max = sb("neg_max", [P, NT, NK, HJ], F32)
        shift = sb("shift", [H, S], F16)
        l_max = sb("l_max", [P, NT], F32)
        l_sub = sb("l_sub", [P, NT, NE], F32)
        l_exp = sb("l_exp", [P, NT, NE], F32)
        ranked = sb("ranked", [P, NT, NE], F32)
        top_rank = sb("top_rank", [P, NT], F32)
        choice = sb("choice", [P, NT, NE], BF16)
        l_sum = sb("l_sum", [P, NT], F32)
        gate = sb("gate", [P, NT], F32)
        place_all = sb("place_all", [P, NT, NE], F32)
        place = sb("place", [P, NT], F32)
        place_hot = sb("place_hot", [P, NT, CAP], F32)
        token = sb("token", [P, NT], F32)
        entry = sb("entry", [P, NT, 2, NE], F32)
        rows = xb[0:CAP, 0:2, :, :].rearrange("p a t d -> p (a t) d")
        far = sb("far", [CAP, NE], F32)
        row_ix = sb("row_ix", [CAP, NE], U32)
        coef = sb("coef", [CAP, NE], F32)
        t_bn = sb("t_bn", [CAP, NE, 6], F32)
        t_mv = sb("t_mv", [CAP, NE, 2], F32)
        t_ve = sb("t_ve", [CAP, NE], F32)
        t_rstd = sb("t_rstd", [CAP, NE], F32)

        ps = st.enter_context(nc.psum_tensor("ps", [P, 8, 512], F32))
        quad = ps[:, 0:4, :]
        num_b, den_b, g0_b, g1_b = (ps[:, i, :] for i in range(4, 8))

        s_const = sem("s_const")
        s_bqk = sem("s_bqk")
        s_gates = sem("s_gates")
        s_set = sem("s_set")
        s_setv = sem("s_setv")
        s_tanh = sem("s_tanh")
        s_raw = [sem(f"s_raw{i}") for i in range(4)]
        s_ctx = [sem(f"s_ctx{i}") for i in range(2)]
        s_pt = sem("s_pt")
        s_pa = sem("s_pa")
        s_pv = sem("s_pv")
        s_ws = sem("s_ws")
        s_kst = sem("s_kst")
        s_x = [sem(f"s_xload{i}") for i in range(NX)]
        s_bn1 = sem("s_bn1")
        s_mv1 = sem("s_mv1")
        s_ve1 = sem("s_ve1")
        s_rs1 = sem("s_rs1")
        s_xn = sem("s_xn")
        s_xt = sem("s_xt")
        s_xhi = sem("s_xhi")
        s_xlo = sem("s_xlo")
        s_q = sem("s_q")
        s_qhi = sem("s_qhi")
        s_qlo = sem("s_qlo")
        s_ks = [sem(f"s_ks{i}") for i in range(2)]
        s_kd = sem("s_kd")
        s_ms = sem("s_ms")
        s_mx = sem("s_mx")
        s_mt = sem("s_mt")
        s_sh = sem("s_sh")
        s_rq = sem("s_rq")
        s_rsh = sem("s_rsh")
        s_sc = sem("s_sc")
        s_ex = sem("s_ex")
        s_val = sem("s_val")
        s_num = sem("s_num")
        s_rec = sem("s_rec")
        s_rhi = sem("s_rhi")
        s_rlo = sem("s_rlo")
        s_bc = sem("s_bc")
        s_at = sem("s_at")
        s_ahi = sem("s_ahi")
        s_alo = sem("s_alo")
        s_mix = sem("s_mix")
        s_xbias = sem("s_xbias")
        s_x1 = sem("s_x1")
        s_st = sem("s_st")
        s_bn2 = sem("s_bn2")
        s_mv2 = sem("s_mv2")
        s_ve2 = sem("s_ve2")
        s_rs2 = sem("s_rs2")
        s_x2n = sem("s_x2n")
        s_x2t = sem("s_x2t")
        s_x2e = sem("s_x2e")
        s_lp = sem("s_lp")
        s_lpe = sem("s_lpe")
        s_lg = sem("s_lg")
        s_lmax = sem("s_lmax")
        s_lsub = sem("s_lsub")
        s_lexp = sem("s_lexp")
        s_g = sem("s_g")
        s_ch = sem("s_ch")
        s_pl = sem("s_pl")
        s_plr = sem("s_plr")
        s_en = sem("s_en")
        s_tb = sem("s_tb")
        s_tab = sem("s_tab")
        s_tail = sem("s_tail")
        s_row = sem("s_row")
        s_clr = sem("s_clr")
        s_we = sem("s_we")
        s_wehi = sem("s_wehi")
        s_welo = sem("s_welo")
        s_ga = [sem(f"s_ga{e}") for e in range(NE)]
        s_tbn = sem("s_tbn")
        s_tmv = sem("s_tmv")
        s_tve = sem("s_tve")
        s_trs = sem("s_trs")
        s_txn = sem("s_txn")
        s_tt = sem("s_tt")
        s_thi = sem("s_thi")
        s_tlo = sem("s_tlo")
        s_tmm = sem("s_tmm")
        s_tb1 = sem("s_tb1")
        s_to = sem("s_to")
        s_sca = sem("s_sca")

        SET, SETV, N_CONST = 13, 15, 3 + NK

        units, made = [], {}

        def unit(name, pe, needs=(), act=None, dve=None):
            n_act = sum(u["act"] is not None for u in units) + (act is not None)
            n_dve = sum(u["dve"] is not None for u in units) + (dve is not None)
            done = ([(s_pa, n_act)] if act else []) + ([(s_pv, n_dve)] if dve else [])
            units.append(dict(pe=pe, needs=list(needs), act=act, dve=dve, done=done))
            made[name] = done

        def needs_of(*names):
            return [w for n in names for w in made[n]]

        def copy_evac(i, dst, view=lambda b: b, scale=None):
            if i % 2 == 0:
                return dict(act=lambda e, b: e.activation(dst, view(b), ACT.Copy, scale=scale or 1.0))
            if scale is None:
                return dict(dve=lambda e, b: e.tensor_copy(dst, view(b)))
            return dict(dve=lambda e, b: e.tensor_scalar(dst, view(b), scale, None, ALU.mult))

        def turn(src_of, n, cols, rows):
            def pe(e, b):
                for i in range(n):
                    ins = e.transpose(b[0:rows, i * cols:(i + 1) * cols], src_of(i), ident[0:cols, 0:cols])
                return ins
            return pe

        consts = [(s_set, 2)]

        unit("bias", turn(lambda i: bias_rows[:, :], 1, 2 * NK, P), consts + [(s_bqk, 16 * 2)],
             dve=lambda e, b: e.tensor_scalar(bias_cols[:, :], b[:, 0:2 * NK], QK_SCALE, None, ALU.mult))

        def ctx_units(half):
            for k in range(NK):
                unit(("ctxT", half, k),
                     turn(lambda i, k=k: ctx_raw[:, half * HALF + i, k * P:(k + 1) * P], HALF, SK, P),
                     consts + [(s_ctx[half], 16)],
                     **copy_evac(k, ctxT[:, k, half * HALF * SK:(half + 1) * HALF * SK], lambda b: b[:, 0:HALF * SK]))

        def weight_units(name, slot, dst, scale=None, pair=None):
            for k in range(NK):
                pe = turn(lambda i, k=k: raw[slot][:, i, k * P:(k + 1) * P], NK, P, P)
                if pair is None:
                    unit((name, k), pe, consts + [(s_raw[slot], 16)], **copy_evac(k, dst[:, k, :], scale=scale))
                else:
                    hi, lo = pair
                    unit((name, k), pe, consts + [(s_raw[slot], 16)],
                         act=lambda e, b, k=k: e.activation(hi[:, k, :], b, ACT.Copy, scale=scale),
                         dve=lambda e, b, k=k: e.scalar_tensor_tensor(
                             out=lo[:, k, :], in0=b, scalar=scale, in1=hi[:, k, :].bitcast(F32),
                             op0=ALU.mult, op1=ALU.subtract))

        def k_units(half):
            lo_b, hi_b = half * HALF, (half + 1) * HALF
            for g in range(NK):
                def pe(e, b, g=g):
                    for k in range(NK):
                        ins = e.matmul(b[:, 0:HALF * SK], wkT[:, k, g * P:(g + 1) * P],
                                       ctxT[:, k, lo_b * SK:hi_b * SK], start=(k == 0), stop=(k == NK - 1))
                    return ins
                unit(("k", half, g), pe,
                     needs_of(*[("wkT", k) for k in range(NK)], *[("ctxT", half, k) for k in range(NK)], "bias"),
                     act=lambda e, b, g=g: e.activation(
                         k_hi[:, lo_b:hi_b, g, :], b[:, 0:HALF * SK].rearrange("p (b s) -> p b s", s=SK),
                         ACT.Identity, bias=bias_cols[:, NK + g:NK + g + 1]),
                     dve=lambda e, b, g=g: e.scalar_tensor_tensor(
                         out=k_lo[:, lo_b:hi_b, g, :], in0=b[:, 0:HALF * SK].rearrange("p (b s) -> p b s", s=SK),
                         scalar=bias_cols[:, NK + g:NK + g + 1], in1=k_hi[:, lo_b:hi_b, g, :],
                         op0=ALU.add, op1=ALU.subtract))

        def v_unit(b_):
            def pe(e, b):
                for k in range(NK):
                    ins = e.matmul(b[0:SK, :], ctxT[:, k, b_ * SK:(b_ + 1) * SK], wvT[:, k, :],
                                   start=(k == 0), stop=(k == NK - 1))
                return ins
            unit(("v", b_), pe,
                 needs_of(*[("wvT", k) for k in range(NK)], *[("ctxT", b_ // HALF, k) for k in range(NK)]) + [(s_const, 16 * N_CONST)],
                 dve=lambda e, b: e.tensor_tensor(v_all[:, b_, :], b[0:SK, :], bv_bc[:, :], ALU.add))

        def mix_units():
            def col(e, b):
                for k in range(NK):
                    ins = e.matmul(b[:, k:k + 1], be_sb[:, k * P:(k + 1) * P], ones_col[0:NE, :],
                                   start=True, stop=True)
                return ins
            unit("be_col", col, [(s_const, 16 * N_CONST), (s_set, 4)],
                 dve=lambda e, b: e.tensor_scalar(be_col[:, :], b[:, 0:NK], 1.0 / NE, None, ALU.mult))

            def row(e, b):
                for k in range(NK):
                    ins = e.matmul(b[:, :], be_col[:, k:k + 1].to_broadcast([P, P]), woT[:, k, :],
                                   start=(k == 0), stop=(k == NK - 1))
                return ins
            unit("mix_bias", row, needs_of("be_col", *[("woT", k) for k in range(NK)]) + [(s_const, 16 * N_CONST)],
                 dve=lambda e, b: e.tensor_tensor(mix_bias[:, :], b[:, :], bo_bc[:, :], ALU.add))
            for k in range(NK):
                def pe(e, b, k=k):
                    for o in range(NK):
                        ins = e.matmul(b[:, :], w_sum[:, o, k * P:(k + 1) * P], woT[:, o, :],
                                       start=(o == 0), stop=(o == NK - 1))
                    return ins
                unit(("mix", k), pe, needs_of(*[("woT", o) for o in range(NK)]) + [(s_ws, NE - 1)],
                     act=lambda e, b, k=k: e.activation(mixT_hi[:, k, :], b, ACT.Copy, scale=mix_scale[:, 0:1]),
                     dve=lambda e, b, k=k: e.scalar_tensor_tensor(
                         out=mixT_lo[:, k, :], in0=b, scalar=mix_scale[:, 0:1], in1=mixT_hi[:, k, :].bitcast(F32),
                         op0=ALU.mult, op1=ALU.subtract))

        weight_units("wkT", 0, wkT, scale=QK_SCALE)
        ctx_units(0)
        k_units(0)
        ctx_units(1)
        k_units(1)
        weight_units("wvT", 1, wvT)
        for b_ in range(B):
            v_unit(b_)
        weight_units("wqT", 2, None, scale=QK_SCALE, pair=(wqT_hi, wqT_lo))
        weight_units("woT", 3, woT)
        mix_units()
        N_ACT = sum(u["act"] is not None for u in units)
        N_DVE = sum(u["dve"] is not None for u in units)
        last_turn = {n: 1 + max(i for i, u in enumerate(units) if u["done"] == made[(n, NK - 1)])
                     for n in ("wkT", "wvT", "wqT")}
        last_k = {h: made[("k", h, NK - 1)] for h in range(2)}

        def prologue_over(e):
            e.wait_ge(s_pa, N_ACT)
            e.wait_ge(s_pv, N_DVE)
            e.wait_ge(s_kst, 16 * 2 * 3 * HJ)

        def rounds():
            return range(-1, B + 2)

        def ok(b):
            return 0 <= b < B

        block = st.enter_context(nc.Block())

        @block.sync
        def _(e):
            def load(dst, src, s):
                e.dma_start(dst, src).then_inc(s, 16)

            def w_view(w):
                return w.rearrange("(t p) d -> p t d", p=P)

            load(bias_rows[0:NK, :], bq.rearrange("(t p) -> t p", p=P), s_bqk)
            load(bias_rows[NK:2 * NK, :], bk.rearrange("(t p) -> t p", p=P), s_bqk)
            load(raw[0][:, :, :], w_view(Wk), s_raw[0])
            load(ctx_raw[:, 0:HALF, :], ctx[0:HALF].rearrange("b s d -> s b d"), s_ctx[0])
            load(xb[:, 0, :, :], x_rows[0], s_x[0])
            load(ctx_raw[:, HALF:B, :], ctx[HALF:B].rearrange("b s d -> s b d"), s_ctx[1])
            load(raw[1][:, :, :], w_view(Wv), s_raw[1])
            load(gates[:, 0:1], g_xattn.partition_broadcast(P), s_gates)
            load(gates[:, 1:2], g_ffn.partition_broadcast(P), s_gates)
            load(bv_bc[:, :], bv.partition_broadcast(SK), s_const)
            load(bo_bc[:, :], bo.partition_broadcast(P), s_const)
            load(be_sb[:, :], be, s_const)
            e.wait_ge(s_setv, 1)
            for k in range(NK):
                load(wg[:, k, 0:NE], w_gate[k * P:(k + 1) * P, :], s_const)
            load(raw[2][:, :, :], w_view(Wq), s_raw[2])
            load(raw[3][:, :, :], w_view(Wo), s_raw[3])
            load(xb[:, 1, :, :], x_rows[1], s_x[1])
            for ex in range(NE):
                slot = ex % 3
                if ex < 3:
                    e.wait_ge(s_pt, last_turn[("wkT", "wvT", "wqT")[slot]])
                else:
                    e.wait_ge(s_ws, max(1, ex - 3))
                load(raw[slot][:, :, :], w_view(We[ex]), s_raw[slot])
                if ex == 1:
                    load(xb[:, 2, :, :], x_rows[2], s_x[2])

            prologue_over(e)
            for r in rounds():
                if ok(r + 1):
                    slot = (r + 1) % 2
                    if ok(r - 1):
                        e.wait_ge(s_sc, 4 * r)
                        e.wait_ge(s_kd, HJ * r)
                    load(k_stack[0:3 * DK, slot, :, :], k_scratch[r + 1], s_ks[slot])
                if ok(r):
                    e.wait_ge(s_qhi, 4 * (r + 1))
                    e.wait_ge(s_qlo, 4 * (r + 1))
                    e.wait_ge(s_sc, 4 * r)
                    for part, src in enumerate((q_hi, q_lo, q_hi)):
                        for j in range(HJ):
                            load(q_stack[part * DK:(part + 1) * DK, j, :, :], src[j * DK:(j + 1) * DK, :, :], s_rq)
                    e.wait_ge(s_sh, r + 1)
                    load(q_stack[3 * DK:STACK, :, :, :].rearrange("o j g s -> o (j g) s"),
                         shift[:, :], s_rsh)
                if ok(r - 1):
                    e.wait_ge(s_x1, 4 * r)
                    load(out_rows[r - 1], xb[:, (r - 1) % NX, :, :], s_st)
                if ok(r + 3) and r >= 0:
                    if ok(r - 1):
                        e.wait_ge(s_st, 16 * r)
                        e.wait_ge(s_x2n, 4 * r)
                    load(xb[:, (r + 3) % NX, :, :], x_rows[r + 3], s_x[(r + 3) % NX])
                if r == B - 1:
                    e.wait_ge(s_st, 16 * (B - 1))
                    e.wait_ge(s_x2n, 4 * (B - 1))
                    load(xb[:, (B - 2) % NX, :, :], w_expert.rearrange("(k p) n -> p k n", p=P), s_we)
            e.wait_ge(s_bc, 4 * B)
            e.wait_ge(s_rlo, B)
            e.wait_ge(s_rhi, B)
            load(rden[:, :], b_expert.partition_broadcast(P), s_tail)
            e.wait_ge(s_st, 16 * B)

        @block.tensor
        def _(e):
            def mm(out_, a, b, start=True, stop=True, **kw):
                return e.matmul(out_, a, b, start=start, stop=stop, **kw)

            for i, u in enumerate(units):
                for s_, n in u["needs"]:
                    e.wait_ge(s_, n)
                if i >= 8:
                    for s_, n in units[i - 8]["done"]:
                        e.wait_ge(s_, n)
                u["pe"](e, ps[:, i % 8, :]).then_inc(s_pt, 1)
            prologue_over(e)
            e.wait_ge(s_setv, SETV)
            e.wait_ge(s_set, SET)

            def parts3(bank, a_hi, a_lo, b_hi, b_lo, n=NK):
                steps = [(a_hi(k), b(k)) for k in range(n) for b in (b_hi, b_lo)]
                steps += [(a_lo(k), b_hi(k)) for k in range(n)]
                for i, (a, b) in enumerate(steps):
                    ins = mm(bank, a, b, start=(i == 0), stop=(i == len(steps) - 1))
                return ins

            def x_turn(r, t):
                bank = (g1_b, g0_b)[t % 2]
                b = r + 1
                e.wait_ge(s_xn, 4 * b + t + 1)
                if t < 2:
                    if ok(r - 1):
                        e.wait_ge(s_sh, r)
                    if ok(r - 2):
                        e.wait_ge(s_lpe, r - 1)
                        e.wait_ge(s_lsub, r - 1)
                    if ok(r):
                        e.wait_ge(s_qhi, 4 * r + 4)
                        e.wait_ge(s_qlo, 4 * r + 4)
                else:
                    e.wait_ge(s_xhi, 4 * b + t - 1)
                    e.wait_ge(s_xlo, 4 * b + t - 1)
                for k in range(NK):
                    ins = e.transpose(bank[:, k * P:(k + 1) * P], xn[:, t % 2, k * P:(k + 1) * P], ident[:, :])
                ins.then_inc(s_xt, 1)

            def spread_rden(b, g):
                bank = (den_b, num_b)[g % 2]
                e.wait_ge(s_rhi, b + 1)
                e.wait_ge(s_rlo, b + 1)
                if g < 2:
                    e.wait_ge(s_num, 4 * b + 4)
                else:
                    e.wait_ge(s_at, 4 * b + g - 1)
                mm(bank, head_sel[:, g, :], rden_hi[:, :], stop=False)
                mm(bank, head_sel[:, g, :], rden_lo[:, :], start=False).then_inc(s_bc, 1)

            def max_turn(r):
                e.wait_ge(s_mx, 4 * r + 4)
                if ok(r + 1):
                    e.wait_ge(s_xhi, 4 * (r + 1) + 3)
                    e.wait_ge(s_xlo, 4 * (r + 1) + 3)
                if ok(r - 2):
                    e.wait_ge(s_lpe, r - 1)
                if ok(r - 1):
                    e.wait_ge(s_sh, r)
                for t in range(NT):
                    ins = e.transpose(g1_b[0:H, t * P:(t + 1) * P], neg_max[:, t, :, :], ident[:, :])
                ins.then_inc(s_mt, 1)

            def places(b):
                e.wait_ge(s_ch, b + 1)
                e.wait_ge(s_at, 4 * min(b + 1, B - 1) + 3)
                ch = choice[:, :, :].rearrange("p t e -> p (t e)")
                mm(den_b[:, 0:NT * NE], tri[:, :], ch, stop=False)
                mm(den_b[:, 0:NT * NE], ones_bf[:, :], base_cnt[:, b % 2, :, :].rearrange("p t e -> p (t e)"),
                   start=False).then_inc(s_pl, 1)

            def table_rows(b):
                e.wait_ge(s_en, b + 1)
                e.wait_ge(s_at, 4 * min(b + 1, B - 1) + 4)
                for t in range(NT):
                    ins = mm(num_b[0:CAP, 0:2 * NE], place_hot[:, t, :], entry[:, t, :, :].rearrange("p w e -> p (w e)"),
                             start=(t == 0), stop=(t == NT - 1))
                ins.then_inc(s_tb, 1)

            def mix(b, t):
                e.wait_ge(s_ahi, 4 * b + 4)
                e.wait_ge(s_alo, 4 * b + 4)
                if ok(b + 1):
                    e.wait_ge(s_mx, 4 * (b + 1) + 4)
                else:
                    e.wait_ge(s_ex, 4 * b + 4)
                tok = slice(t * P, (t + 1) * P)
                parts3(quad[:, t, :], lambda k: attn_hi[:, k, tok], lambda k: attn_lo[:, k, tok],
                       lambda k: mixT_hi[:, k, :], lambda k: mixT_lo[:, k, :]).then_inc(s_mix, 1)

            def scores(b, g):
                if g == 0:
                    e.wait_ge(s_rq, 16 * 3 * HJ * (b + 1))
                    e.wait_ge(s_rsh, 16 * (b + 1))
                    e.wait_ge(s_ks[b % 2], 16 * (b // 2 + 1))
                    e.wait_ge(s_mx, 4 * b + 4)
                    if ok(b - 1):
                        e.wait_ge(s_x1, 4 * b)
                else:
                    e.wait_ge(s_ex, 4 * b + g)
                    if g >= 2 and ok(b + 1):
                        e.wait_ge(s_mx, 4 * (b + 1) + g - 1)
                for j in range(HJ):
                    ins = mm(quad[0:SK, j, :], k_stack[0:STACK, b % 2, j, g * SK:(g + 1) * SK],
                             q_stack[0:STACK, j, g, :])
                ins.then_inc(s_sc, 1)

            def q_tile(b, g):
                if g == 0:
                    e.wait_ge(s_xhi, 4 * b + 4)
                    e.wait_ge(s_xlo, 4 * b + 4)
                else:
                    e.wait_ge(s_qhi, 4 * b + g)
                    e.wait_ge(s_qlo, 4 * b + g)
                col = slice(g * P, (g + 1) * P)
                parts3(g0_b, lambda k: wqT_hi[:, k, col], lambda k: wqT_lo[:, k, col],
                       lambda k: xnT_hi[:, k, :], lambda k: xnT_lo[:, k, :]).then_inc(s_q, 1)

            def max_scores(b, g):
                e.wait_ge(s_qhi, 4 * b + g + 1)
                e.wait_ge(s_kd, HJ * (b + 1))
                if ok(b - 1):
                    e.wait_ge(s_ex, 4 * (b - 1) + min(g + 2, 4))
                if g:
                    e.wait_ge(s_mx, 4 * b + g)
                for t in range(NT):
                    ins = mm(quad[:, t, 0:HJ * SK], q_hi[:, g, t * P:(t + 1) * P], k_diag[:, g, :])
                ins.then_inc(s_ms, 1)

            def values(b, g):
                e.wait_ge(s_ex, 4 * b + g + 1)
                if g == 0:
                    if ok(b - 1):
                        e.wait_ge(s_at, 4 * b)
                    if ok(b - 2):
                        e.wait_ge(s_tab, b - 1)
                        e.wait_ge(s_plr, b - 1)
                else:
                    e.wait_ge(s_num, 4 * b + g)
                for j in range(HJ):
                    row = slice(j * DK, (j + 1) * DK)
                    col = g * P + j * DK
                    mm(num_b[row, :], v_all[:, b, col:col + DK], probs[:, j, :])
                for j in range(HJ):
                    row = slice(j * DK, (j + 1) * DK)
                    ins = mm(den_b[row, :], den_sel[:, g, :], probs[:, j, :], start=(g == 0), stop=(g == NK - 1))
                ins.then_inc(s_val, 1)

            def x2_turn(b, t):
                e.wait_ge(s_x2n, 4 * b + t + 1)
                if t:
                    e.wait_ge(s_x2e, 4 * b + t)
                else:
                    if ok(b + 1):
                        e.wait_ge(s_sh, b + 2)
                    if ok(b - 1):
                        e.wait_ge(s_lpe, b)
                for k in range(NK):
                    ins = e.transpose(g1_b[:, k * P:(k + 1) * P], x2n[:, t % 2, k * P:(k + 1) * P], ident[:, :])
                ins.then_inc(s_x2t, 1)

            def partial_logits(b):
                e.wait_ge(s_x2e, 4 * b + 4)
                for k in range(NK):
                    ins = mm(g1_b[k * DK:(k + 1) * DK, :], wg[:, k, :], x2nT[:, k, :])
                ins.then_inc(s_lp, 1)

            def logits(b):
                e.wait_ge(s_lpe, b + 1)
                if ok(b + 2):
                    e.wait_ge(s_qhi, 4 * (b + 2) + 4)
                    e.wait_ge(s_qlo, 4 * (b + 2) + 4)
                if ok(b - 1):
                    e.wait_ge(s_lsub, b)
                for t in range(NT):
                    ins = mm(g0_b[:, t * NE:(t + 1) * NE], partT[:, t * P:(t + 1) * P], gate_sum[:, :])
                ins.then_inc(s_lg, 1)

            for r in rounds():
                if ok(r + 1):
                    for t in range(NT):
                        x_turn(r, t)
                if ok(r - 1):
                    spread_rden(r - 1, 0)
                    spread_rden(r - 1, 1)
                if ok(r):
                    max_turn(r)
                if ok(r - 1):
                    spread_rden(r - 1, 2)
                    spread_rden(r - 1, 3)
                if ok(r - 2):
                    places(r - 2)
                for t in range(NT):
                    if ok(r - 1):
                        mix(r - 1, t)
                    if ok(r - 2) and t == 1:
                        table_rows(r - 2)
                for g in range(NK):
                    if ok(r):
                        scores(r, g)
                    if ok(r + 1):
                        q_tile(r + 1, g)
                        if g:
                            max_scores(r + 1, g - 1)
                    if ok(r):
                        values(r, g)
                    if ok(r - 1):
                        x2_turn(r - 1, g)
                if ok(r - 1):
                    partial_logits(r - 1)
                if ok(r + 1):
                    max_scores(r + 1, NK - 1)
                if ok(r - 1):
                    logits(r - 1)

            e.wait_ge(s_tab, B)
            e.wait_ge(s_x1, 4 * B)
            e.wait_ge(s_wehi, 1)
            e.wait_ge(s_welo, NK)

            def row_turn(x_):
                bank = (g1_b, g0_b)[x_ % 2]
                e.wait_ge(s_txn, x_ + 1)
                if x_ >= 2:
                    e.wait_ge(s_thi, x_ - 1)
                    e.wait_ge(s_tlo, x_ - 1)
                for k in range(NK):
                    ins = e.transpose(bank[:, k * P:k * P + CAP], xn[0:CAP, x_ % 2, k * P:(k + 1) * P],
                                      ident[0:CAP, 0:CAP])
                ins.then_inc(s_tt, 1)

            def row_product(x_):
                e.wait_ge(s_thi, x_ + 1)
                e.wait_ge(s_tlo, x_ + 1)
                if x_ >= 4:
                    e.wait_ge(s_to, x_ - 3)
                tok = slice((x_ % 4) * P, (x_ % 4) * P + CAP)
                parts3(quad[0:CAP, x_ % 4, :], lambda k: xnT_hi[:, k, tok], lambda k: xnT_lo[:, k, tok],
                       lambda k: wqT_hi[:, k, :], lambda k: wqT_lo[:, k, :]).then_inc(s_tmm, 1)

            row_turn(0)
            for x_ in range(NE):
                if x_ + 1 < NE:
                    row_turn(x_ + 1)
                row_product(x_)

        @block.scalar
        def _(e):
            def act(out_, in_, func=ACT.Copy, **kw):
                return e.activation(out_, in_, func, **kw)

            e.wait_ge(s_gates, 16 * 2)
            act(tanh_g[:, :], gates[:, :], ACT.Tanh).then_inc(s_tanh, 1)
            e.wait_ge(s_tanh, 1)
            act(mix_scale[:, :], tanh_g[:, 0:1], scale=1.0 / NE).then_inc(s_tanh, 1)
            e.wait_ge(s_tanh, 2)

            def store_k(half):
                for s_, n in last_k[half]:
                    e.wait_ge(s_, n)
                for part, src in enumerate((k_hi, k_hi, k_lo)):
                    for j in range(HJ):
                        bs = slice(half * HALF, (half + 1) * HALF)
                        e.dma_start(k_scratch[bs, part * DK:(part + 1) * DK, j, :].rearrange("b d s -> d b s"),
                                    src[j * DK:(j + 1) * DK, bs, :, :].rearrange("d b g s -> d b (g s)")
                                    ).then_inc(s_kst, 16)

            for i, u in enumerate(units):
                if u["act"] is not None:
                    e.wait_ge(s_pt, i + 1)
                    u["act"](e, ps[:, i % 8, :]).then_inc(s_pa, 1)
                for half in range(2):
                    if i >= 4 and units[i - 4]["done"] == made[("k", half, NK - 1)]:
                        store_k(half)
            prologue_over(e)

            def x_hi(b, t):
                e.wait_ge(s_xt, 4 * b + t + 1)
                e.wait_ge(s_q, 4 * b)
                bank = (g1_b, g0_b)[t % 2]
                act(xnT_hi[:, :, t * P:(t + 1) * P], bank.rearrange("p (k s) -> p k s", k=NK)).then_inc(s_xhi, 1)

            def rden_high(b):
                e.wait_ge(s_rec, b + 1)
                e.wait_ge(s_bc, 4 * b)
                act(rden_hi[:, :], rden[:, :]).then_inc(s_rhi, 1)

            def shift_row(b):
                e.wait_ge(s_mt, b + 1)
                e.wait_ge(s_rsh, 16 * b)
                act(shift[:, :], g1_b[0:H, :], scale=1.0 / SHIFT_UNIT).then_inc(s_sh, 1)

            def attn_high(b, g):
                e.wait_ge(s_at, 4 * b + g + 1)
                e.wait_ge(s_mix, 4 * b)
                act(attn_hi[:, g, :], attn[:, g, :]).then_inc(s_ahi, 1)

            def exp(b, g):
                e.wait_ge(s_sc, 4 * b + g + 1)
                e.wait_ge(s_val, 4 * b + g)
                act(probs[:, :, :], quad[0:SK, :, :], ACT.Exp,
                    scale=1.0 / (QK_SCALE * QK_SCALE * float(DK) ** 0.5)).then_inc(s_ex, 1)

            def q_high(b, g):
                e.wait_ge(s_q, 4 * b + g + 1)
                if ok(b - 1):
                    e.wait_ge(s_rq, 16 * 3 * HJ * b)
                    e.wait_ge(s_ms, 4 * b)
                act(q_hi[:, g, :], g0_b, ACT.Identity, bias=bias_cols[:, g:g + 1]).then_inc(s_qhi, 1)

            def value_out(b, g):
                e.wait_ge(s_val, 4 * b + g + 1)
                e.wait_ge(s_ahi, 4 * b)
                e.wait_ge(s_alo, 4 * b)
                act(attn[:, g, :], num_b).then_inc(s_num, 1)

            def x2_out(b, t):
                e.wait_ge(s_x2t, 4 * b + t + 1)
                e.wait_ge(s_lp, b)
                act(x2nT[:, :, t * P:(t + 1) * P], g1_b.rearrange("p (k s) -> p k s", k=NK)).then_inc(s_x2e, 1)

            for r in rounds():
                if ok(r + 1):
                    x_hi(r + 1, 0)
                    x_hi(r + 1, 1)
                if ok(r - 1):
                    rden_high(r - 1)
                if ok(r + 1):
                    x_hi(r + 1, 2)
                    x_hi(r + 1, 3)
                if ok(r):
                    shift_row(r)
                if ok(r - 1):
                    for g in range(NK):
                        attn_high(r - 1, g)
                for g in range(NK):
                    if ok(r):
                        exp(r, g)
                    if ok(r + 1):
                        q_high(r + 1, g)
                    if ok(r):
                        value_out(r, g)
                    if ok(r - 1):
                        x2_out(r - 1, g)
                if ok(r - 1):
                    e.wait_ge(s_lp, r)
                    e.wait_ge(s_lg, r - 1)
                    act(partT[:, :], g1_b).then_inc(s_lpe, 1)
                    e.wait_ge(s_lsub, r)
                    act(l_exp[:, :, :], l_sub[:, :, :], ACT.Exp).then_inc(s_lexp, 1)
                if r == B:
                    e.wait_ge(s_we, 16)
                    e.wait_ge(s_q, 4 * B)
                    act(wqT_hi[:, :, :], xb[:, (B - 2) % NX, :, :]).then_inc(s_wehi, 1)
            for x_ in range(NE):
                e.wait_ge(s_tt, x_ + 1)
                if x_ >= 4:
                    e.wait_ge(s_tmm, x_ - 3)
                bank = (g1_b, g0_b)[x_ % 2]
                act(xnT_hi[:, :, (x_ % 4) * P:(x_ % 4) * P + CAP],
                    bank.rearrange("p (k s) -> p k s", k=NK)[:, :, 0:CAP]).then_inc(s_thi, 1)

        @block.vector
        def _(e):
            e.memset(wg[:, :, :], 0.0).then_inc(s_setv, 1)
            e.memset(den_sel[:, :, :], 0.0).then_inc(s_setv, 1)
            e.wait_ge(s_setv, 2)
            for g in range(NK):
                e.memset(den_sel[:, g, g::NK], 1.0).then_inc(s_setv, 1)
            e.wait_ge(s_set, 2)
            for g in range(NK):
                e.tensor_copy(head_sel[:, g, :].rearrange("p (j d) -> p j d", d=DK),
                              ident[:, g::DK].unsqueeze(2).to_broadcast([P, HJ, DK])).then_inc(s_setv, 1)
            e.tensor_reduce(gate_sum[:, :], ident[:, :].rearrange("p (k c) -> p c k", k=NK)[:, 0:NE, :],
                            AX.X, ALU.add).then_inc(s_setv, 1)

            def stats1(b, t):
                e.wait_ge(s_x[b % NX], 16 * (b // NX + 1))
                if b:
                    e.wait_ge(s_mv1, 4 * b)
                e.bn_stats(bn_raw[:, 0, t, :], xb[:, b % NX, t, :]).then_inc(s_bn1, 1)

            def moments1(b):
                for t in range(NT):
                    e.wait_ge(s_bn1, 4 * b + t + 1)
                    e.bn_aggr(mv[:, b % 2, t, :], bn_raw[:, 0, t, :]).then_inc(s_mv1, 1)

            for i, u in enumerate(units):
                if u["dve"] is not None:
                    e.wait_ge(s_pt, i + 1)
                    if u["act"] is not None:
                        e.wait_ge(*u["done"][0])
                    u["dve"](e, ps[:, i % 8, :]).then_inc(s_pv, 1)
                if u["done"] == made[("k", 0, NK - 1)]:
                    for t in range(NT):
                        stats1(0, t)
                    moments1(0)
            prologue_over(e)
            e.wait_ge(s_tanh, 2)
            e.tensor_scalar(mix_bias[:, :], mix_bias[:, :], tanh_g[:, 0:1], None, ALU.mult).then_inc(s_setv, 1)
            for i in range(2):
                e.memset(k_stack[3 * DK:STACK, i, :, :], SHIFT_UNIT).then_inc(s_setv, 1)
            e.memset(k_diag[:, :, :], 0.0).then_inc(s_setv, 1)
            e.wait_ge(s_setv, SETV)

            def diag(b):
                e.wait_ge(s_ks[b % 2], 16 * (b // 2 + 1))
                e.wait_ge(s_ms, 4 * b)
                for j in range(HJ):
                    e.tensor_copy(k_diag[j * DK:(j + 1) * DK, :, j * SK:(j + 1) * SK],
                                  k_stack[0:DK, b % 2, j, :].rearrange("d (g s) -> d g s", g=NK)).then_inc(s_kd, 1)

            def normalise1(b, t):
                e.wait_ge(s_rs1, b + 1)
                e.wait_ge(s_mv1, 4 * b + 4)
                e.wait_ge(s_xt, max(0, 4 * b + t - 1))
                e.tensor_scalar(xn[:, t % 2, :], xb[:, b % NX, t, :], mv[:, b % 2, t, 0:1], rstd[:, b % 2, t:t + 1],
                                ALU.subtract, ALU.mult).then_inc(s_xn, 1)

            def x_lo(b, t):
                e.wait_ge(s_xhi, 4 * b + t + 1)
                bank = (g1_b, g0_b)[t % 2].rearrange("p (k s) -> p k s", k=NK)
                tok = slice(t * P, (t + 1) * P)
                e.tensor_tensor(xnT_lo[:, :, tok], bank, xnT_hi[:, :, tok].bitcast(F32), ALU.subtract).then_inc(s_xlo, 1)

            def reciprocal(b):
                e.wait_ge(s_val, 4 * b + 4)
                e.wait_ge(s_rhi, b)
                e.wait_ge(s_rlo, b)
                e.reciprocal(rden[:, :], den_b).then_inc(s_rec, 1)

            def rden_low(b):
                e.wait_ge(s_rhi, b + 1)
                e.wait_ge(s_rec, b + 1)
                e.tensor_tensor(rden_lo[:, :], rden[:, :], rden_hi[:, :].bitcast(F32), ALU.subtract).then_inc(s_rlo, 1)

            def divide(b, g):
                e.wait_ge(s_bc, 4 * b + g + 1)
                e.tensor_tensor(attn[:, g, :], (den_b, num_b)[g % 2], attn[:, g, :], ALU.mult).then_inc(s_at, 1)

            def x1_tile(b, t):
                e.wait_ge(s_mix, 4 * b + t + 1)
                e.wait_ge(s_xbias, b + 1)
                row = xb[:, b % NX, t, :]
                e.tensor_tensor(row, quad[:, t, :], row, ALU.add).then_inc(s_x1, 1)
                e.wait_ge(s_x1, 4 * b + t + 1)
                e.wait_ge(s_mv2, 4 * b)
                e.bn_stats(bn_raw[:, 1, t, :], row).then_inc(s_bn2, 1)

            def moments2(b):
                e.wait_ge(s_x2n, 4 * b)
                for t in range(NT):
                    e.wait_ge(s_bn2, 4 * b + t + 1)
                    e.bn_aggr(mv[:, 2, t, :], bn_raw[:, 1, t, :]).then_inc(s_mv2, 1)

            def normalise2(b, t):
                e.wait_ge(s_rs2, b + 1)
                e.wait_ge(s_mv2, 4 * b + 4)
                e.wait_ge(s_x2t, max(0, 4 * b + t - 1))
                e.tensor_scalar(x2n[:, t % 2, :], xb[:, b % NX, t, :], mv[:, 2, t, 0:1], rstd[:, 2, t:t + 1],
                                ALU.subtract, ALU.mult).then_inc(s_x2n, 1)

            def q_low(b, g):
                e.wait_ge(s_qhi, 4 * b + g + 1)
                e.scalar_tensor_tensor(out=q_lo[:, g, :], in0=g0_b, scalar=bias_cols[:, g:g + 1], in1=q_hi[:, g, :],
                                       op0=ALU.add, op1=ALU.subtract).then_inc(s_qlo, 1)

            def maxima(b, g):
                e.wait_ge(s_ms, 4 * b + g + 1)
                e.wait_ge(s_mt, b)
                e.tensor_reduce(neg_max[:, :, g, :], quad[:, :, 0:HJ * SK].rearrange("p t (j s) -> p t j s", j=HJ),
                                AX.X, ALU.max, negate=True).then_inc(s_mx, 1)

            steps = [0]

            def link(ins):
                steps[0] += 1
                ins.then_inc(s_g, 1)
                e.wait_ge(s_g, steps[0])

            def wide(a):
                return a.unsqueeze(2).to_broadcast([P, NT, NE])

            def choose(b):
                e.wait_ge(s_lg, b + 1)
                lg = g0_b[:, 0:NT * NE].rearrange("p (t e) -> p t e", e=NE)
                link(e.tensor_reduce(l_max[:, :], lg, AX.X, ALU.max))
                e.tensor_tensor(l_sub[:, :, :], lg, wide(l_max[:, :]), ALU.subtract).then_inc(s_lsub, 1)
                e.wait_ge(s_lsub, b + 1)
                flat = "p t e -> p (t e)"
                link(e.scalar_tensor_tensor(out=ranked[:, :, :].rearrange(flat), in0=l_sub[:, :, :].rearrange(flat),
                                            scalar=0.0, in1=rank8[:, :, :].rearrange(flat),
                                            op0=ALU.is_equal, op1=ALU.mult))
                link(e.tensor_reduce(top_rank[:, :], ranked[:, :, :], AX.X, ALU.max))
                link(e.tensor_tensor(choice[:, :, :], ranked[:, :, :], wide(top_rank[:, :]), ALU.is_equal))
                for t in range(NT):
                    nxt = base_cnt[:, b % 2, t + 1, :] if t + 1 < NT else base_cnt[:, (b + 1) % 2, 0, :]
                    link(e.tensor_tensor(nxt, base_cnt[:, b % 2, t, :], choice[:, t, :], ALU.add))
                e.wait_ge(s_lexp, b + 1)
                link(e.tensor_reduce(l_sum[:, :], l_exp[:, :, :], AX.X, ALU.add))
                e.reciprocal(gate[:, :], l_sum[:, :]).then_inc(s_ch, 1)

            def enter(b):
                e.wait_ge(s_pl, b + 1)
                e.wait_ge(s_ch, b + 1)
                pl = den_b[:, 0:NT * NE].rearrange("p (t e) -> p t e", e=NE)
                e.tensor_tensor(place_all[:, :, :], pl, choice[:, :, :], ALU.mult).then_inc(s_plr, 1)
                e.wait_ge(s_plr, b + 1)
                link(e.tensor_reduce(place[:, :], place_all[:, :, :], AX.X, ALU.add))
                e.wait_ge(s_tb, b)
                for t in range(NT):
                    e.tensor_scalar(place_hot[:, t, :], place_iota[:, :], place[:, t:t + 1], None, ALU.is_equal)
                link(e.tensor_scalar(token[:, :], token_iota[:, :], float(b * S), None, ALU.add))
                e.tensor_tensor(entry[:, :, 0, :], choice[:, :, :], wide(token[:, :]), ALU.mult)
                e.tensor_tensor(entry[:, :, 1, :], choice[:, :, :], wide(gate[:, :]), ALU.mult).then_inc(s_en, 1)

            def add_table(b):
                e.wait_ge(s_tb, b + 1)
                e.wait_ge(s_tab, b)
                flat = "p w e -> p (w e)"
                tab = table[:, :, :].rearrange(flat)
                e.tensor_tensor(tab, num_b[0:CAP, 0:2 * NE], tab, ALU.add).then_inc(s_tab, 1)

            for r in rounds():
                if ok(r + 1):
                    diag(r + 1)
                    normalise1(r + 1, 0)
                    normalise1(r + 1, 1)
                if ok(r - 1):
                    reciprocal(r - 1)
                if ok(r + 1):
                    x_lo(r + 1, 0)
                    normalise1(r + 1, 2)
                    x_lo(r + 1, 1)
                    normalise1(r + 1, 3)
                if ok(r - 1):
                    rden_low(r - 1)
                if ok(r + 1):
                    x_lo(r + 1, 2)
                    x_lo(r + 1, 3)
                if ok(r - 1):
                    for g in range(NK):
                        divide(r - 1, g)
                if ok(r - 2):
                    enter(r - 2)
                for t in range(NT):
                    if ok(r - 1):
                        x1_tile(r - 1, t)
                    if ok(r - 2) and t == 1:
                        add_table(r - 2)
                if ok(r - 1):
                    moments2(r - 1)
                    normalise2(r - 1, 0)
                    normalise2(r - 1, 1)
                for g in range(NK):
                    if ok(r - 1) and g >= 2:
                        normalise2(r - 1, g)
                    if ok(r + 1):
                        q_low(r + 1, g)
                        if g:
                            maxima(r + 1, g - 1)
                    if ok(r + 2):
                        stats1(r + 2, g)
                if ok(r + 1):
                    maxima(r + 1, NK - 1)
                if ok(r + 2):
                    moments1(r + 2)
                if ok(r - 1):
                    choose(r - 1)

            e.wait_ge(s_tab, B)
            link(e.tensor_scalar(far[:, :], table[:, 0, :], 0.0, FAR, ALU.is_equal, ALU.mult))
            e.scalar_tensor_tensor(out=row_ix[:, :], in0=far[:, :], scalar=-1.0, in1=table[:, 0, :],
                                   op0=ALU.add, op1=ALU.add).then_inc(s_row, 1)
            e.tensor_scalar(coef[:, :], table[:, 1, :], tanh_g[0:CAP, 1:2], None, ALU.mult).then_inc(s_row, 1)
            for x_ in range(NE):
                e.wait_ge(s_ga[x_], 16)
                e.bn_stats(t_bn[:, x_, :], rows[:, x_, :]).then_inc(s_tbn, 1)
            for x_ in range(NE):
                e.wait_ge(s_tbn, x_ + 1)
                e.bn_aggr(t_mv[:, x_, :], t_bn[:, x_, :]).then_inc(s_tmv, 1)

            def row_norm(x_):
                e.wait_ge(s_trs, 1)
                e.wait_ge(s_tmv, NE)
                if x_ >= 2:
                    e.wait_ge(s_tt, x_ - 1)
                e.tensor_scalar(xn[0:CAP, x_ % 2, :], rows[:, x_, :], t_mv[:, x_, 0:1], t_rstd[:, x_:x_ + 1],
                                ALU.subtract, ALU.mult).then_inc(s_txn, 1)

            def row_lo(x_):
                e.wait_ge(s_thi, x_ + 1)
                if x_ >= 4:
                    e.wait_ge(s_tmm, x_ - 3)
                tok = slice((x_ % 4) * P, (x_ % 4) * P + CAP)
                bank = (g1_b, g0_b)[x_ % 2].rearrange("p (k s) -> p k s", k=NK)[:, :, 0:CAP]
                e.tensor_tensor(xnT_lo[:, :, tok], bank, xnT_hi[:, :, tok].bitcast(F32), ALU.subtract).then_inc(s_tlo, 1)

            def row_base(x_):
                e.wait_ge(s_txn, x_ + 1)
                e.wait_ge(s_row, 2)
                e.wait_ge(s_tail, 16)
                e.scalar_tensor_tensor(out=rows[:, x_, :], in0=rden[0:CAP, :], scalar=coef[:, x_:x_ + 1],
                                       in1=rows[:, x_, :], op0=ALU.mult, op1=ALU.add).then_inc(s_tb1, 1)

            def row_out(x_):
                e.wait_ge(s_tmm, x_ + 1)
                e.wait_ge(s_tb1, x_ + 1)
                e.scalar_tensor_tensor(out=rows[:, x_, :], in0=quad[0:CAP, x_ % 4, :], scalar=coef[:, x_:x_ + 1],
                                       in1=rows[:, x_, :], op0=ALU.mult, op1=ALU.add).then_inc(s_to, 1)

            row_norm(0)
            row_norm(1)
            row_lo(0)
            row_base(0)
            for x_ in range(NE):
                if x_ + 2 < NE:
                    row_norm(x_ + 2)
                if x_ + 1 < NE:
                    row_lo(x_ + 1)
                    row_base(x_ + 1)
                row_out(x_)

        @block.gpsimd
        def _(e):
            n = [0]

            def made_const(ins):
                n[0] += 1
                ins.then_inc(s_set, 1)

            made_const(e.memset(ident[:, :], 0.0))
            e.wait_ge(s_set, 1)
            made_const(e.affine_select(out=ident[:, :], in_=ident[:, :], compare_op=ALU.not_equal, fill=1.0,
                                       base=0, pattern=[[-1, P]], channel_multiplier=1))
            made_const(e.memset(neg_half[:, :], -0.5))
            made_const(e.memset(ones_col[:, :], 1.0))
            made_const(e.memset(tri[:, :], 1.0))
            e.wait_ge(s_set, 5)
            made_const(e.affine_select(out=tri[:, :], in_=tri[:, :], compare_op=ALU.is_ge, fill=0.0,
                                       base=0, pattern=[[1, P]], channel_multiplier=-1))
            made_const(e.memset(ones_bf[:, :], 1.0))
            made_const(e.iota(place_iota[:, :], pattern=[[1, CAP]], base=1, channel_multiplier=0,
                              allow_small_or_imprecise_dtypes=True))
            made_const(e.iota(token_iota[:, :], pattern=[[P, NT]], base=1, channel_multiplier=1,
                              allow_small_or_imprecise_dtypes=True))
            made_const(e.iota(rank8[:, :, :], pattern=[[0, NT], [-1, NE]], base=NE, channel_multiplier=0,
                              allow_small_or_imprecise_dtypes=True))
            made_const(e.memset(table[:, :, :], 0.0))
            made_const(e.memset(base_cnt[:, :, :, :], 0.0))
            made_const(e.memset(t_half[:, :], -0.5))
            assert n[0] == SET

            def rsqrt(slot, cols, done_mv, s_ve, s_rs, mean_var, tmp, dst, half_c):
                e.tensor_scalar(tmp, mean_var, EPS, None, ALU.add).then_inc(s_ve, 1)
                e.wait_ge(s_ve, done_mv)
                e.tensor_tensor(dst, tmp, half_c, ALU.pow).then_inc(s_rs, 1)

            def rstd1(b):
                e.wait_ge(s_mv1, 4 * b + 4)
                if b >= 2:
                    e.wait_ge(s_xn, 4 * (b - 1))
                rsqrt(0, NT, b + 1, s_ve1, s_rs1, mv[:, b % 2, :, 1], veps[:, b % 2, :], rstd[:, b % 2, :], neg_half[:, :])

            def rstd2(b):
                e.wait_ge(s_mv2, 4 * b + 4)
                e.wait_ge(s_x2n, 4 * b)
                rsqrt(2, NT, b + 1, s_ve2, s_rs2, mv[:, 2, :, 1], veps[:, 2, :], rstd[:, 2, :], neg_half[:, :])

            def sum_we(ex):
                e.wait_ge(s_raw[ex % 3], 16 * (ex // 3 + 2))
                if ex == 1:
                    e.wait_ge(s_raw[0], 16 * 2)
                    e.tensor_tensor(w_sum[:, :, :], raw[0][:, :, :], raw[1][:, :, :], ALU.add).then_inc(s_ws, 1)
                else:
                    e.wait_ge(s_ws, ex - 1)
                    e.tensor_tensor(w_sum[:, :, :], w_sum[:, :, :], raw[ex % 3][:, :, :], ALU.add).then_inc(s_ws, 1)

            for ex in range(1, NE):
                sum_we(ex)
                if ex == 1:
                    rstd1(0)
            prologue_over(e)

            def attn_low(b, g):
                e.wait_ge(s_ahi, 4 * b + g + 1)
                e.wait_ge(s_mix, 4 * b)
                e.tensor_tensor(attn_lo[:, g, :], attn[:, g, :], attn_hi[:, g, :].bitcast(F32),
                                ALU.subtract).then_inc(s_alo, 1)

            def add_bias(b):
                e.wait_ge(s_setv, SETV)
                e.wait_ge(s_xn, 4 * b + 4)
                for t in range(NT):
                    row = xb[:, b % NX, t, :]
                    ins = e.tensor_tensor(row, row, mix_bias[:, :], ALU.add)
                ins.then_inc(s_xbias, 1)

            for r in rounds():
                if ok(r - 1):
                    for g in range(NK):
                        attn_low(r - 1, g)
                    rstd2(r - 1)
                if ok(r):
                    add_bias(r)
                if ok(r + 2):
                    rstd1(r + 2)
                if r == B:
                    e.wait_ge(s_wehi, 1)
                    for k in range(NK):
                        e.tensor_tensor(wqT_lo[:, k, :], xb[:, (B - 2) % NX, k, :], wqT_hi[:, k, :].bitcast(F32),
                                        ALU.subtract).then_inc(s_welo, 1)

            e.wait_ge(s_st, 16 * B)
            e.wait_ge(s_x2n, 4 * B)
            e.memset(rows[:, :, :], 0.0).then_inc(s_clr, 1)
            e.wait_ge(s_clr, 1)
            e.wait_ge(s_row, 1)
            for x_ in range(NE):
                e.indirect_dma_start(
                    out=rows[:, x_, :], out_offset=None, in_=out_flat[:, :],
                    in_offset=bass.IndirectOffsetOnAxis(ap=row_ix[:, x_:x_ + 1], axis=0),
                    bounds_check=B * S - 1, oob_is_err=False).then_inc(s_ga[x_], 16)
            e.wait_ge(s_tmv, NE)
            rsqrt(0, NE, 1, s_tve, s_trs, t_mv[:, :, 1], t_ve[:, :], t_rstd[:, :], t_half[:, :])
            for x_ in range(NE):
                e.wait_ge(s_to, x_ + 1)
                e.indirect_dma_start(
                    out=out_flat[:, :], out_offset=bass.IndirectOffsetOnAxis(ap=row_ix[:, x_:x_ + 1], axis=0),
                    in_=rows[:, x_, :], in_offset=None,
                    bounds_check=B * S - 1, oob_is_err=False).then_inc(s_sca, 16)
            e.wait_ge(s_sca, 16 * NE)


_INS = ['x', 'ctx_1024', 'g_xattn', 'g_ffn', 'L0_xattn_Wq', 'L0_xattn_bq', 'L0_xattn_Wk', 'L0_xattn_bk',
        'L0_xattn_Wv', 'L0_xattn_bv', 'L0_xattn_We', 'L0_xattn_be', 'L0_xattn_Wo', 'L0_xattn_bo',
        'L0_ffn_w_gate', 'L0_ffn_w_expert', 'L0_ffn_b_expert']


def kernel(**inputs):
    import numpy as _np
    import concourse.bacc as _bacc
    from concourse import mybir as _mybir
    from concourse.bass_utils import run_bass_kernel_spmd as _run

    nc = _bacc.Bacc("TRN2", target_bir_lowering=False, num_devices=1)
    arrays, args = {}, []
    for name in _INS:
        a = _np.ascontiguousarray(inputs[name])
        arrays[f"in_{name}_dram"] = a
        args.append(nc.dram_tensor(f"in_{name}_dram", a.shape, _mybir.dt.from_np(a.dtype), kind="ExternalInput").ap())
    out = nc.dram_tensor("out_0_dram", (B, S, D), F32, kind="ExternalOutput").ap()
    build(nc, *args, out)
    r = _run(nc, [arrays], core_ids=[0])
    return r.results[0]["out_0_dram"]
```

```python
from contextlib import ExitStack

import concourse.bass as bass
from concourse import mybir

F32 = mybir.dt.float32
F32R = mybir.dt.float32r
F16 = mybir.dt.float16
BF16 = mybir.dt.bfloat16
U32 = mybir.dt.uint32
ALU = mybir.AluOpType
ACT = mybir.ActivationFunctionType
AX = mybir.AxisListType

P = 128
B, S, D = 8, 512, 512
SK = 120
H, DK = 16, 32
NE = 8
CAP = 100
NT = S // P
NK = D // P
HJ = P // DK
HALF = B // 2
QK_SCALE = 16.0
SHIFT_UNIT = 1024.0
EPS = 1e-5
NX = 4
STACK = 3 * DK + 1
FAR = 1.0e6


def build(nc, x, ctx, g_xattn, g_ffn, Wq, bq, Wk, bk, Wv, bv, We, be, Wo, bo, w_gate, w_expert, b_expert, out):
    assert x.shape == (B, S, D) and ctx.shape == (B, SK, D) and H * DK == D
    x_rows = x.rearrange("b (t p) d -> b p t d", p=P)
    out_rows = out.rearrange("b (t p) d -> b p t d", p=P)
    out_flat = out.rearrange("b s d -> (b s) d")
    k_scratch = nc.dram_tensor("k_scratch", (B, 3 * DK, HJ, NK * SK), F16, kind="Internal").ap()

    with ExitStack() as st:
        def sb(name, shape, dt):
            return st.enter_context(nc.sbuf_tensor(name, shape, dt))

        def sem(name):
            return st.enter_context(nc.semaphore(name))

        xb = sb("xb", [P, NX, NT, D], F32)
        wqT_hi = sb("wqT_hi", [P, NK, D], F32R)
        wqT_lo = sb("wqT_lo", [P, NK, D], F32R)
        mixT_hi = sb("mixT_hi", [P, NK, D], F32R)
        mixT_lo = sb("mixT_lo", [P, NK, D], F32R)
        v_all = sb("v_all", [SK, B, D], F32)
        mix_bias = sb("mix_bias", [P, D], F32)
        ident = sb("ident", [P, P], F32)
        tri = sb("tri", [P, P], BF16)
        ones_bf = sb("ones_bf", [P, P], BF16)
        den_sel = sb("den_sel", [SK, NK, DK], F32)
        head_sel = sb("head_sel", [P, NK, P], F32R)
        gate_sum = sb("gate_sum", [P, NE], F32)
        wg = sb("wg", [P, NK, DK], F32)
        bias_rows = sb("bias_rows", [2 * NK, P], F32)
        bias_cols = sb("bias_cols", [P, 2 * NK], F32)
        gates = sb("gates", [P, 2], F32)
        tanh_g = sb("tanh_g", [P, 2], F32)
        mix_scale = sb("mix_scale", [P, 1], F32)
        neg_half = sb("neg_half", [P, NT], F32)
        t_half = sb("t_half", [CAP, NE], F32)
        ones_col = sb("ones_col", [P, 1], F32)
        place_iota = sb("place_iota", [P, CAP], F32)
        token_iota = sb("token_iota", [P, NT], F32)
        rank8 = sb("rank8", [P, NT, NE], F32)
        table = sb("table", [CAP, 2, NE], F32)
        base_cnt = sb("base_cnt", [P, 2, NT, NE], BF16)

        bn_raw = sb("bn_raw", [P, 2, NT, 6], F32)
        mv = sb("mv", [P, 3, NT, 2], F32)
        veps = sb("veps", [P, 3, NT], F32)
        rstd = sb("rstd", [P, 3, NT], F32)

        with ExitStack() as pro:
            def pb(name, shape, dt):
                return pro.enter_context(nc.sbuf_tensor(name, shape, dt))
            raw = [pb(f"raw{i}", [P, NK, D], F32) for i in range(3)]
            w_sum = pb("w_sum", [P, NK, D], F32)
            woT = pb("woT", [P, NK, D], F32)
            be_sb = pb("be_sb", [NE, D], F32)
            bo_bc = pb("bo_bc", [P, D], F32)
            be_col = pb("be_col", [P, NK], F32)
        probs = sb("probs", [SK, 2, HJ, S], F32)
        attn = sb("attn", [P, NK, S], F32)
        attn_hi = sb("attn_hi", [P, NK, S], F32R)
        with nc.sbuf_tensor("x2nT", [P, NK, S], F32) as x2nT:
            pass
        attn_lo = sb("attn_lo", [P, NK, S], F32R)
        rden = sb("rden", [P, S], F32)
        rden_hi = sb("rden_hi", [P, S], F32R)
        rden_lo = sb("rden_lo", [P, S], F32R)
        x2n = sb("x2n", [P, 2, D], F32)
        partT = sb("partT", [P, S], F32)
        with ExitStack() as pro:
            ctx_raw = pb("ctx_raw", [SK, B, D], F32)
            ctxT = pb("ctxT", [P, NK, B * SK], F32)
            wkT = pb("wkT", [P, NK, D], F32)
            wvT = pb("wvT", [P, NK, D], F32)
            k_hi = pb("k_hi", [P, B, NK, SK], F16)
            k_lo = pb("k_lo", [P, B, NK, SK], F16)
            bv_bc = pb("bv_bc", [SK, D], F32)
        k_stack = sb("k_stack", [P, 2, HJ, NK * SK], F16)
        k_diag = sb("k_diag", [P, NK, HJ * SK], F16)
        xn = sb("xn", [P, 2, D], F32)
        xnT_hi = sb("xnT_hi", [P, NK, S], F32R)
        xnT_lo = sb("xnT_lo", [P, NK, S], F32R)
        q_hi = sb("q_hi", [P, NK, S], F16)
        q_lo = sb("q_lo", [P, NK, S], F16)
        q_stack = sb("q_stack", [P, HJ, NK, S], F16)
        neg_max = sb("neg_max", [P, NT, NK, HJ], F32)
        shift = sb("shift", [H, S], F16)
        l_max = sb("l_max", [P, NT], F32)
        l_sub = sb("l_sub", [P, NT, NE], F32)
        l_exp = sb("l_exp", [P, NT, NE], F32)
        ranked = sb("ranked", [P, NT, NE], F32)
        top_rank = sb("top_rank", [P, NT], F32)
        choice = sb("choice", [P, NT, NE], BF16)
        l_sum = sb("l_sum", [P, NT], F32)
        gate = sb("gate", [P, NT], F32)
        place_all = sb("place_all", [P, NT, NE], F32)
        place = sb("place", [P, NT], F32)
        place_hot = sb("place_hot", [P, NT, CAP], F32)
        token = sb("token", [P, NT], F32)
        entry = sb("entry", [P, NT, 2, NE], F32)
        rows = probs[0:CAP, :, :, :].rearrange("p a j s -> p (a j) s")
        far = sb("far", [CAP, NE], F32)
        row_ix = sb("row_ix", [CAP, NE], U32)
        coef = sb("coef", [CAP, NE], F32)
        t_bn = sb("t_bn", [CAP, NE, 6], F32)
        t_mv = sb("t_mv", [CAP, NE, 2], F32)
        t_ve = sb("t_ve", [CAP, NE], F32)
        t_rstd = sb("t_rstd", [CAP, NE], F32)

        ps = st.enter_context(nc.psum_tensor("ps", [P, 8, 512], F32))
        quad = ps[:, 0:4, :]
        num_b, den_b, g0_b, g1_b = (ps[:, i, :] for i in range(4, 8))
        pair_b = (g1_b, g0_b)

        s_const = sem("s_const")
        s_bqk = sem("s_bqk")
        s_gates = sem("s_gates")
        s_set = sem("s_set")
        s_setv = sem("s_setv")
        s_tanh = sem("s_tanh")
        s_wt = {n: [sem(f"s_{n}{i}") for i in range(NK)] for n in ("wkT", "wvT", "wqT", "woT")}
        s_raw = [sem(f"s_raw{i}") for i in range(5)]
        s_ctx = [sem(f"s_ctx{i}") for i in range(B)]
        s_pt = sem("s_pt")
        s_pa = sem("s_pa")
        s_pv = sem("s_pv")
        s_ws = sem("s_ws")
        s_kst = sem("s_kst")
        s_x = [sem(f"s_xload{i}") for i in range(NX)]
        s_bn1 = sem("s_bn1")
        s_mv1 = sem("s_mv1")
        s_ve1 = sem("s_ve1")
        s_rs1 = sem("s_rs1")
        s_xn = sem("s_xn")
        s_xt = sem("s_xt")
        s_xhi = sem("s_xhi")
        s_xlo = sem("s_xlo")
        s_q = sem("s_q")
        s_qhi = sem("s_qhi")
        s_qlo = sem("s_qlo")
        s_ks = [sem(f"s_ks{i}") for i in range(2)]
        s_kd = sem("s_kd")
        s_ms = sem("s_ms")
        s_mx = sem("s_mx")
        s_mt = sem("s_mt")
        s_sh = sem("s_sh")
        s_rq = sem("s_rq")
        s_rsh = sem("s_rsh")
        s_sc = sem("s_sc")
        s_ex = sem("s_ex")
        s_val = sem("s_val")
        s_num = sem("s_num")
        s_rec = sem("s_rec")
        s_rhi = sem("s_rhi")
        s_rlo = sem("s_rlo")
        s_bc = sem("s_bc")
        s_at = sem("s_at")
        s_ahi = sem("s_ahi")
        s_alo = sem("s_alo")
        s_mix = sem("s_mix")
        s_xbias = sem("s_xbias")
        s_x1 = sem("s_x1")
        s_st = sem("s_st")
        s_bn2 = sem("s_bn2")
        s_mv2 = sem("s_mv2")
        s_ve2 = sem("s_ve2")
        s_rs2 = sem("s_rs2")
        s_x2n = sem("s_x2n")
        s_x2t = sem("s_x2t")
        s_x2e = sem("s_x2e")
        s_lp = sem("s_lp")
        s_lpe = sem("s_lpe")
        s_lg = sem("s_lg")
        s_lmax = sem("s_lmax")
        s_lsub = sem("s_lsub")
        s_lexp = sem("s_lexp")
        s_g = sem("s_g")
        s_ch = sem("s_ch")
        s_pl = sem("s_pl")
        s_plr = sem("s_plr")
        s_en = sem("s_en")
        s_tb = sem("s_tb")
        s_tab = sem("s_tab")
        s_tail = sem("s_tail")
        s_row = sem("s_row")
        s_clr = sem("s_clr")
        s_we = sem("s_we")
        s_wehi = sem("s_wehi")
        s_welo = sem("s_welo")
        s_ga = [sem(f"s_ga{e}") for e in range(NE)]
        s_tbn = sem("s_tbn")
        s_tmv = sem("s_tmv")
        s_tve = sem("s_tve")
        s_trs = sem("s_trs")
        s_txn = sem("s_txn")
        s_tt = sem("s_tt")
        s_thi = sem("s_thi")
        s_tlo = sem("s_tlo")
        s_tmm = sem("s_tmm")
        s_tb1 = sem("s_tb1")
        s_to = sem("s_to")
        s_sca = sem("s_sca")

        SET, SETV, N_CONST = 13, 15, 3 + NK

        units, made, late = [], {}, []

        def unit(name, pe, needs=(), act=None, dve=None):
            n_act = sum(u["act"] is not None for u in units) + (act is not None)
            n_dve = sum(u["dve"] is not None for u in units) + (dve is not None)
            done = ([(s_pa, n_act)] if act else []) + ([(s_pv, n_dve)] if dve else [])
            i = len(units)
            if late:
                bank, before = 5 - (i - late[0]) % 2, units[i - 2]["done"] if i - late[0] >= 2 else []
            else:
                bank, before = i % 8, units[i - 8]["done"] if i >= 8 else []
            units.append(dict(pe=pe, needs=list(needs), free=before, bank=ps[:, bank, :], act=act, dve=dve, done=done))
            made[name] = done

        def needs_of(*names):
            return [w for n in names for w in made[n]]

        def copy_evac(i, dst, view=lambda b: b, scale=None):
            if i % 2 == 0:
                return dict(act=lambda e, b: e.activation(dst, view(b), ACT.Copy, scale=scale or 1.0))
            if scale is None:
                return dict(dve=lambda e, b: e.tensor_copy(dst, view(b)))
            return dict(dve=lambda e, b: e.tensor_scalar(dst, view(b), scale, None, ALU.mult))

        def turn(src_of, n, cols, rows):
            def pe(e, b):
                for i in range(n):
                    ins = e.transpose(b[0:rows, i * cols:(i + 1) * cols], src_of(i), ident[0:cols, 0:cols])
                return ins
            return pe

        consts = [(s_set, 2)]

        unit("bias", turn(lambda i: bias_rows[:, :], 1, 2 * NK, P), consts + [(s_bqk, 16 * 2)],
             dve=lambda e, b: e.tensor_scalar(bias_cols[:, :], b[:, 0:2 * NK], QK_SCALE, None, ALU.mult))

        slots = [r_[:, :, :] for r_ in raw] + [xb[:, 2, :, :], xb[:, 3, :, :]]
        slot_of = {"wkT": 0, "wvT": 1, "wqT": 2, "woT": 3, "we0": 4,
                   "we1": 0, "we2": 1, "we3": 2, "we4": 3, "we5": 4, "we6": 0, "we7": 1}

        def loaded(ex):
            earlier = [n for n in range(ex + 1) if slot_of[f"we{n}"] == slot_of[f"we{ex}"]]
            return s_raw[slot_of[f"we{ex}"]], 16 * len(earlier)

        def ctx_unit(b_):
            unit(("ctxT", b_), turn(lambda i: ctx_raw[:, b_, i * P:(i + 1) * P], NK, SK, P),
                 consts + [(s_ctx[b_], 16)],
                 **copy_evac(b_, ctxT[:, :, b_ * SK:(b_ + 1) * SK],
                             lambda b: b[:, 0:NK * SK].rearrange("p (k s) -> p k s", k=NK)))

        def weight_units(name, dst, scale=None, pair=None):
            for i in range(NK):
                pe = turn(lambda k, i=i: slots[slot_of[name]][:, i, k * P:(k + 1) * P], NK, P, P)
                cols = slice(i * P, (i + 1) * P)
                view = lambda b: b.rearrange("p (k s) -> p k s", k=NK)
                if pair is None:
                    unit((name, i), pe, consts + [(s_wt[name][i], 16)],
                         **copy_evac(i, dst[:, :, cols], view, scale=scale))
                else:
                    hi, lo = pair
                    unit((name, i), pe, consts + [(s_wt[name][i], 16)],
                         act=lambda e, b, cols=cols: e.activation(hi[:, :, cols], view(b), ACT.Copy, scale=scale),
                         dve=lambda e, b, cols=cols: e.scalar_tensor_tensor(
                             out=lo[:, :, cols], in0=view(b), scalar=scale, in1=hi[:, :, cols].bitcast(F32),
                             op0=ALU.mult, op1=ALU.subtract))

        def k_units(half):
            lo_b, hi_b = half * HALF, (half + 1) * HALF
            for g in range(NK):
                def pe(e, b, g=g):
                    for k in range(NK):
                        ins = e.matmul(b[:, 0:HALF * SK], wkT[:, k, g * P:(g + 1) * P],
                                       ctxT[:, k, lo_b * SK:hi_b * SK], start=(k == 0), stop=(k == NK - 1))
                    return ins
                unit(("k", half, g), pe,
                     needs_of(*[("wkT", k) for k in range(NK)], *[("ctxT", b_) for b_ in range(lo_b, hi_b)], "bias"),
                     act=lambda e, b, g=g: e.activation(
                         k_hi[:, lo_b:hi_b, g, :], b[:, 0:HALF * SK].rearrange("p (b s) -> p b s", s=SK),
                         ACT.Identity, bias=bias_cols[:, NK + g:NK + g + 1]),
                     dve=lambda e, b, g=g: e.scalar_tensor_tensor(
                         out=k_lo[:, lo_b:hi_b, g, :], in0=b[:, 0:HALF * SK].rearrange("p (b s) -> p b s", s=SK),
                         scalar=bias_cols[:, NK + g:NK + g + 1], in1=k_hi[:, lo_b:hi_b, g, :],
                         op0=ALU.add, op1=ALU.subtract))

        def v_unit(b_):
            def pe(e, b):
                for k in range(NK):
                    ins = e.matmul(b[0:SK, :], ctxT[:, k, b_ * SK:(b_ + 1) * SK], wvT[:, k, :],
                                   start=(k == 0), stop=(k == NK - 1))
                return ins
            unit(("v", b_), pe,
                 needs_of(*[("wvT", k) for k in range(NK)], ("ctxT", b_)) + [(s_const, 16 * N_CONST)],
                 dve=lambda e, b: e.tensor_tensor(v_all[:, b_, :], b[0:SK, :], bv_bc[:, :], ALU.add))

        def mix_units():
            def col(e, b):
                for k in range(NK):
                    ins = e.matmul(b[:, k:k + 1], be_sb[:, k * P:(k + 1) * P], ones_col[0:NE, :],
                                   start=True, stop=True)
                return ins
            unit("be_col", col, [(s_const, 16 * N_CONST), (s_set, 4)],
                 dve=lambda e, b: e.tensor_scalar(be_col[:, :], b[:, 0:NK], 1.0 / NE, None, ALU.mult))

            def row(e, b):
                for k in range(NK):
                    ins = e.matmul(b[:, :], be_col[:, k:k + 1].to_broadcast([P, P]), woT[:, k, :],
                                   start=(k == 0), stop=(k == NK - 1))
                return ins
            unit("mix_bias", row, needs_of("be_col", *[("woT", k) for k in range(NK)]) + [(s_const, 16 * N_CONST)],
                 dve=lambda e, b: e.tensor_tensor(mix_bias[:, :], b[:, :], bo_bc[:, :], ALU.add))
            for k in range(NK):
                def pe(e, b, k=k):
                    for o in range(NK):
                        ins = e.matmul(b[:, :], w_sum[:, o, k * P:(k + 1) * P], woT[:, o, :],
                                       start=(o == 0), stop=(o == NK - 1))
                    return ins
                unit(("mix", k), pe, needs_of(*[("woT", o) for o in range(NK)]) + [(s_ws, NE - 1)],
                     act=lambda e, b, k=k: e.activation(mixT_hi[:, k, :], b, ACT.Copy, scale=mix_scale[:, 0:1]),
                     dve=lambda e, b, k=k: e.scalar_tensor_tensor(
                         out=mixT_lo[:, k, :], in0=b, scalar=mix_scale[:, 0:1], in1=mixT_hi[:, k, :].bitcast(F32),
                         op0=ALU.mult, op1=ALU.subtract))

        weight_units("wkT", wkT, scale=QK_SCALE)
        for b_ in range(HALF):
            ctx_unit(b_)
        k_units(0)
        for b_ in range(HALF, B):
            ctx_unit(b_)
        weight_units("wvT", wvT)
        k_units(1)
        weight_units("wqT", None, scale=QK_SCALE, pair=(wqT_hi, wqT_lo))
        weight_units("woT", woT)
        for b_ in range(B):
            v_unit(b_)
        N_FIRST = len(units)
        FIRST_ACT = sum(u["act"] is not None for u in units)
        FIRST_DVE = sum(u["dve"] is not None for u in units)
        late.append(N_FIRST)
        mix_units()
        N_LATE = len(units) - N_FIRST
        N_ACT = sum(u["act"] is not None for u in units)
        N_DVE = sum(u["dve"] is not None for u in units)
        last_turn = {n: 1 + max(i for i, u in enumerate(units) if u["done"] == made[(n, NK - 1)])
                     for n in ("wkT", "wvT", "wqT", "woT")}
        last_k = {h: made[("k", h, NK - 1)] for h in range(2)}

        def first_units_over(e):
            e.wait_ge(s_pa, FIRST_ACT)
            e.wait_ge(s_pv, FIRST_DVE)
            e.wait_ge(s_kst, 16 * 2 * 3 * HJ)

        def prologue_over(e):
            e.wait_ge(s_pa, N_ACT)
            e.wait_ge(s_pv, N_DVE)

        def rounds():
            return range(-1, B + 1)

        def ok(b):
            return 0 <= b < B

        def run(over, order):
            for r in over:
                for step, ahead, arg in order:
                    if ok(r + ahead):
                        step(r + ahead, arg)

        block = st.enter_context(nc.Block())

        @block.sync
        def _(e):
            def load(dst, src, s):
                e.dma_start(dst, src).then_inc(s, 16)

            def w_view(w):
                return w.rearrange("(t p) d -> p t d", p=P)

            def load_tiles(n, w):
                for i in range(NK):
                    load(slots[slot_of[n]][:, i, :], w[i * P:(i + 1) * P, :], s_wt[n][i])

            load(bias_rows[0:NK, :], bq.rearrange("(t p) -> t p", p=P), s_bqk)
            load(bias_rows[NK:2 * NK, :], bk.rearrange("(t p) -> t p", p=P), s_bqk)
            load_tiles("wkT", Wk)
            for b_ in range(B):
                load(ctx_raw[:, b_, :], ctx[b_], s_ctx[b_])
            load(gates[:, 0:1], g_xattn.partition_broadcast(P), s_gates)
            load(gates[:, 1:2], g_ffn.partition_broadcast(P), s_gates)
            load_tiles("wvT", Wv)
            load_tiles("wqT", Wq)
            load(bv_bc[:, :], bv.partition_broadcast(SK), s_const)
            load(bo_bc[:, :], bo.partition_broadcast(P), s_const)
            load(be_sb[:, :], be, s_const)
            e.wait_ge(s_setv, 1)
            for k in range(NK):
                load(wg[:, k, 0:NE], w_gate[k * P:(k + 1) * P, :], s_const)
            load_tiles("woT", Wo)
            load(xb[:, 0, :, :], x_rows[0], s_x[0])
            for ex in range(NE):
                name, slot = f"we{ex}", slot_of[f"we{ex}"]
                before = [n for n in slot_of if slot_of[n] == slot and list(slot_of).index(n) < list(slot_of).index(name)]
                if before:
                    n = before[-1]
                    if n in last_turn:
                        e.wait_ge(s_pt, last_turn[n])
                    else:
                        e.wait_ge(s_ws, max(1, int(n[2:])))
                load(slots[slot], w_view(We[ex]), s_raw[slot])
                if ex == 2:
                    load(xb[:, 1, :, :], x_rows[1], s_x[1])
            e.wait_ge(s_ws, 5)
            load(xb[:, 2, :, :], x_rows[2], s_x[2])

            first_units_over(e)
            e.wait_ge(s_setv, SETV)
            for r in rounds():
                if ok(r + 1):
                    slot = (r + 1) % 2
                    e.wait_ge(s_sc, 4 * max(0, r))
                    load(k_stack[0:3 * DK, slot, :, :], k_scratch[r + 1], s_ks[slot])
                    e.wait_ge(s_ms, 4 * (r + 1))
                    for j in range(HJ):
                        load(k_diag[j * DK:(j + 1) * DK, :, j * SK:(j + 1) * SK],
                             k_scratch[r + 1, 0:DK, j, :].rearrange("d (g s) -> d g s", g=NK), s_kd)
                if ok(r - 1):
                    e.wait_ge(s_x1, 4 * r)
                    load(out_rows[r - 1], xb[:, (r - 1) % NX, :, :], s_st)
                if 0 <= r <= B - 3:
                    if ok(r - 1):
                        e.wait_ge(s_st, 16 * r)
                        e.wait_ge(s_x2n, 4 * r)
                    if ok(r + 3):
                        load(xb[:, (r + 3) % NX, :, :], x_rows[r + 3], s_x[(r + 3) % NX])
                    else:
                        load(xb[:, (r + 3) % NX, :, :], w_expert.rearrange("(k p) n -> p k n", p=P), s_we)
                if ok(r + 1):
                    e.wait_ge(s_sc, 4 * (r + 1))
                    e.wait_ge(s_qhi, 4 * (r + 2))
                    e.wait_ge(s_qlo, 4 * (r + 2))
                    for part, src in enumerate((q_hi, q_lo, q_hi)):
                        for j in range(HJ):
                            load(q_stack[part * DK:(part + 1) * DK, j, :, :], src[j * DK:(j + 1) * DK, :, :], s_rq)
                    e.wait_ge(s_sh, r + 2)
                    load(q_stack[3 * DK:STACK, :, :, :].rearrange("o j g s -> o (j g) s"),
                         shift[:, :], s_rsh)
            e.wait_ge(s_bc, 4 * B)
            e.wait_ge(s_rlo, B)
            e.wait_ge(s_rhi, B)
            load(rden[:, :], b_expert.partition_broadcast(P), s_tail)
            e.wait_ge(s_st, 16 * B)

        @block.tensor
        def _(e):
            def mm(out_, a, b, start=True, stop=True, **kw):
                return e.matmul(out_, a, b, start=start, stop=stop, **kw)

            def prepare(_, i):
                u = units[i]
                for s_, n in u["needs"] + u["free"]:
                    e.wait_ge(s_, n)
                u["pe"](e, u["bank"]).then_inc(s_pt, 1)

            for i in range(N_FIRST):
                prepare(0, i)
            first_units_over(e)
            e.wait_ge(s_setv, SETV - 1)
            e.wait_ge(s_set, SET)

            def parts3(bank, a_hi, a_lo, b_hi, b_lo, hi_wait=None, lo_wait=None):
                steps = [(a_hi(k), b(k), hi_wait, k) for k in range(NK) for b in (b_hi, b_lo)]
                steps += [(a_lo(k), b_hi(k), lo_wait, k) for k in range(NK)]
                for i, (a, b, wait, k) in enumerate(steps):
                    if wait:
                        e.wait_ge(wait[0], wait[1] + k + 1)
                    ins = mm(bank, a, b, start=(i == 0), stop=(i == len(steps) - 1))
                return ins

            def x_turn(b, t):
                e.wait_ge(s_xn, 4 * b + t + 1)
                if t < 2:
                    if ok(b - 2):
                        e.wait_ge(s_x1, 4 * (b - 2) + t + 3)
                    elif ok(b - 1):
                        e.wait_ge(s_qhi, 4 * b)
                        e.wait_ge(s_qlo, 4 * b)
                else:
                    e.wait_ge(s_xhi, 4 * b + t - 1)
                    e.wait_ge(s_xlo, 4 * b + t - 1)
                for k in range(NK):
                    ins = e.transpose(pair_b[t % 2][:, k * P:(k + 1) * P], xn[:, t % 2, k * P:(k + 1) * P], ident[:, :])
                ins.then_inc(s_xt, 1)

            def scores(b, g):
                if g == 0:
                    e.wait_ge(s_rq, 16 * 3 * HJ * (b + 1))
                    e.wait_ge(s_rsh, 16 * (b + 1))
                    e.wait_ge(s_ks[b % 2], 16 * (b // 2 + 1))
                    e.wait_ge(s_mx, 4 * b + 4)
                else:
                    e.wait_ge(s_ex, 4 * b + g)
                for j in range(HJ):
                    ins = mm(quad[0:SK, j, :], k_stack[0:STACK, b % 2, j, g * SK:(g + 1) * SK],
                             q_stack[0:STACK, j, g, :])
                ins.then_inc(s_sc, 1)

            def values(b, g):
                e.wait_ge(s_ex, 4 * b + g + 1)
                if g == 0:
                    if b == 0:
                        prologue_over(e)
                    e.wait_ge(s_at, 4 * b)
                    if ok(b - 2):
                        e.wait_ge(s_tab, b - 1)
                    e.wait_ge(s_sh, b + 1)
                else:
                    e.wait_ge(s_num, 4 * b + g)
                for j in range(HJ):
                    row = slice(j * DK, (j + 1) * DK)
                    col = g * P + j * DK
                    mm(num_b[row, :], v_all[:, b, col:col + DK], probs[:, g % 2, j, :])
                for j in range(HJ):
                    row = slice(j * DK, (j + 1) * DK)
                    ins = mm(den_b[row, :], den_sel[:, g, :], probs[:, g % 2, j, :], start=(g == 0), stop=(g == NK - 1))
                ins.then_inc(s_val, 1)

            def x2_turn(b, t):
                e.wait_ge(s_x2n, 4 * b + t + 1)
                if t < 2:
                    if ok(b + 2):
                        e.wait_ge(s_xhi, 4 * (b + 2) + t + 3)
                        e.wait_ge(s_xlo, 4 * (b + 2) + t + 3)
                else:
                    e.wait_ge(s_x2e, 4 * b + t - 1)
                for k in range(NK):
                    ins = e.transpose(pair_b[t % 2][:, k * P:(k + 1) * P], x2n[:, t % 2, k * P:(k + 1) * P], ident[:, :])
                ins.then_inc(s_x2t, 1)

            def partial_logits(b, _):
                e.wait_ge(s_x2e, 4 * b + 4)
                for k in range(NK):
                    ins = mm(g0_b[k * DK:(k + 1) * DK, :], wg[:, k, :], x2nT[:, k, :])
                ins.then_inc(s_lp, 1)

            def logits(b, _):
                e.wait_ge(s_lpe, b + 1)
                if ok(b + 1):
                    e.wait_ge(s_num, 4 * (b + 1) + 4)
                else:
                    e.wait_ge(s_at, 4 * B)
                    e.wait_ge(s_tab, b)
                for t in range(NT):
                    ins = mm(num_b[:, t * NE:(t + 1) * NE], partT[:, t * P:(t + 1) * P], gate_sum[:, :])
                ins.then_inc(s_lg, 1)

            def q_tile(b, g):
                if g == 0:
                    e.wait_ge(s_xhi, 4 * b + 4)
                    e.wait_ge(s_xlo, 4 * b + 4)
                    if ok(b - 2):
                        e.wait_ge(s_x2e, 4 * (b - 2) + 3)
                elif g == 1:
                    if ok(b - 2):
                        e.wait_ge(s_lpe, b - 1)
                else:
                    e.wait_ge(s_qhi, 4 * b + g - 1)
                    e.wait_ge(s_qlo, 4 * b + g - 1)
                col = slice(g * P, (g + 1) * P)
                parts3(pair_b[g % 2], lambda k: wqT_hi[:, k, col], lambda k: wqT_lo[:, k, col],
                       lambda k: xnT_hi[:, k, :], lambda k: xnT_lo[:, k, :]).then_inc(s_q, 1)

            def max_scores(b, g):
                e.wait_ge(s_qhi, 4 * b + g + 1)
                if g:
                    e.wait_ge(s_mx, 4 * b + g)
                else:
                    e.wait_ge(s_kd, 16 * HJ * (b + 1))
                    e.wait_ge(s_ex, 4 * b)
                for t in range(NT):
                    ins = mm(quad[:, t, 0:HJ * SK], q_hi[:, g, t * P:(t + 1) * P], k_diag[:, g, :])
                ins.then_inc(s_ms, 1)

            def spread_rden(b, g):
                bank = (den_b, num_b)[g % 2]
                e.wait_ge(s_rhi, b + 1)
                e.wait_ge(s_rlo, b + 1)
                if g < 2:
                    e.wait_ge(s_num, 4 * b + 4)
                    if ok(b - 1):
                        e.wait_ge(s_lsub, b)
                else:
                    e.wait_ge(s_at, 4 * b + g - 1)
                mm(bank, head_sel[:, g, :], rden_hi[:, :], stop=False)
                mm(bank, head_sel[:, g, :], rden_lo[:, :], start=False).then_inc(s_bc, 1)

            def mix(b, t):
                if t < 2:
                    if ok(b + 1):
                        e.wait_ge(s_qhi, 4 * (b + 1) + t + 3)
                        e.wait_ge(s_qlo, 4 * (b + 1) + t + 3)
                    else:
                        e.wait_ge(s_x2e, 4 * b)
                        e.wait_ge(s_lpe, b)
                else:
                    e.wait_ge(s_x1, 4 * b + t - 1)
                tok = slice(t * P, (t + 1) * P)
                parts3(pair_b[t % 2], lambda k: attn_hi[:, k, tok], lambda k: attn_lo[:, k, tok],
                       lambda k: mixT_hi[:, k, :], lambda k: mixT_lo[:, k, :],
                       (s_ahi, 4 * b), (s_alo, 4 * b)).then_inc(s_mix, 1)

            def max_turn(b, _):
                e.wait_ge(s_mx, 4 * b + 4)
                if ok(b - 1):
                    e.wait_ge(s_at, 4 * (b - 1) + 3)
                else:
                    for s_, n in made[("mix", 2)]:
                        e.wait_ge(s_, n)
                if ok(b - 2):
                    e.wait_ge(s_plr, b - 1)
                for t in range(NT):
                    ins = e.transpose(den_b[0:H, t * P:(t + 1) * P], neg_max[:, t, :, :], ident[:, :])
                ins.then_inc(s_mt, 1)

            def places(b, _):
                e.wait_ge(s_ch, b + 1)
                e.wait_ge(s_at, 4 * min(b + 1, B - 1) + 3)
                ch = choice[:, :, :].rearrange("p t e -> p (t e)")
                mm(den_b[:, 0:NT * NE], tri[:, :], ch, stop=False)
                mm(den_b[:, 0:NT * NE], ones_bf[:, :], base_cnt[:, b % 2, :, :].rearrange("p t e -> p (t e)"),
                   start=False).then_inc(s_pl, 1)

            def table_rows(b, _):
                e.wait_ge(s_en, b + 1)
                e.wait_ge(s_at, 4 * min(b + 2, B))
                for t in range(NT):
                    ins = mm(num_b[0:CAP, 0:2 * NE], place_hot[:, t, :], entry[:, t, :, :].rearrange("p w e -> p (w e)"),
                             start=(t == 0), stop=(t == NT - 1))
                ins.then_inc(s_tb, 1)

            def late_unit(i):
                return prepare, 1, N_FIRST + i

            run([-1], [
                (x_turn, 1, 0), (x_turn, 1, 1), (x_turn, 1, 2), (x_turn, 1, 3), late_unit(0), late_unit(1),
                (q_tile, 1, 0), late_unit(2), (max_scores, 1, 0), (q_tile, 1, 1), late_unit(3), (q_tile, 1, 2),
                (max_scores, 1, 1), late_unit(4), (q_tile, 1, 3), (max_scores, 1, 2), (max_scores, 1, 3),
                late_unit(5), (max_turn, 1, 0),
            ])
            run(range(0, B + 1), [
                (x_turn, 1, 0), (x_turn, 1, 1), (scores, 0, 0), (x_turn, 1, 2), (x_turn, 1, 3),
                (scores, 0, 1), (values, 0, 0),
                (scores, 0, 2), (values, 0, 1), (x2_turn, -1, 0), (x2_turn, -1, 1),
                (scores, 0, 3), (values, 0, 2), (x2_turn, -1, 2), (x2_turn, -1, 3), (values, 0, 3),
                (partial_logits, -1, 0), (q_tile, 1, 0), (logits, -1, 0), (q_tile, 1, 1),
                (spread_rden, 0, 0), (spread_rden, 0, 1), (max_scores, 1, 0), (q_tile, 1, 2),
                (spread_rden, 0, 2), (spread_rden, 0, 3), (max_scores, 1, 1), (q_tile, 1, 3),
                (mix, 0, 0), (max_scores, 1, 2), (mix, 0, 1), (max_scores, 1, 3), (places, -1, 0),
                (mix, 0, 2), (max_turn, 1, 0), (mix, 0, 3), (table_rows, -1, 0),
            ])

            e.wait_ge(s_tab, B)
            e.wait_ge(s_wehi, 1)
            e.wait_ge(s_welo, NK)

            def row_turn(x_):
                bank = (g1_b, g0_b)[x_ % 2]
                e.wait_ge(s_txn, x_ + 1)
                if x_ >= 2:
                    e.wait_ge(s_thi, x_ - 1)
                    e.wait_ge(s_tlo, x_ - 1)
                for k in range(NK):
                    ins = e.transpose(bank[:, k * P:k * P + CAP], xn[0:CAP, x_ % 2, k * P:(k + 1) * P],
                                      ident[0:CAP, 0:CAP])
                ins.then_inc(s_tt, 1)

            def row_product(x_):
                e.wait_ge(s_thi, x_ + 1)
                e.wait_ge(s_tlo, x_ + 1)
                if x_ >= 4:
                    e.wait_ge(s_to, x_ - 3)
                tok = slice((x_ % 4) * P, (x_ % 4) * P + CAP)
                parts3(quad[0:CAP, x_ % 4, :], lambda k: xnT_hi[:, k, tok], lambda k: xnT_lo[:, k, tok],
                       lambda k: wqT_hi[:, k, :], lambda k: wqT_lo[:, k, :]).then_inc(s_tmm, 1)

            row_turn(0)
            for x_ in range(NE):
                if x_ + 1 < NE:
                    row_turn(x_ + 1)
                row_product(x_)

        @block.scalar
        def _(e):
            def act(out_, in_, func=ACT.Copy, **kw):
                return e.activation(out_, in_, func, **kw)

            def store_k(half):
                for s_, n in last_k[half]:
                    e.wait_ge(s_, n)
                for part, src in enumerate((k_hi, k_hi, k_lo)):
                    for j in range(HJ):
                        bs = slice(half * HALF, (half + 1) * HALF)
                        e.dma_start(k_scratch[bs, part * DK:(part + 1) * DK, j, :].rearrange("b d s -> d b s"),
                                    src[j * DK:(j + 1) * DK, bs, :, :].rearrange("d b g s -> d b (g s)")
                                    ).then_inc(s_kst, 16)

            def prepare(_, i):
                u = units[i]
                if u["act"] is not None:
                    e.wait_ge(s_pt, i + 1)
                    u["act"](e, u["bank"]).then_inc(s_pa, 1)

            for i in range(N_FIRST):
                prepare(0, i)
                for half in range(2):
                    if i >= 4 and units[i - 4]["done"] == made[("k", half, NK - 1)]:
                        store_k(half)
            e.wait_ge(s_gates, 16 * 2)
            act(tanh_g[:, :], gates[:, :], ACT.Tanh).then_inc(s_tanh, 1)
            e.wait_ge(s_tanh, 1)
            act(mix_scale[:, :], tanh_g[:, 0:1], scale=1.0 / NE).then_inc(s_tanh, 1)
            e.wait_ge(s_tanh, 2)
            first_units_over(e)

            def x_hi(b, t):
                e.wait_ge(s_xt, 4 * b + t + 1)
                e.wait_ge(s_q, 4 * b)
                act(xnT_hi[:, :, t * P:(t + 1) * P], pair_b[t % 2].rearrange("p (k s) -> p k s", k=NK)).then_inc(s_xhi, 1)

            def rden_high(b, _):
                e.wait_ge(s_rec, b + 1)
                e.wait_ge(s_bc, 4 * b)
                act(rden_hi[:, :], rden[:, :]).then_inc(s_rhi, 1)

            def shift_row(b, _):
                e.wait_ge(s_mt, b + 1)
                e.wait_ge(s_rsh, 16 * b)
                act(shift[:, :], den_b[0:H, :], scale=1.0 / SHIFT_UNIT).then_inc(s_sh, 1)

            def attn_high(b, g):
                e.wait_ge(s_at, 4 * b + g + 1)
                e.wait_ge(s_mix, 4 * b)
                act(attn_hi[:, g, :], attn[:, g, :]).then_inc(s_ahi, 1)

            def exp(b, g):
                if b == 0 and g == 0:
                    prologue_over(e)
                e.wait_ge(s_sc, 4 * b + g + 1)
                e.wait_ge(s_val, max(0, 4 * b + g - 1))
                act(probs[:, g % 2, :, :], quad[0:SK, :, :], ACT.Exp,
                    scale=1.0 / (QK_SCALE * QK_SCALE * float(DK) ** 0.5)).then_inc(s_ex, 1)

            def q_high(b, g):
                e.wait_ge(s_q, 4 * b + g + 1)
                e.wait_ge(s_rq, 16 * 3 * HJ * b)
                e.wait_ge(s_ms, 4 * b)
                act(q_hi[:, g, :], pair_b[g % 2], ACT.Identity, bias=bias_cols[:, g:g + 1]).then_inc(s_qhi, 1)

            def value_out(b, g):
                e.wait_ge(s_val, 4 * b + g + 1)
                e.wait_ge(s_ahi, 4 * b)
                e.wait_ge(s_alo, 4 * b)
                act(attn[:, g, :], num_b).then_inc(s_num, 1)

            def x2_out(b, t):
                e.wait_ge(s_x2t, 4 * b + t + 1)
                e.wait_ge(s_mix, 4 * b + 4)
                act(x2nT[:, :, t * P:(t + 1) * P], pair_b[t % 2].rearrange("p (k s) -> p k s", k=NK)).then_inc(s_x2e, 1)

            def part_out(b, _):
                e.wait_ge(s_lp, b + 1)
                e.wait_ge(s_lg, b)
                act(partT[:, :], g0_b).then_inc(s_lpe, 1)

            def gate_exp(b, _):
                e.wait_ge(s_lsub, b + 1)
                act(l_exp[:, :, :], l_sub[:, :, :], ACT.Exp).then_inc(s_lexp, 1)

            order = [
                (x_hi, 1, 0), (x_hi, 1, 1), (exp, 0, 0), (x_hi, 1, 2), (x_hi, 1, 3), (exp, 0, 1), (value_out, 0, 0),
                (exp, 0, 2), (value_out, 0, 1), (x2_out, -1, 0), (x2_out, -1, 1),
                (exp, 0, 3), (value_out, 0, 2), (x2_out, -1, 2), (x2_out, -1, 3), (value_out, 0, 3),
                (part_out, -1, 0), (rden_high, 0, 0), (q_high, 1, 0), (gate_exp, -1, 0), (q_high, 1, 1),
                (attn_high, 0, 0), (attn_high, 0, 1), (q_high, 1, 2), (attn_high, 0, 2), (attn_high, 0, 3), (q_high, 1, 3),
                (shift_row, 1, 0),
            ]
            late_unit = lambda i: (prepare, 1, N_FIRST + i)
            run([-1], [
                (x_hi, 1, 0), (x_hi, 1, 1), (x_hi, 1, 2), (x_hi, 1, 3), (q_high, 1, 0), late_unit(2), (q_high, 1, 1),
                late_unit(3), (q_high, 1, 2), late_unit(4), (q_high, 1, 3), late_unit(5), (shift_row, 1, 0),
            ])
            run(range(0, B), order)
            e.wait_ge(s_we, 16)
            e.wait_ge(s_q, 4 * B)
            act(wqT_hi[:, :, :], xb[:, B % NX, :, :]).then_inc(s_wehi, 1)
            run([B], order)
            for x_ in range(NE):
                e.wait_ge(s_tt, x_ + 1)
                if x_ >= 4:
                    e.wait_ge(s_tmm, x_ - 3)
                bank = (g1_b, g0_b)[x_ % 2]
                act(xnT_hi[:, :, (x_ % 4) * P:(x_ % 4) * P + CAP],
                    bank.rearrange("p (k s) -> p k s", k=NK)[:, :, 0:CAP]).then_inc(s_thi, 1)

        @block.vector
        def _(e):
            e.memset(wg[:, :, :], 0.0).then_inc(s_setv, 1)
            e.memset(den_sel[:, :, :], 0.0).then_inc(s_setv, 1)
            e.wait_ge(s_setv, 2)
            for g in range(NK):
                e.memset(den_sel[:, g, g::NK], 1.0).then_inc(s_setv, 1)
            e.wait_ge(s_set, 2)
            for g in range(NK):
                e.tensor_copy(head_sel[:, g, :].rearrange("p (j d) -> p j d", d=DK),
                              ident[:, g::DK].unsqueeze(2).to_broadcast([P, HJ, DK])).then_inc(s_setv, 1)
            e.tensor_reduce(gate_sum[:, :], ident[:, :].rearrange("p (k c) -> p c k", k=NK)[:, 0:NE, :],
                            AX.X, ALU.add).then_inc(s_setv, 1)

            def stats1(b, t):
                e.wait_ge(s_x[b % NX], 16 * (b // NX + 1))
                if b:
                    e.wait_ge(s_mv1, 4 * b)
                e.bn_stats(bn_raw[:, 0, t, :], xb[:, b % NX, t, :]).then_inc(s_bn1, 1)

            def moments1(b, _):
                for t in range(NT):
                    e.wait_ge(s_bn1, 4 * b + t + 1)
                    e.bn_aggr(mv[:, b % 2, t, :], bn_raw[:, 0, t, :]).then_inc(s_mv1, 1)

            def prepare(_, i):
                u = units[i]
                if u["dve"] is not None:
                    e.wait_ge(s_pt, i + 1)
                    if u["act"] is not None:
                        e.wait_ge(*u["done"][0])
                    u["dve"](e, u["bank"]).then_inc(s_pv, 1)

            for i in range(N_FIRST):
                prepare(0, i)
                if units[i]["done"] == made[("v", 1)]:
                    for t in range(NT):
                        stats1(0, t)
                    moments1(0, 0)
            first_units_over(e)
            for i in range(2):
                e.memset(k_stack[3 * DK:STACK, i, :, :], SHIFT_UNIT).then_inc(s_setv, 1)
            e.memset(k_diag[:, :, :], 0.0).then_inc(s_setv, 1)

            def scale_bias(_, __):
                e.wait_ge(s_tanh, 2)
                e.wait_ge(*made["mix_bias"][0])
                e.tensor_scalar(mix_bias[:, :], mix_bias[:, :], tanh_g[:, 0:1], None, ALU.mult).then_inc(s_setv, 1)

            def normalise1(b, t):
                e.wait_ge(s_rs1, b + 1)
                e.wait_ge(s_mv1, 4 * b + 4)
                e.wait_ge(s_xt, max(0, 4 * b + t - 1))
                e.tensor_scalar(xn[:, t % 2, :], xb[:, b % NX, t, :], mv[:, b % 2, t, 0:1], rstd[:, b % 2, t:t + 1],
                                ALU.subtract, ALU.mult).then_inc(s_xn, 1)

            def x_lo(b, t):
                e.wait_ge(s_xhi, 4 * b + t + 1)
                tok = slice(t * P, (t + 1) * P)
                e.tensor_tensor(xnT_lo[:, :, tok], pair_b[t % 2].rearrange("p (k s) -> p k s", k=NK),
                                xnT_hi[:, :, tok].bitcast(F32), ALU.subtract).then_inc(s_xlo, 1)

            def reciprocal(b, _):
                e.wait_ge(s_val, 4 * b + 4)
                e.wait_ge(s_rhi, b)
                e.wait_ge(s_rlo, b)
                e.reciprocal(rden[:, :], den_b).then_inc(s_rec, 1)

            def rden_low(b, _):
                e.wait_ge(s_rhi, b + 1)
                e.wait_ge(s_rec, b + 1)
                e.tensor_tensor(rden_lo[:, :], rden[:, :], rden_hi[:, :].bitcast(F32), ALU.subtract).then_inc(s_rlo, 1)

            def divide(b, g):
                e.wait_ge(s_bc, 4 * b + g + 1)
                e.tensor_tensor(attn[:, g, :], (den_b, num_b)[g % 2], attn[:, g, :], ALU.mult).then_inc(s_at, 1)

            def x1_tile(b, t):
                e.wait_ge(s_mix, 4 * b + t + 1)
                e.wait_ge(s_xbias, b + 1)
                row = xb[:, b % NX, t, :]
                e.tensor_tensor(row, pair_b[t % 2], row, ALU.add).then_inc(s_x1, 1)
                e.wait_ge(s_x1, 4 * b + t + 1)
                e.wait_ge(s_mv2, 4 * b)
                e.bn_stats(bn_raw[:, 1, t, :], row).then_inc(s_bn2, 1)

            def moments2(b, _):
                e.wait_ge(s_x2n, 4 * b)
                for t in range(NT):
                    e.wait_ge(s_bn2, 4 * b + t + 1)
                    e.bn_aggr(mv[:, 2, t, :], bn_raw[:, 1, t, :]).then_inc(s_mv2, 1)

            def normalise2(b, t):
                e.wait_ge(s_rs2, b + 1)
                e.wait_ge(s_mv2, 4 * b + 4)
                e.wait_ge(s_x2t, max(0, 4 * b + t - 1))
                e.tensor_scalar(x2n[:, t % 2, :], xb[:, b % NX, t, :], mv[:, 2, t, 0:1], rstd[:, 2, t:t + 1],
                                ALU.subtract, ALU.mult).then_inc(s_x2n, 1)

            def q_low(b, g):
                e.wait_ge(s_qhi, 4 * b + g + 1)
                e.scalar_tensor_tensor(out=q_lo[:, g, :], in0=pair_b[g % 2], scalar=bias_cols[:, g:g + 1], in1=q_hi[:, g, :],
                                       op0=ALU.add, op1=ALU.subtract).then_inc(s_qlo, 1)

            def maxima(b, g):
                e.wait_ge(s_ms, 4 * b + g + 1)
                e.wait_ge(s_mt, b)
                e.tensor_reduce(neg_max[:, :, g, :], quad[:, :, 0:HJ * SK].rearrange("p t (j s) -> p t j s", j=HJ),
                                AX.X, ALU.max, negate=True).then_inc(s_mx, 1)

            steps = [0]

            def link(ins):
                steps[0] += 1
                ins.then_inc(s_g, 1)
                e.wait_ge(s_g, steps[0])

            def wide(a):
                return a.unsqueeze(2).to_broadcast([P, NT, NE])

            def logit_gap(b, _):
                e.wait_ge(s_lg, b + 1)
                lg = num_b[:, 0:NT * NE].rearrange("p (t e) -> p t e", e=NE)
                link(e.tensor_reduce(l_max[:, :], lg, AX.X, ALU.max))
                e.tensor_tensor(l_sub[:, :, :], lg, wide(l_max[:, :]), ALU.subtract).then_inc(s_lsub, 1)

            def choose(b, _):
                e.wait_ge(s_lsub, b + 1)
                flat = "p t e -> p (t e)"
                link(e.scalar_tensor_tensor(out=ranked[:, :, :].rearrange(flat), in0=l_sub[:, :, :].rearrange(flat),
                                            scalar=0.0, in1=rank8[:, :, :].rearrange(flat),
                                            op0=ALU.is_equal, op1=ALU.mult))
                link(e.tensor_reduce(top_rank[:, :], ranked[:, :, :], AX.X, ALU.max))
                link(e.tensor_tensor(choice[:, :, :], ranked[:, :, :], wide(top_rank[:, :]), ALU.is_equal))
                for t in range(NT):
                    nxt = base_cnt[:, b % 2, t + 1, :] if t + 1 < NT else base_cnt[:, (b + 1) % 2, 0, :]
                    link(e.tensor_tensor(nxt, base_cnt[:, b % 2, t, :], choice[:, t, :], ALU.add))
                e.wait_ge(s_lexp, b + 1)
                link(e.tensor_reduce(l_sum[:, :], l_exp[:, :, :], AX.X, ALU.add))
                e.reciprocal(gate[:, :], l_sum[:, :]).then_inc(s_ch, 1)

            def enter(b, _):
                e.wait_ge(s_pl, b + 1)
                e.wait_ge(s_ch, b + 1)
                pl = den_b[:, 0:NT * NE].rearrange("p (t e) -> p t e", e=NE)
                e.tensor_tensor(place_all[:, :, :], pl, choice[:, :, :], ALU.mult).then_inc(s_plr, 1)
                e.wait_ge(s_plr, b + 1)
                link(e.tensor_reduce(place[:, :], place_all[:, :, :], AX.X, ALU.add))
                e.wait_ge(s_tb, b)
                for t in range(NT):
                    e.tensor_scalar(place_hot[:, t, :], place_iota[:, :], place[:, t:t + 1], None, ALU.is_equal)
                link(e.tensor_scalar(token[:, :], token_iota[:, :], float(b * S), None, ALU.add))
                e.tensor_tensor(entry[:, :, 0, :], choice[:, :, :], wide(token[:, :]), ALU.mult)
                e.tensor_tensor(entry[:, :, 1, :], choice[:, :, :], wide(gate[:, :]), ALU.mult).then_inc(s_en, 1)

            def add_table(b, _):
                e.wait_ge(s_tb, b + 1)
                e.wait_ge(s_tab, b)
                flat = "p w e -> p (w e)"
                tab = table[:, :, :].rearrange(flat)
                e.tensor_tensor(tab, num_b[0:CAP, 0:2 * NE], tab, ALU.add).then_inc(s_tab, 1)

            normalise1(0, 0)
            normalise1(0, 1)
            late_unit = lambda i: (prepare, 1, N_FIRST + i)
            run([-1], [
                (x_lo, 1, 0), (normalise1, 1, 2), (x_lo, 1, 1), (normalise1, 1, 3), (x_lo, 1, 2), (x_lo, 1, 3),
                late_unit(0), (stats1, 2, 0), (stats1, 2, 1), late_unit(1), (scale_bias, 1, 0), (q_low, 1, 0),
                late_unit(2), (maxima, 1, 0), (q_low, 1, 1), late_unit(3), (stats1, 2, 2), (q_low, 1, 2),
                (maxima, 1, 1), late_unit(4), (q_low, 1, 3), (maxima, 1, 2), (maxima, 1, 3), late_unit(5),
                (stats1, 2, 3), (moments1, 2, 0), (normalise1, 2, 0), (normalise1, 2, 1),
            ])
            run(range(0, B + 1), [
                (x_lo, 1, 0), (normalise1, 1, 2), (x_lo, 1, 1), (normalise1, 1, 3), (normalise2, -1, 0), (normalise2, -1, 1),
                (x_lo, 1, 2), (stats1, 2, 0), (stats1, 2, 1), (x_lo, 1, 3), (normalise2, -1, 2), (stats1, 2, 2),
                (stats1, 2, 3), (normalise2, -1, 3), (moments1, 2, 0),
                (reciprocal, 0, 0), (rden_low, 0, 0), (q_low, 1, 0), (logit_gap, -1, 0), (q_low, 1, 1),
                (divide, 0, 0), (divide, 0, 1), (maxima, 1, 0), (q_low, 1, 2), (divide, 0, 2), (divide, 0, 3),
                (maxima, 1, 1), (q_low, 1, 3), (choose, -1, 0),
                (x1_tile, 0, 0), (maxima, 1, 2), (x1_tile, 0, 1), (maxima, 1, 3), (enter, -1, 0), (x1_tile, 0, 2),
                (normalise1, 2, 0), (normalise1, 2, 1), (x1_tile, 0, 3), (moments2, 0, 0), (add_table, -1, 0),
            ])

            e.wait_ge(s_tab, B)
            link(e.tensor_scalar(far[:, :], table[:, 0, :], 0.0, FAR, ALU.is_equal, ALU.mult))
            e.scalar_tensor_tensor(out=row_ix[:, :], in0=far[:, :], scalar=-1.0, in1=table[:, 0, :],
                                   op0=ALU.add, op1=ALU.add).then_inc(s_row, 1)
            e.tensor_scalar(coef[:, :], table[:, 1, :], tanh_g[0:CAP, 1:2], None, ALU.mult).then_inc(s_row, 1)
            for x_ in range(NE):
                e.wait_ge(s_ga[x_], 16)
                e.bn_stats(t_bn[:, x_, :], rows[:, x_, :]).then_inc(s_tbn, 1)
            for x_ in range(NE):
                e.wait_ge(s_tbn, x_ + 1)
                e.bn_aggr(t_mv[:, x_, :], t_bn[:, x_, :]).then_inc(s_tmv, 1)

            def row_norm(x_):
                e.wait_ge(s_trs, 1)
                e.wait_ge(s_tmv, NE)
                if x_ >= 2:
                    e.wait_ge(s_tt, x_ - 1)
                e.tensor_scalar(xn[0:CAP, x_ % 2, :], rows[:, x_, :], t_mv[:, x_, 0:1], t_rstd[:, x_:x_ + 1],
                                ALU.subtract, ALU.mult).then_inc(s_txn, 1)

            def row_lo(x_):
                e.wait_ge(s_thi, x_ + 1)
                if x_ >= 4:
                    e.wait_ge(s_tmm, x_ - 3)
                tok = slice((x_ % 4) * P, (x_ % 4) * P + CAP)
                bank = (g1_b, g0_b)[x_ % 2].rearrange("p (k s) -> p k s", k=NK)[:, :, 0:CAP]
                e.tensor_tensor(xnT_lo[:, :, tok], bank, xnT_hi[:, :, tok].bitcast(F32), ALU.subtract).then_inc(s_tlo, 1)

            def row_base(x_):
                e.wait_ge(s_txn, x_ + 1)
                e.wait_ge(s_row, 2)
                e.wait_ge(s_tail, 16)
                e.scalar_tensor_tensor(out=rows[:, x_, :], in0=rden[0:CAP, :], scalar=coef[:, x_:x_ + 1],
                                       in1=rows[:, x_, :], op0=ALU.mult, op1=ALU.add).then_inc(s_tb1, 1)

            def row_out(x_):
                e.wait_ge(s_tmm, x_ + 1)
                e.wait_ge(s_tb1, x_ + 1)
                e.scalar_tensor_tensor(out=rows[:, x_, :], in0=quad[0:CAP, x_ % 4, :], scalar=coef[:, x_:x_ + 1],
                                       in1=rows[:, x_, :], op0=ALU.mult, op1=ALU.add).then_inc(s_to, 1)

            row_norm(0)
            row_norm(1)
            row_lo(0)
            row_base(0)
            for x_ in range(NE):
                if x_ + 2 < NE:
                    row_norm(x_ + 2)
                if x_ + 1 < NE:
                    row_lo(x_ + 1)
                    row_base(x_ + 1)
                row_out(x_)

        @block.gpsimd
        def _(e):
            n = [0]

            def made_const(ins):
                n[0] += 1
                ins.then_inc(s_set, 1)

            made_const(e.memset(ident[:, :], 0.0))
            e.wait_ge(s_set, 1)
            made_const(e.affine_select(out=ident[:, :], in_=ident[:, :], compare_op=ALU.not_equal, fill=1.0,
                                       base=0, pattern=[[-1, P]], channel_multiplier=1))
            made_const(e.memset(neg_half[:, :], -0.5))
            made_const(e.memset(ones_col[:, :], 1.0))
            made_const(e.memset(tri[:, :], 1.0))
            e.wait_ge(s_set, 5)
            made_const(e.affine_select(out=tri[:, :], in_=tri[:, :], compare_op=ALU.is_ge, fill=0.0,
                                       base=0, pattern=[[1, P]], channel_multiplier=-1))
            made_const(e.memset(ones_bf[:, :], 1.0))
            made_const(e.iota(place_iota[:, :], pattern=[[1, CAP]], base=1, channel_multiplier=0,
                              allow_small_or_imprecise_dtypes=True))
            made_const(e.iota(token_iota[:, :], pattern=[[P, NT]], base=1, channel_multiplier=1,
                              allow_small_or_imprecise_dtypes=True))
            made_const(e.iota(rank8[:, :, :], pattern=[[0, NT], [-1, NE]], base=NE, channel_multiplier=0,
                              allow_small_or_imprecise_dtypes=True))
            made_const(e.memset(table[:, :, :], 0.0))
            made_const(e.memset(base_cnt[:, :, :, :], 0.0))
            made_const(e.memset(t_half[:, :], -0.5))
            assert n[0] == SET

            def rsqrt(slot, cols, done_mv, s_ve, s_rs, mean_var, tmp, dst, half_c):
                e.tensor_scalar(tmp, mean_var, EPS, None, ALU.add).then_inc(s_ve, 1)
                e.wait_ge(s_ve, done_mv)
                e.tensor_tensor(dst, tmp, half_c, ALU.pow).then_inc(s_rs, 1)

            def rstd1(b, _):
                e.wait_ge(s_mv1, 4 * b + 4)
                if b >= 2:
                    e.wait_ge(s_xn, 4 * (b - 1))
                rsqrt(0, NT, b + 1, s_ve1, s_rs1, mv[:, b % 2, :, 1], veps[:, b % 2, :], rstd[:, b % 2, :], neg_half[:, :])

            def rstd2(b, _):
                e.wait_ge(s_mv2, 4 * b + 4)
                e.wait_ge(s_x2n, 4 * b)
                rsqrt(2, NT, b + 1, s_ve2, s_rs2, mv[:, 2, :, 1], veps[:, 2, :], rstd[:, 2, :], neg_half[:, :])

            def sum_we(ex):
                e.wait_ge(*loaded(ex))
                if ex == 1:
                    e.wait_ge(*loaded(0))
                    first = slots[slot_of["we0"]]
                else:
                    e.wait_ge(s_ws, ex - 1)
                    first = w_sum[:, :, :]
                e.tensor_tensor(w_sum[:, :, :], first, slots[slot_of[f"we{ex}"]], ALU.add).then_inc(s_ws, 1)

            for ex in range(1, NE):
                sum_we(ex)
            rstd1(0, 0)

            def attn_low(b, g):
                e.wait_ge(s_ahi, 4 * b + g + 1)
                e.wait_ge(s_mix, 4 * b)
                if ok(b - 1):
                    e.wait_ge(s_lp, b)
                e.tensor_tensor(attn_lo[:, g, :], attn[:, g, :], attn_hi[:, g, :].bitcast(F32),
                                ALU.subtract).then_inc(s_alo, 1)

            def add_bias(b, _):
                e.wait_ge(s_setv, SETV)
                e.wait_ge(s_xn, 4 * b + 4)
                for t in range(NT):
                    row = xb[:, b % NX, t, :]
                    ins = e.tensor_tensor(row, row, mix_bias[:, :], ALU.add)
                ins.then_inc(s_xbias, 1)

            order = [
                (rstd2, -1, 0), (add_bias, 0, 0), (rstd1, 2, 0),
                (attn_low, 0, 0), (attn_low, 0, 1), (attn_low, 0, 2), (attn_low, 0, 3),
            ]
            run(range(-1, B), order)
            e.wait_ge(s_wehi, 1)
            for k in range(NK):
                e.tensor_tensor(wqT_lo[:, k, :], xb[:, B % NX, k, :], wqT_hi[:, k, :].bitcast(F32),
                                ALU.subtract).then_inc(s_welo, 1)
            run([B], order)

            e.wait_ge(s_val, 4 * B)
            e.memset(rows[:, :, :], 0.0).then_inc(s_clr, 1)
            e.wait_ge(s_clr, 1)
            e.wait_ge(s_st, 16 * B)
            e.wait_ge(s_row, 1)
            for x_ in range(NE):
                e.indirect_dma_start(
                    out=rows[:, x_, :], out_offset=None, in_=out_flat[:, :],
                    in_offset=bass.IndirectOffsetOnAxis(ap=row_ix[:, x_:x_ + 1], axis=0),
                    bounds_check=B * S - 1, oob_is_err=False).then_inc(s_ga[x_], 16)
            e.wait_ge(s_tmv, NE)
            rsqrt(0, NE, 1, s_tve, s_trs, t_mv[:, :, 1], t_ve[:, :], t_rstd[:, :], t_half[:, :])
            for x_ in range(NE):
                e.wait_ge(s_to, x_ + 1)
                e.indirect_dma_start(
                    out=out_flat[:, :], out_offset=bass.IndirectOffsetOnAxis(ap=row_ix[:, x_:x_ + 1], axis=0),
                    in_=rows[:, x_, :], in_offset=None,
                    bounds_check=B * S - 1, oob_is_err=False).then_inc(s_sca, 16)
            e.wait_ge(s_sca, 16 * NE)


_INS = ['x', 'ctx_1024', 'g_xattn', 'g_ffn', 'L0_xattn_Wq', 'L0_xattn_bq', 'L0_xattn_Wk', 'L0_xattn_bk',
        'L0_xattn_Wv', 'L0_xattn_bv', 'L0_xattn_We', 'L0_xattn_be', 'L0_xattn_Wo', 'L0_xattn_bo',
        'L0_ffn_w_gate', 'L0_ffn_w_expert', 'L0_ffn_b_expert']


def kernel(**inputs):
    import numpy as _np
    import concourse.bacc as _bacc
    from concourse import mybir as _mybir
    from concourse.bass_utils import run_bass_kernel_spmd as _run

    nc = _bacc.Bacc("TRN2", target_bir_lowering=False, num_devices=1)
    arrays, args = {}, []
    for name in _INS:
        a = _np.ascontiguousarray(inputs[name])
        arrays[f"in_{name}_dram"] = a
        args.append(nc.dram_tensor(f"in_{name}_dram", a.shape, _mybir.dt.from_np(a.dtype), kind="ExternalInput").ap())
    out = nc.dram_tensor("out_0_dram", (B, S, D), F32, kind="ExternalOutput").ap()
    build(nc, *args, out)
    r = _run(nc, [arrays], core_ids=[0])
    return r.results[0]["out_0_dram"]
```

```python
from contextlib import ExitStack

import concourse.bass as bass
from concourse import mybir

F32 = mybir.dt.float32
F32R = mybir.dt.float32r
F16 = mybir.dt.float16
BF16 = mybir.dt.bfloat16
U32 = mybir.dt.uint32
ALU = mybir.AluOpType
ACT = mybir.ActivationFunctionType
AX = mybir.AxisListType

P = 128
B, S, D = 8, 512, 512
SK = 120
H, DK = 16, 32
NE = 8
CAP = 100
NT = S // P
NK = D // P
HJ = P // DK
HALF = B // 2
QK_SCALE = 16.0
SHIFT_UNIT = 1024.0
EPS = 1e-5
NX = 4
STACK = 3 * DK + 1
ROW_GROUPS = ((0, 1), (2, 3, 4), (5, 6, 7))
ACT_STACKS = ((2, 0), (2, 1))
STACK_DMAS = 3 * HJ - len(ACT_STACKS)
FAR = 1.0e6


def build(nc, x, ctx, g_xattn, g_ffn, Wq, bq, Wk, bk, Wv, bv, We, be, Wo, bo, w_gate, w_expert, b_expert, out):
    assert x.shape == (B, S, D) and ctx.shape == (B, SK, D) and H * DK == D
    x_rows = x.rearrange("b (t p) d -> b p t d", p=P)
    out_rows = out.rearrange("b (t p) d -> b p t d", p=P)
    out_flat = out.rearrange("b s d -> (b s) d")
    k_scratch = nc.dram_tensor("k_scratch", (B, 3 * DK, HJ, NK * SK), F16, kind="Internal").ap()

    with ExitStack() as st:
        def sb(name, shape, dt):
            return st.enter_context(nc.sbuf_tensor(name, shape, dt))

        def sem(name):
            return st.enter_context(nc.semaphore(name))

        xb = sb("xb", [P, NX, NT, D], F32)
        wqT_hi = sb("wqT_hi", [P, NK, D], F32R)
        wqT_lo = sb("wqT_lo", [P, NK, D], F32R)
        mixT_hi = sb("mixT_hi", [P, NK, D], F32R)
        mixT_lo = sb("mixT_lo", [P, NK, D], F32R)
        with nc.sbuf_tensor("wkT_hi", [P, NK, D], F32R) as wkT_hi, nc.sbuf_tensor("wkT_lo", [P, NK, D], F32R) as wkT_lo:
            pass
        v_all = sb("v_all", [SK, B, D], F32)
        mix_bias = sb("mix_bias", [P, D], F32)
        ident = sb("ident", [P, P], F32)
        tri = sb("tri", [P, P], BF16)
        ones_bf = sb("ones_bf", [P, P], BF16)
        den_sel = sb("den_sel", [SK, NK, DK], F32)
        head_sel = sb("head_sel", [P, NK, P], F32R)
        gate_sum = sb("gate_sum", [P, NE], F32)
        wg = sb("wg", [P, NK, DK], F32)
        bias_rows = sb("bias_rows", [2 * NK, P], F32)
        bias_cols = sb("bias_cols", [P, 2 * NK], F32)
        gates = sb("gates", [P, 2], F32)
        tanh_g = sb("tanh_g", [P, 2], F32)
        mix_scale = sb("mix_scale", [P, 1], F32)
        neg_half = sb("neg_half", [P, NT], F32)
        t_half = sb("t_half", [CAP, NE], F32)
        ones_col = sb("ones_col", [P, 1], F32)
        place_iota = sb("place_iota", [P, CAP], F32)
        token_iota = sb("token_iota", [P, NT], F32)
        rank8 = sb("rank8", [P, NT, NE], F32)
        table = sb("table", [CAP, 2, NE], F32)
        base_cnt = sb("base_cnt", [P, 2, NT, NE], BF16)

        bn_raw = sb("bn_raw", [P, 2, NT, 6], F32)
        mv = sb("mv", [P, 3, NT, 2], F32)
        veps = sb("veps", [P, 3, NT], F32)
        rstd = sb("rstd", [P, 3, NT], F32)

        with ExitStack() as pro:
            def pb(name, shape, dt):
                return pro.enter_context(nc.sbuf_tensor(name, shape, dt))
            raw = [pb(f"raw{i}", [P, NK, D], F32) for i in range(3)]
            w_sum = pb("w_sum", [P, NK, D], F32)
            woT = pb("woT", [P, NK, D], F32)
            be_sb = pb("be_sb", [NE, D], F32)
            bo_bc = pb("bo_bc", [P, D], F32)
            be_col = pb("be_col", [P, NK], F32)
        probs = sb("probs", [SK, 2, HJ, S], F32)
        attn = sb("attn", [P, NK, S], F32)
        attn_hi = sb("attn_hi", [P, NK, S], F32R)
        with nc.sbuf_tensor("x2nT", [P, NK, S], F32) as x2nT:
            pass
        attn_lo = sb("attn_lo", [P, NK, S], F32R)
        rden = sb("rden", [P, S], F32)
        rden_hi = sb("rden_hi", [P, S], F32R)
        rden_lo = sb("rden_lo", [P, S], F32R)
        partT = sb("partT", [P, S], F32)
        with ExitStack() as pro:
            ctx_raw = pb("ctx_raw", [SK, B, D], F32)
            ctxT_hi = pb("ctxT_hi", [P, NK, B * SK], F32R)
            ctxT_lo = pb("ctxT_lo", [P, NK, B * SK], F32R)
            k_hi = pb("k_hi", [P, B, NK, SK], F16)
            k_lo = pb("k_lo", [P, B, NK, SK], F16)
            bv_bc = pb("bv_bc", [SK, D], F32)
        xn = sb("xn", [P, NT, D], F32)
        k_diag = sb("k_diag", [P, NK, HJ * SK], F16)
        k_stack = sb("k_stack", [P, 2, HJ, NK * SK], F16)
        xnT_hi = sb("xnT_hi", [P, NK, S], F32R)
        xnT_lo = sb("xnT_lo", [P, NK, S], F32R)
        q_hi = sb("q_hi", [P, NK, S], F16)
        q_lo = sb("q_lo", [P, NK, S], F16)
        q_stack = sb("q_stack", [P, HJ, NK, S], F16)
        neg_max = sb("neg_max", [P, NT, NK, HJ], F32)
        shift = sb("shift", [H, S], F16)
        l_max = sb("l_max", [P, NT], F32)
        l_sub = sb("l_sub", [P, NT, NE], F32)
        l_exp = sb("l_exp", [P, NT, NE], F32)
        ranked = sb("ranked", [P, NT, NE], F32)
        top_rank = sb("top_rank", [P, NT], F32)
        choice = sb("choice", [P, NT, NE], BF16)
        l_sum = sb("l_sum", [P, NT], F32)
        gate = sb("gate", [P, NT], F32)
        place_all = sb("place_all", [P, NT, NE], F32)
        place = sb("place", [P, NT], F32)
        place_hot = sb("place_hot", [P, NT, CAP], F32)
        token = sb("token", [P, NT], F32)
        entry = sb("entry", [P, NT, 2, NE], F32)
        rows = probs[0:CAP, :, :, :].rearrange("p a j s -> p (a j) s")
        row_n = xb[0:CAP, (B - 3) % NX, :, :]
        last_coef = sb("last_coef", [P, NT], F32)
        far = sb("far", [CAP, NE], F32)
        row_ix = sb("row_ix", [CAP, NE], U32)
        coef = sb("coef", [CAP, NE], F32)
        t_bn = sb("t_bn", [CAP, NE, 6], F32)
        t_mv = sb("t_mv", [CAP, NE, 2], F32)
        t_ve = sb("t_ve", [CAP, NE], F32)
        t_rstd = sb("t_rstd", [CAP, NE], F32)

        ps = st.enter_context(nc.psum_tensor("ps", [P, 8, 512], F32))
        quad = ps[:, 0:4, :]
        num_b, den_b, g0_b, g1_b = (ps[:, i, :] for i in range(4, 8))
        pair_b = (g1_b, g0_b)

        s_const = sem("s_const")
        s_bqk = sem("s_bqk")
        s_gates = sem("s_gates")
        s_set = sem("s_set")
        s_setv = sem("s_setv")
        s_tanh = sem("s_tanh")
        s_wt = {n: [sem(f"s_{n}{i}") for i in range(NK)] for n in ("wkT", "wvT", "wqT", "woT")}
        s_raw = [sem(f"s_raw{i}") for i in range(5)]
        s_ctx = [sem(f"s_ctx{i}") for i in range(B)]
        s_pt = sem("s_pt")
        s_pa = sem("s_pa")
        s_pv = sem("s_pv")
        s_ws = sem("s_ws")
        s_kst = sem("s_kst")
        s_x = [sem(f"s_xload{i}") for i in range(NX)]
        s_bn1 = sem("s_bn1")
        s_mv1 = sem("s_mv1")
        s_ve1 = sem("s_ve1")
        s_rs1 = sem("s_rs1")
        s_xn = sem("s_xn")
        s_xt = sem("s_xt")
        s_xhi = sem("s_xhi")
        s_xlo = sem("s_xlo")
        s_q = sem("s_q")
        s_qhi = sem("s_qhi")
        s_qlo = sem("s_qlo")
        s_ks = [sem(f"s_ks{i}") for i in range(2)]
        s_kd = sem("s_kd")
        s_ms = sem("s_ms")
        s_mx = sem("s_mx")
        s_mt = sem("s_mt")
        s_sh = sem("s_sh")
        s_rq = sem("s_rq")
        s_rsk = sem("s_rsk")
        s_rsh = sem("s_rsh")
        s_sc = sem("s_sc")
        s_ex = sem("s_ex")
        s_val = sem("s_val")
        s_num = sem("s_num")
        s_rec = sem("s_rec")
        s_rhi = sem("s_rhi")
        s_rlo = sem("s_rlo")
        s_bc = sem("s_bc")
        s_at = sem("s_at")
        s_ahi = sem("s_ahi")
        s_alo = sem("s_alo")
        s_mix = sem("s_mix")
        s_xbias = sem("s_xbias")
        s_x1 = sem("s_x1")
        s_st = sem("s_st")
        s_bn2 = sem("s_bn2")
        s_mv2 = sem("s_mv2")
        s_ve2 = sem("s_ve2")
        s_rs2 = sem("s_rs2")
        s_x2n = sem("s_x2n")
        s_x2t = sem("s_x2t")
        s_x2e = sem("s_x2e")
        s_lp = sem("s_lp")
        s_lpe = sem("s_lpe")
        s_lg = sem("s_lg")
        s_lsub = sem("s_lsub")
        s_lexp = sem("s_lexp")
        s_g = sem("s_g")
        s_ch = sem("s_ch")
        s_pl = sem("s_pl")
        s_plr = sem("s_plr")
        s_en = sem("s_en")
        s_tb = sem("s_tb")
        s_tab = sem("s_tab")
        s_tail = sem("s_tail")
        s_row = sem("s_row")
        s_clr = sem("s_clr")
        s_we = sem("s_we")
        s_wehi = sem("s_wehi")
        s_welo = sem("s_welo")
        s_ga = [sem(f"s_ga{e}") for e in range(NE)]
        s_tbn = sem("s_tbn")
        s_tmv = sem("s_tmv")
        s_tve = sem("s_tve")
        s_trs = sem("s_trs")
        s_txn = sem("s_txn")
        s_tt = sem("s_tt")
        s_thi = sem("s_thi")
        s_tlo = sem("s_tlo")
        s_tmm = sem("s_tmm")
        s_tb1 = sem("s_tb1")
        s_to = sem("s_to")
        s_sca = sem("s_sca")
        s_x2h = sem("s_x2h")
        s_x2l = sem("s_x2l")
        s_lm = sem("s_lm")
        s_lc = sem("s_lc")
        s_lb = sem("s_lb")
        s_lo = sem("s_lo")
        s_ls = sem("s_ls")

        SET, SETV, N_CONST = 13, 13, 3 + NK

        units, made, late = [], {}, []

        def unit(name, pe, needs=(), act=None, dve=None):
            n_act = sum(u["act"] is not None for u in units) + (act is not None)
            n_dve = sum(u["dve"] is not None for u in units) + (dve is not None)
            done = ([(s_pa, n_act)] if act else []) + ([(s_pv, n_dve)] if dve else [])
            i = len(units)
            if late:
                bank = (4, 5, 5, 4, 7)[i - late[0]]
                before = next(u["done"] for u in reversed(units) if u["bank_no"] == bank)
            else:
                bank, before = i % 8, units[i - 8]["done"] if i >= 8 else []
            units.append(dict(pe=pe, needs=list(needs), free=before, bank=ps[:, bank, :], bank_no=bank,
                              act=act, dve=dve, done=done))
            made[name] = done

        def needs_of(*names):
            return [w for n in names for w in made[n]]

        def copy_evac(i, dst, view):
            if i % 2 == 0:
                return dict(act=lambda e, b: e.activation(dst, view(b), ACT.Copy))
            return dict(dve=lambda e, b: e.tensor_copy(dst, view(b)))

        def pair_evac(hi, lo, view, scale):
            return dict(act=lambda e, b: e.activation(hi, view(b), ACT.Copy, scale=scale),
                        dve=lambda e, b: e.scalar_tensor_tensor(out=lo, in0=view(b), scalar=scale,
                                                                in1=hi.bitcast(F32), op0=ALU.mult, op1=ALU.subtract))

        def turn(src_of, n, cols, rows):
            def pe(e, b):
                for i in range(n):
                    ins = e.transpose(b[0:rows, i * cols:(i + 1) * cols], src_of(i), ident[0:cols, 0:cols])
                return ins
            return pe

        consts = [(s_set, 2)]

        unit("bias", turn(lambda i: bias_rows[:, :], 1, 2 * NK, P), consts + [(s_bqk, 16 * 2)],
             dve=lambda e, b: e.tensor_scalar(bias_cols[:, :], b[:, 0:2 * NK], QK_SCALE, None, ALU.mult))

        slots = [r_[:, :, :] for r_ in raw] + [xb[:, 2, :, :], xb[:, 3, :, :]]
        slot_of = {"wkT": 0, "wvT": 1, "wqT": 2, "woT": 3, "we0": 4,
                   "we1": 0, "we2": 1, "we3": 2, "we4": 3, "we5": 4, "we6": 0, "we7": 1}

        def loaded(ex):
            earlier = [n for n in range(ex + 1) if slot_of[f"we{n}"] == slot_of[f"we{ex}"]]
            return s_raw[slot_of[f"we{ex}"]], 16 * len(earlier)

        def ctx_unit(b_):
            unit(("ctxT", b_), turn(lambda i: ctx_raw[:, b_, i * P:(i + 1) * P], NK, SK, P),
                 consts + [(s_ctx[b_], 16)],
                 **pair_evac(ctxT_hi[:, :, b_ * SK:(b_ + 1) * SK], ctxT_lo[:, :, b_ * SK:(b_ + 1) * SK],
                             lambda b: b[:, 0:NK * SK].rearrange("p (k s) -> p k s", k=NK), 1.0))

        def weight_units(name, whole=None, pair=None, scale=1.0):
            for i in range(NK):
                pe = turn(lambda k, i=i: slots[slot_of[name]][:, i, k * P:(k + 1) * P], NK, P, P)
                cols = slice(i * P, (i + 1) * P)
                view = lambda b: b.rearrange("p (k s) -> p k s", k=NK)
                if pair is None:
                    evac = copy_evac(i, whole[:, :, cols], view)
                else:
                    evac = pair_evac(pair[0][:, :, cols], pair[1][:, :, cols], view, scale)
                unit((name, i), pe, consts + [(s_wt[name][i], 16)], **evac)

        def products3(e, out_, a, b):
            steps = [(k, pa, pb_) for k in range(NK) for pa, pb_ in ((0, 0), (0, 1), (1, 0))]
            for i, (k, pa, pb_) in enumerate(steps):
                ins = e.matmul(out_, a(pa, k), b(pb_, k), start=(i == 0), stop=(i == len(steps) - 1))
            return ins

        def k_units(half):
            lo_b, hi_b = half * HALF, (half + 1) * HALF
            for g in range(NK):
                def pe(e, b, g=g):
                    return products3(e, b[:, 0:HALF * SK],
                                     lambda p, k: (wkT_hi, wkT_lo)[p][:, k, g * P:(g + 1) * P],
                                     lambda p, k: (ctxT_hi, ctxT_lo)[p][:, k, lo_b * SK:hi_b * SK])
                unit(("k", half, g), pe,
                     needs_of(*[("wkT", k) for k in range(NK)], *[("ctxT", b_) for b_ in range(lo_b, hi_b)], "bias"),
                     act=lambda e, b, g=g: e.activation(
                         k_hi[:, lo_b:hi_b, g, :], b[:, 0:HALF * SK].rearrange("p (b s) -> p b s", s=SK),
                         ACT.Identity, bias=bias_cols[:, NK + g:NK + g + 1]),
                     dve=lambda e, b, g=g: e.scalar_tensor_tensor(
                         out=k_lo[:, lo_b:hi_b, g, :], in0=b[:, 0:HALF * SK].rearrange("p (b s) -> p b s", s=SK),
                         scalar=bias_cols[:, NK + g:NK + g + 1], in1=k_hi[:, lo_b:hi_b, g, :],
                         op0=ALU.add, op1=ALU.subtract))

        def v_unit(b_):
            def pe(e, b):
                return products3(e, b[0:SK, :], lambda p, k: (ctxT_hi, ctxT_lo)[p][:, k, b_ * SK:(b_ + 1) * SK],
                                 lambda p, k: (mixT_hi, mixT_lo)[p][:, k, :])
            unit(("v", b_), pe,
                 needs_of(*[("wvT", k) for k in range(NK)], ("ctxT", b_)) + [(s_const, 16 * N_CONST)],
                 dve=lambda e, b: e.tensor_tensor(v_all[:, b_, :], b[0:SK, :], bv_bc[:, :], ALU.add))

        def be_unit():
            def col(e, b):
                for k in range(NK):
                    ins = e.matmul(b[:, k:k + 1], be_sb[:, k * P:(k + 1) * P], ones_col[0:NE, :],
                                   start=True, stop=True)
                return ins
            unit("be_col", col, [(s_const, 16 * N_CONST), (s_set, 4)],
                 dve=lambda e, b: e.tensor_scalar(be_col[:, :], b[:, 0:NK], 1.0 / NE, None, ALU.mult))

        def mix_units():
            def row(e, b):
                for k in range(NK):
                    ins = e.matmul(b[:, :], be_col[:, k:k + 1].to_broadcast([P, P]), woT[:, k, :],
                                   start=(k == 0), stop=(k == NK - 1))
                return ins
            unit("mix_bias", row, needs_of("be_col", *[("woT", k) for k in range(NK)]) + [(s_const, 16 * N_CONST)],
                 dve=lambda e, b: e.tensor_tensor(mix_bias[:, :], b[:, :], bo_bc[:, :], ALU.add))
            for k in range(NK):
                def pe(e, b, k=k):
                    for o in range(NK):
                        ins = e.matmul(b[:, :], w_sum[:, o, k * P:(k + 1) * P], woT[:, o, :],
                                       start=(o == 0), stop=(o == NK - 1))
                    return ins
                unit(("mix", k), pe, needs_of(*[("woT", o) for o in range(NK)]) + [(s_ws, NE - 1)]
                     + ([(s_qhi, 3), (s_qlo, 3)] if k == NK - 1 else []),
                     act=lambda e, b, k=k: e.activation(mixT_hi[:, k, :], b, ACT.Copy, scale=mix_scale[:, 0:1]),
                     dve=lambda e, b, k=k: e.scalar_tensor_tensor(
                         out=mixT_lo[:, k, :], in0=b, scalar=mix_scale[:, 0:1], in1=mixT_hi[:, k, :].bitcast(F32),
                         op0=ALU.mult, op1=ALU.subtract))

        weight_units("wkT", pair=(wkT_hi, wkT_lo), scale=QK_SCALE)
        for b_ in range(HALF):
            ctx_unit(b_)
        k_units(0)
        for b_ in range(HALF, B):
            ctx_unit(b_)
        weight_units("wvT", pair=(mixT_hi, mixT_lo))
        k_units(1)
        weight_units("wqT", pair=(wqT_hi, wqT_lo), scale=QK_SCALE)
        weight_units("woT", whole=woT)
        be_unit()
        for b_ in range(B):
            v_unit(b_)
        N_FIRST = len(units)
        FIRST_ACT = sum(u["act"] is not None for u in units)
        FIRST_DVE = sum(u["dve"] is not None for u in units)
        late.append(N_FIRST)
        mix_units()
        N_LATE = len(units) - N_FIRST
        N_ACT = sum(u["act"] is not None for u in units)
        N_DVE = sum(u["dve"] is not None for u in units)
        last_turn = {n: 1 + max(i for i, u in enumerate(units) if u["done"] == made[(n, NK - 1)])
                     for n in ("wkT", "wvT", "wqT", "woT")}
        CTX_TURNED = 1 + max(i for i, u in enumerate(units) if u["done"] == made[("ctxT", B - 1)])
        last_k = {h: made[("k", h, NK - 1)] for h in range(2)}

        def first_units_over(e):
            e.wait_ge(s_pa, FIRST_ACT)
            e.wait_ge(s_pv, FIRST_DVE)
            e.wait_ge(s_kst, 16 * 2 * 3 * HJ)

        def prologue_over(e):
            e.wait_ge(s_pa, N_ACT)
            e.wait_ge(s_pv, N_DVE)

        def ok(b):
            return 0 <= b < B

        def run(over, order):
            for r in over:
                for step, ahead, arg in order:
                    if ok(r + ahead):
                        step(r + ahead, arg)

        tail_uses = [("row", 0), ("row", 1), ("row", 2), ("x2", 0), ("x2", 1), ("x2", 2), ("x2", 3), ("logits", 0),
                     ("row", 3), ("row", 4), ("row", 5), ("row", 6), ("row", 7)]

        def tail_bank(kind, i):
            return pair_b[tail_uses.index((kind, i)) % 2]

        def tail_bank_free(e, kind, i):
            n = tail_uses.index((kind, i))
            if n < 2:
                e.wait_ge(s_x1, 4 * (B - 1) + 3 + n)
                return
            kind, i = tail_uses[n - 2]
            if kind == "row":
                e.wait_ge(s_thi, i + 1)
                e.wait_ge(s_tlo, i + 1)
            elif kind == "x2":
                e.wait_ge(s_x2e, 4 * (B - 1) + i + 1)
                e.wait_ge(s_x2h, i + 1)
                e.wait_ge(s_x2l, i + 1)
            else:
                e.wait_ge(s_lpe, B)

        def places_bank(b):
            return pair_b[0] if b == B - 3 else den_b

        def table_bank(b):
            return pair_b[1] if b == B - 4 else pair_b[0] if b == B - 3 else num_b

        def x_bank(t):
            return pair_b[(0, 0, 1, 0)[t]]

        def x2_bank(b, t):
            return pair_b[(t + 1) % 2] if b < B - 1 else tail_bank("x2", t)

        def part_bank(b):
            return g0_b if b < B - 1 else tail_bank("logits", 0)

        block = st.enter_context(nc.Block())

        @block.sync
        def _(e):
            def load(dst, src, s):
                e.dma_start(dst, src).then_inc(s, 16)

            def w_view(w):
                return w.rearrange("(t p) d -> p t d", p=P)

            def load_tiles(n, w):
                for i in range(NK):
                    load(slots[slot_of[n]][:, i, :], w[i * P:(i + 1) * P, :], s_wt[n][i])

            load(bias_rows[0:NK, :], bq.rearrange("(t p) -> t p", p=P), s_bqk)
            load(bias_rows[NK:2 * NK, :], bk.rearrange("(t p) -> t p", p=P), s_bqk)
            load_tiles("wkT", Wk)
            for b_ in range(B):
                load(ctx_raw[:, b_, :], ctx[b_], s_ctx[b_])
            load(gates[:, 0:1], g_xattn.partition_broadcast(P), s_gates)
            load(gates[:, 1:2], g_ffn.partition_broadcast(P), s_gates)
            load_tiles("wvT", Wv)
            load_tiles("wqT", Wq)
            load(bv_bc[:, :], bv.partition_broadcast(SK), s_const)
            load(bo_bc[:, :], bo.partition_broadcast(P), s_const)
            load(be_sb[:, :], be, s_const)
            e.wait_ge(s_setv, 1)
            for k in range(NK):
                load(wg[:, k, 0:NE], w_gate[k * P:(k + 1) * P, :], s_const)
            load_tiles("woT", Wo)
            load(xb[:, 0, :, :], x_rows[0], s_x[0])
            for ex in range(NE):
                name, slot = f"we{ex}", slot_of[f"we{ex}"]
                names = list(slot_of)
                before = [n for n in names[:names.index(name)] if slot_of[n] == slot]
                if before:
                    n = before[-1]
                    if n in last_turn:
                        e.wait_ge(s_pt, last_turn[n])
                    else:
                        e.wait_ge(s_ws, max(1, int(n[2:])))
                load(slots[slot], w_view(We[ex]), s_raw[slot])
                if ex == 2:
                    load(xb[:, 1, :, :], x_rows[1], s_x[1])
            e.wait_ge(s_ws, 5)
            load(xb[:, 2, :, :], x_rows[2], s_x[2])

            first_units_over(e)
            e.wait_ge(s_setv, SETV - 1)
            for r in range(-1, B):
                if ok(r + 1):
                    slot = (r + 1) % 2
                    e.wait_ge(s_sc, 4 * max(0, r))
                    load(k_stack[0:3 * DK, slot, :, :], k_scratch[r + 1], s_ks[slot])
                    e.wait_ge(s_ms, 4 * (r + 1))
                    for j in range(HJ):
                        load(k_diag[j * DK:(j + 1) * DK, :, j * SK:(j + 1) * SK],
                             k_scratch[r + 1, 0:DK, j, :].rearrange("d (g s) -> d g s", g=NK), s_kd)
                if 1 <= r < B:
                    e.wait_ge(s_x1, 4 * r)
                    load(out_rows[r - 1], xb[:, (r - 1) % NX, :, :], s_st)
                if 0 <= r <= B - 3:
                    if ok(r - 1):
                        e.wait_ge(s_st, 16 * r)
                        e.wait_ge(s_x2n, 4 * r)
                    if ok(r + 3):
                        load(xb[:, (r + 3) % NX, :, :], x_rows[r + 3], s_x[(r + 3) % NX])
                    else:
                        load(xb[:, (r + 3) % NX, :, :], w_expert.rearrange("(k p) n -> p k n", p=P), s_we)
                if ok(r + 1):
                    e.wait_ge(s_sc, 4 * (r + 1))
                    e.wait_ge(s_qhi, 4 * (r + 2))
                    for part, src in ((0, q_hi), (2, q_hi), (1, q_lo)):
                        if part == 1:
                            e.wait_ge(s_qlo, 4 * (r + 2))
                        for j in range(HJ):
                            if (part, j) not in ACT_STACKS:
                                load(q_stack[part * DK:(part + 1) * DK, j, :, :], src[j * DK:(j + 1) * DK, :, :], s_rq)
                    e.wait_ge(s_sh, r + 2)
                    load(q_stack[3 * DK:STACK, :, :, :].rearrange("o j g s -> o (j g) s"),
                         shift[:, :], s_rsh)
            e.wait_ge(s_bc, 4 * B)
            e.wait_ge(s_rlo, B)
            e.wait_ge(s_rhi, B)
            load(rden[:, :], b_expert.partition_broadcast(P), s_tail)
            for t in range(NT):
                e.wait_ge(s_lo, t + 1)
                load(out_rows[B - 1][:, t, :], xb[:, (B - 1) % NX, t, :], s_ls)
            e.wait_ge(s_st, 16 * (B - 1))
            e.wait_ge(s_ls, 16 * NT)

        @block.tensor
        def _(e):
            def mm(out_, a, b, start=True, stop=True, **kw):
                return e.matmul(out_, a, b, start=start, stop=stop, **kw)

            def prepare(_, i):
                u = units[i]
                for s_, n in u["needs"] + u["free"]:
                    e.wait_ge(s_, n)
                u["pe"](e, u["bank"]).then_inc(s_pt, 1)

            for i in range(N_FIRST):
                prepare(0, i)
            e.wait_ge(s_set, SET)

            def parts3(bank, a_hi, a_lo, b_hi, b_lo, hi_wait=None, lo_wait=None, steps_of=slice(None)):
                steps = [(a_hi(k), b(k), hi_wait, k) for k in range(NK) for b in (b_hi, b_lo)]
                steps += [(a_lo(k), b_hi(k), lo_wait, k) for k in range(NK)]
                for i, (a, b, wait, k) in list(enumerate(steps))[steps_of]:
                    if wait:
                        e.wait_ge(wait[0], wait[1] + k + 1)
                    ins = mm(bank, a, b, start=(i == 0), stop=(i == len(steps) - 1))
                return ins

            def x_turn(b, t):
                if b == 0 and t == 0:
                    first_units_over(e)
                e.wait_ge(s_xn, 4 * b + t + 1)
                if t in (0, 2):
                    if ok(b - 2):
                        e.wait_ge(s_x1, 4 * (b - 2) + 3 + t // 2)
                    elif ok(b - 1):
                        e.wait_ge(s_qhi, 4 * b)
                        e.wait_ge(s_qlo, 4 * b)
                        for s_, n in made[("mix", NK - 1)]:
                            e.wait_ge(s_, n)
                if t % 2:
                    e.wait_ge(s_xhi, 4 * b + (t + 1) // 2)
                    e.wait_ge(s_xlo, 4 * b + (t + 1) // 2)
                for k in range(NK):
                    ins = e.transpose(x_bank(t)[:, k * P:(k + 1) * P], xn[:, t, k * P:(k + 1) * P], ident[:, :])
                ins.then_inc(s_xt, 1)

            def scores(b, g):
                if g == 0:
                    e.wait_ge(s_setv, SETV)
                    e.wait_ge(s_set, SET + 2)
                    e.wait_ge(s_rq, 16 * STACK_DMAS * (b + 1))
                    e.wait_ge(s_rsk, len(ACT_STACKS) * (b + 1))
                    e.wait_ge(s_rsh, 16 * (b + 1))
                    e.wait_ge(s_ks[b % 2], 16 * (b // 2 + 1))
                    e.wait_ge(s_mx, 4 * b + 4)
                else:
                    e.wait_ge(s_ex, 4 * b + g)
                for j in range(HJ):
                    ins = mm(quad[0:SK, j, :], k_stack[0:STACK, b % 2, j, g * SK:(g + 1) * SK],
                             q_stack[0:STACK, j, g, :])
                ins.then_inc(s_sc, 1)

            def values(b, g):
                e.wait_ge(s_ex, 4 * b + g + 1)
                if g == 0:
                    if b == 0:
                        prologue_over(e)
                    e.wait_ge(s_at, 4 * b)
                    e.wait_ge(s_sh, b + 1)
                else:
                    e.wait_ge(s_num, 4 * b + g)
                for j in range(HJ):
                    row = slice(j * DK, (j + 1) * DK)
                    col = g * P + j * DK
                    mm(num_b[row, :], v_all[:, b, col:col + DK], probs[:, g % 2, j, :])
                for j in range(HJ):
                    row = slice(j * DK, (j + 1) * DK)
                    ins = mm(den_b[row, :], den_sel[:, g, :], probs[:, g % 2, j, :], start=(g == 0), stop=(g == NK - 1))
                ins.then_inc(s_val, 1)

            def x2_turn(b, t):
                e.wait_ge(s_x2n, 4 * b + t + 1)
                if b == B - 1:
                    tail_bank_free(e, "x2", t)
                elif b == B - 2 and t < 2:
                    e.wait_ge(s_plr, B - 2)
                    e.wait_ge(s_tab, B - 3)
                elif t < 2:
                    if ok(b + 2):
                        e.wait_ge(s_xhi, 4 * (b + 2) + t + 3)
                        e.wait_ge(s_xlo, 4 * (b + 2) + t + 3)
                else:
                    e.wait_ge(s_x2e, 4 * b + t - 1)
                for k in range(NK):
                    ins = e.transpose(x2_bank(b, t)[:, k * P:(k + 1) * P], xn[:, t, k * P:(k + 1) * P], ident[:, :])
                ins.then_inc(s_x2t, 1)

            def partial_logits(b, _):
                e.wait_ge(s_x2e, 4 * b + 4)
                if b == B - 1:
                    tail_bank_free(e, "logits", 0)
                for k in range(NK):
                    ins = mm(part_bank(b)[k * DK:(k + 1) * DK, :], wg[:, k, :], x2nT[:, k, :])
                ins.then_inc(s_lp, 1)

            def logits(b, _):
                e.wait_ge(s_lpe, b + 1)
                if ok(b + 1):
                    e.wait_ge(s_num, 4 * (b + 1) + 4)
                else:
                    e.wait_ge(s_at, 4 * B)
                e.wait_ge(s_tab, max(0, b - 1) if b < B - 1 else B - 1)
                for t in range(NT):
                    ins = mm(num_b[:, t * NE:(t + 1) * NE], partT[:, t * P:(t + 1) * P], gate_sum[:, :])
                ins.then_inc(s_lg, 1)

            def q_tile(b, g):
                if g == 0:
                    e.wait_ge(s_xhi, 4 * b + 4)
                    e.wait_ge(s_xlo, 4 * b + 4)
                    if ok(b - 2):
                        e.wait_ge(s_x2e, 4 * (b - 2) + 4)
                elif g == 1:
                    if ok(b - 2):
                        e.wait_ge(s_lpe, b - 1)
                else:
                    e.wait_ge(s_qhi, 4 * b + g - 1)
                    e.wait_ge(s_qlo, 4 * b + g - 1)
                col = slice(g * P, (g + 1) * P)
                parts3(pair_b[g % 2], lambda k: wqT_hi[:, k, col], lambda k: wqT_lo[:, k, col],
                       lambda k: xnT_hi[:, k, :], lambda k: xnT_lo[:, k, :]).then_inc(s_q, 1)

            def max_scores(b, g):
                e.wait_ge(s_qhi, 4 * b + g + 1)
                if g:
                    e.wait_ge(s_mx, 4 * b + g)
                else:
                    e.wait_ge(s_kd, 16 * HJ * (b + 1))
                    e.wait_ge(s_ex, 4 * b)
                for t in range(NT):
                    ins = mm(quad[:, t, 0:HJ * SK], q_hi[:, g, t * P:(t + 1) * P], k_diag[:, g, :])
                ins.then_inc(s_ms, 1)

            def spread_rden(b, g):
                bank = (den_b, num_b)[g % 2]
                e.wait_ge(s_rhi, b + 1)
                e.wait_ge(s_rlo, b + 1)
                if g < 2:
                    e.wait_ge(s_num, 4 * b + 4)
                    if ok(b - 1):
                        e.wait_ge(s_lsub, b)
                else:
                    e.wait_ge(s_at, 4 * b + g - 1)
                mm(bank, head_sel[:, g, :], rden_hi[:, :], stop=False)
                mm(bank, head_sel[:, g, :], rden_lo[:, :], start=False).then_inc(s_bc, 1)

            def mix_steps(b, t, steps_of):
                tok = slice(t * P, (t + 1) * P)
                return parts3(pair_b[t % 2], lambda k: attn_hi[:, k, tok], lambda k: attn_lo[:, k, tok],
                              lambda k: mixT_hi[:, k, :], lambda k: mixT_lo[:, k, :],
                              (s_ahi, 4 * b), (s_alo, 4 * b), steps_of)

            def mix_high(b, t):
                if t < 2:
                    if ok(b + 1):
                        e.wait_ge(s_qhi, 4 * (b + 1) + t + 3)
                        e.wait_ge(s_qlo, 4 * (b + 1) + t + 3)
                    else:
                        e.wait_ge(s_x2e, 4 * b)
                        e.wait_ge(s_tab, B - 2)
                        e.wait_ge(s_lpe, b)
                else:
                    e.wait_ge(s_x1, 4 * b + t - 1)
                mix_steps(b, t, slice(0, 2 * NK))

            def mix_low(b, t):
                mix_steps(b, t, slice(2 * NK, 3 * NK)).then_inc(s_mix, 1)

            def max_turn(b, _):
                e.wait_ge(s_mx, 4 * b + 4)
                if ok(b - 1):
                    e.wait_ge(s_at, 4 * (b - 1) + 3)
                else:
                    for s_, n in made[("mix", 1)]:
                        e.wait_ge(s_, n)
                if ok(b - 3):
                    e.wait_ge(s_plr, b - 2)
                for t in range(NT):
                    ins = e.transpose(den_b[0:H, t * P:(t + 1) * P], neg_max[:, t, :, :], ident[:, :])
                ins.then_inc(s_mt, 1)

            def places(b, _):
                e.wait_ge(s_ch, b + 1)
                e.wait_ge(s_plr, b)
                if b == B - 3:
                    e.wait_ge(s_x1, 4 * (B - 1))
                else:
                    e.wait_ge(s_at, 4 * min(b + 2, B - 1) + 3)
                ch = choice[:, :, :].rearrange("p t e -> p (t e)")
                bank = places_bank(b)[:, 0:NT * NE]
                mm(bank, tri[:, :], ch, stop=False)
                mm(bank, ones_bf[:, :], base_cnt[:, b % 2, :, :].rearrange("p t e -> p (t e)"),
                   start=False).then_inc(s_pl, 1)

            def table_rows(b, _):
                e.wait_ge(s_en, b + 1)
                e.wait_ge(s_tab, b)
                if b < B - 4:
                    e.wait_ge(s_num, 4 * (b + 3) + 4)
                elif b == B - 4:
                    e.wait_ge(s_x1, 4 * (B - 1))
                elif b == B - 3:
                    e.wait_ge(s_x2e, 4 * (B - 2) + 4)
                else:
                    e.wait_ge(s_at, 4 * B)
                    e.wait_ge(s_lsub, B - 1)
                for t in range(NT):
                    ins = mm(table_bank(b)[0:CAP, 0:2 * NE], place_hot[:, t, :],
                             entry[:, t, :, :].rearrange("p w e -> p (w e)"), start=(t == 0), stop=(t == NT - 1))
                ins.then_inc(s_tb, 1)

            def late_unit(i):
                return prepare, 1, N_FIRST + i

            run([-1], [
                (x_turn, 1, 0), late_unit(0), (x_turn, 1, 1), (x_turn, 1, 2), (x_turn, 1, 3), late_unit(1),
                (q_tile, 1, 0), (q_tile, 1, 1), (max_scores, 1, 0), (q_tile, 1, 2), (max_scores, 1, 1),
                (q_tile, 1, 3), (max_scores, 1, 2), late_unit(2), (max_scores, 1, 3), late_unit(3), (max_turn, 1, 0),
                late_unit(4), (x_turn, 2, 0), (scores, 1, 0),
            ])
            run(range(0, B - 1), [
                (x_turn, 1, 1), (x_turn, 1, 2), (scores, 0, 1), (values, 0, 0), (x_turn, 1, 3),
                (scores, 0, 2), (values, 0, 1), (x2_turn, -1, 0), (x2_turn, -1, 1),
                (scores, 0, 3), (values, 0, 2), (x2_turn, -1, 2), (x2_turn, -1, 3), (values, 0, 3),
                (partial_logits, -1, 0), (table_rows, -3, 0), (q_tile, 1, 0), (logits, -1, 0), (q_tile, 1, 1),
                (spread_rden, 0, 0), (spread_rden, 0, 1), (max_scores, 1, 0), (q_tile, 1, 2),
                (spread_rden, 0, 2), (spread_rden, 0, 3), (max_scores, 1, 1), (q_tile, 1, 3),
                (mix_high, 0, 0), (max_scores, 1, 2), (mix_low, 0, 0), (places, -2, 0), (mix_high, 0, 1),
                (max_scores, 1, 3), (mix_low, 0, 1), (mix_high, 0, 2), (max_turn, 1, 0), (mix_low, 0, 2),
                (mix_high, 0, 3), (x_turn, 2, 0), (scores, 1, 0), (mix_low, 0, 3),
            ])
            run([B - 1], [
                (scores, 0, 1), (values, 0, 0), (scores, 0, 2), (values, 0, 1), (table_rows, -3, 0), (places, -2, 0),
                (x2_turn, -1, 0), (x2_turn, -1, 1), (scores, 0, 3), (values, 0, 2), (x2_turn, -1, 2),
                (values, 0, 3), (x2_turn, -1, 3), (table_rows, -2, 0),
                (partial_logits, -1, 0), (logits, -1, 0), (spread_rden, 0, 0), (spread_rden, 0, 1),
                (spread_rden, 0, 2), (spread_rden, 0, 3),
                (mix_high, 0, 0), (mix_low, 0, 0), (places, -1, 0), (mix_high, 0, 1), (mix_low, 0, 1),
                (table_rows, -1, 0), (mix_high, 0, 2), (mix_low, 0, 2), (mix_high, 0, 3), (mix_low, 0, 3),
            ])

            e.wait_ge(s_wehi, 1)
            e.wait_ge(s_welo, NK)

            def row_turn(_, x_):
                e.wait_ge(s_txn, x_ + 1)
                tail_bank_free(e, "row", x_)
                for k in range(NK):
                    ins = e.transpose(tail_bank("row", x_)[:, k * P:k * P + CAP], row_n[:, x_ % 4, k * P:(k + 1) * P],
                                      ident[0:CAP, 0:CAP])
                ins.then_inc(s_tt, 1)

            def row_product(_, x_):
                e.wait_ge(s_thi, x_ + 1)
                e.wait_ge(s_tlo, x_ + 1)
                if x_ >= 4:
                    e.wait_ge(s_to, x_ - 3)
                tok = slice((x_ % 4) * P, (x_ % 4) * P + CAP)
                parts3(quad[0:CAP, x_ % 4, :], lambda k: xnT_hi[:, k, tok], lambda k: xnT_lo[:, k, tok],
                       lambda k: wqT_hi[:, k, :], lambda k: wqT_lo[:, k, :]).then_inc(s_tmm, 1)

            def last_product(_, t):
                e.wait_ge(s_x2h, t + 1)
                e.wait_ge(s_x2l, t + 1)
                e.wait_ge(s_to, t + 5)
                tok = slice(t * P, (t + 1) * P)
                parts3(quad[:, t, :], lambda k: attn_hi[:, k, tok], lambda k: mixT_lo[:, k, tok],
                       lambda k: wqT_hi[:, k, :], lambda k: wqT_lo[:, k, :]).then_inc(s_lm, 1)

            run([B - 1], [
                (row_turn, 0, 0), (row_turn, 0, 1), (row_product, 0, 0), (row_turn, 0, 2), (x2_turn, 0, 0),
                (x2_turn, 0, 1), (row_product, 0, 1), (x2_turn, 0, 2), (x2_turn, 0, 3), (row_product, 0, 2),
                (partial_logits, 0, 0), (row_turn, 0, 3), (row_turn, 0, 4), (logits, 0, 0), (row_product, 0, 3),
                (row_turn, 0, 5), (row_product, 0, 4), (row_turn, 0, 6), (places, 0, 0), (row_product, 0, 5),
                (row_turn, 0, 7), (row_product, 0, 6), (row_product, 0, 7),
                (last_product, 0, 0), (last_product, 0, 1), (last_product, 0, 2), (last_product, 0, 3),
            ])

        @block.scalar
        def _(e):
            def act(out_, in_, func=ACT.Copy, **kw):
                return e.activation(out_, in_, func, **kw)

            def store_k(half):
                for s_, n in last_k[half]:
                    e.wait_ge(s_, n)
                for part, src in enumerate((k_hi, k_hi, k_lo)):
                    for j in range(HJ):
                        bs = slice(half * HALF, (half + 1) * HALF)
                        e.dma_start(k_scratch[bs, part * DK:(part + 1) * DK, j, :].rearrange("b d s -> d b s"),
                                    src[j * DK:(j + 1) * DK, bs, :, :].rearrange("d b g s -> d b (g s)")
                                    ).then_inc(s_kst, 16)

            def prepare(_, i):
                u = units[i]
                if u["act"] is not None:
                    e.wait_ge(s_pt, i + 1)
                    u["act"](e, u["bank"]).then_inc(s_pa, 1)

            for i in range(N_FIRST):
                prepare(0, i)
                for half in range(2):
                    if i >= 4 and units[i - 4]["done"] == made[("k", half, NK - 1)]:
                        store_k(half)
            e.wait_ge(s_gates, 16 * 2)
            act(tanh_g[:, :], gates[:, :], ACT.Tanh).then_inc(s_tanh, 1)
            e.wait_ge(s_tanh, 1)
            act(mix_scale[:, :], tanh_g[:, 0:1], scale=1.0 / NE).then_inc(s_tanh, 1)
            e.wait_ge(s_tanh, 2)
            first_units_over(e)

            def x_hi(b, t):
                e.wait_ge(s_xt, 4 * b + t + 1)
                e.wait_ge(s_q, 4 * b)
                act(xnT_hi[:, :, t * P:(t + 1) * P], x_bank(t).rearrange("p (k s) -> p k s", k=NK)).then_inc(s_xhi, 1)

            def rden_high(b, _):
                e.wait_ge(s_rec, b + 1)
                e.wait_ge(s_bc, 4 * b)
                act(rden_hi[:, :], rden[:, :]).then_inc(s_rhi, 1)

            def shift_row(b, _):
                e.wait_ge(s_mt, b + 1)
                e.wait_ge(s_rsh, 16 * b)
                act(shift[:, :], den_b[0:H, :], scale=1.0 / SHIFT_UNIT).then_inc(s_sh, 1)

            def attn_high(b, g):
                e.wait_ge(s_at, 4 * b + g + 1)
                e.wait_ge(s_mix, 4 * b)
                act(attn_hi[:, g, :], attn[:, g, :]).then_inc(s_ahi, 1)

            def exp(b, g):
                if b == 0 and g == 0:
                    prologue_over(e)
                e.wait_ge(s_sc, 4 * b + g + 1)
                e.wait_ge(s_val, max(0, 4 * b + g - 1))
                act(probs[:, g % 2, :, :], quad[0:SK, :, :], ACT.Exp,
                    scale=1.0 / (QK_SCALE * QK_SCALE * float(DK) ** 0.5)).then_inc(s_ex, 1)

            def q_high(b, g):
                e.wait_ge(s_q, 4 * b + g + 1)
                e.wait_ge(s_rq, 16 * STACK_DMAS * b)
                e.wait_ge(s_ms, 4 * b)
                act(q_hi[:, g, :], pair_b[g % 2], ACT.Identity, bias=bias_cols[:, g:g + 1]).then_inc(s_qhi, 1)

            def stack_q(b, i):
                part, j = ACT_STACKS[i]
                e.wait_ge(s_qhi, 4 * b + 4)
                e.wait_ge(s_sc, 4 * b)
                act(q_stack[part * DK:(part + 1) * DK, j, :, :],
                    q_hi[j * DK:(j + 1) * DK, :, :]).then_inc(s_rsk, 1)

            def value_out(b, g):
                e.wait_ge(s_val, 4 * b + g + 1)
                e.wait_ge(s_ahi, 4 * b)
                e.wait_ge(s_alo, 4 * b)
                act(attn[:, g, :], num_b).then_inc(s_num, 1)

            def x2_out(b, t):
                e.wait_ge(s_x2t, 4 * b + t + 1)
                e.wait_ge(s_mix, 4 * b + 4)
                act(x2nT[:, :, t * P:(t + 1) * P], x2_bank(b, t).rearrange("p (k s) -> p k s", k=NK)).then_inc(s_x2e, 1)

            def part_out(b, _):
                e.wait_ge(s_lp, b + 1)
                e.wait_ge(s_lg, b)
                act(partT[:, :], part_bank(b)).then_inc(s_lpe, 1)

            def gate_exp(b, _):
                e.wait_ge(s_lsub, b + 1)
                act(l_exp[:, :, :], l_sub[:, :, :], ACT.Exp).then_inc(s_lexp, 1)

            def expert_high(b, _):
                if b == B - 1:
                    e.wait_ge(s_we, 16)
                    e.wait_ge(s_q, 4 * B)
                    act(wqT_hi[:, :, :], xb[:, B % NX, :, :]).then_inc(s_wehi, 1)

            def row_high(_, x_):
                e.wait_ge(s_tt, x_ + 1)
                if x_ >= 4:
                    e.wait_ge(s_tmm, x_ - 3)
                act(xnT_hi[:, :, (x_ % 4) * P:(x_ % 4) * P + CAP],
                    tail_bank("row", x_).rearrange("p (k s) -> p k s", k=NK)[:, :, 0:CAP]).then_inc(s_thi, 1)

            def x2_high(b, t):
                e.wait_ge(s_x2t, 4 * b + t + 1)
                e.wait_ge(s_mix, 4 * B)
                act(attn_hi[:, :, t * P:(t + 1) * P],
                    tail_bank("x2", t).rearrange("p (k s) -> p k s", k=NK)).then_inc(s_x2h, 1)

            late_unit = lambda i: (prepare, 1, N_FIRST + i)
            run([-1], [
                (x_hi, 1, 0), (x_hi, 1, 1), (x_hi, 1, 2), (x_hi, 1, 3), late_unit(1), (q_high, 1, 0), (q_high, 1, 1),
                (q_high, 1, 2), (q_high, 1, 3), (stack_q, 1, 0), (stack_q, 1, 1), late_unit(2), late_unit(3),
                (shift_row, 1, 0), late_unit(4), (x_hi, 2, 0), (exp, 1, 0),
            ])
            run(range(0, B - 1), [
                (x_hi, 1, 1), (x_hi, 1, 2), (exp, 0, 1), (value_out, 0, 0), (x_hi, 1, 3),
                (exp, 0, 2), (value_out, 0, 1), (x2_out, -1, 0), (x2_out, -1, 1),
                (exp, 0, 3), (value_out, 0, 2), (x2_out, -1, 2), (x2_out, -1, 3), (value_out, 0, 3),
                (part_out, -1, 0), (rden_high, 0, 0), (q_high, 1, 0), (gate_exp, -1, 0), (q_high, 1, 1),
                (attn_high, 0, 0), (attn_high, 0, 1), (q_high, 1, 2), (attn_high, 0, 2), (attn_high, 0, 3),
                (q_high, 1, 3),
                (stack_q, 1, 0), (stack_q, 1, 1), (expert_high, 1, 0), (shift_row, 1, 0), (x_hi, 2, 0), (exp, 1, 0),
            ])
            run([B - 1], [
                (exp, 0, 1), (value_out, 0, 0), (exp, 0, 2), (value_out, 0, 1), (x2_out, -1, 0), (x2_out, -1, 1),
                (exp, 0, 3), (value_out, 0, 2), (x2_out, -1, 2), (value_out, 0, 3), (x2_out, -1, 3),
                (part_out, -1, 0), (rden_high, 0, 0), (gate_exp, -1, 0), (attn_high, 0, 0), (attn_high, 0, 1),
                (attn_high, 0, 2), (attn_high, 0, 3),
                (row_high, 0, 0), (row_high, 0, 1), (row_high, 0, 2), (x2_out, 0, 0), (x2_high, 0, 0),
                (x2_out, 0, 1), (x2_high, 0, 1), (x2_out, 0, 2), (x2_high, 0, 2), (x2_out, 0, 3), (x2_high, 0, 3),
                (part_out, 0, 0), (row_high, 0, 3), (row_high, 0, 4), (gate_exp, 0, 0),
                (row_high, 0, 5), (row_high, 0, 6), (row_high, 0, 7),
            ])

        @block.vector
        def _(e):
            e.memset(wg[:, :, :], 0.0).then_inc(s_setv, 1)
            e.memset(den_sel[:, :, :], 0.0).then_inc(s_setv, 1)
            e.wait_ge(s_setv, 2)
            for g in range(NK):
                e.memset(den_sel[:, g, g::NK], 1.0).then_inc(s_setv, 1)
            e.wait_ge(s_set, 2)
            for g in range(NK):
                e.tensor_copy(head_sel[:, g, :].rearrange("p (j d) -> p j d", d=DK),
                              ident[:, g::DK].unsqueeze(2).to_broadcast([P, HJ, DK])).then_inc(s_setv, 1)
            e.tensor_reduce(gate_sum[:, :], ident[:, :].rearrange("p (k c) -> p c k", k=NK)[:, 0:NE, :],
                            AX.X, ALU.add).then_inc(s_setv, 1)

            def stats1(b, t):
                e.wait_ge(s_x[b % NX], 16 * (b // NX + 1))
                if b:
                    e.wait_ge(s_mv1, 4 * b)
                e.bn_stats(bn_raw[:, 0, t, :], xb[:, b % NX, t, :]).then_inc(s_bn1, 1)

            def moments1(b, _):
                for t in range(NT):
                    e.wait_ge(s_bn1, 4 * b + t + 1)
                    e.bn_aggr(mv[:, b % 2, t, :], bn_raw[:, 0, t, :]).then_inc(s_mv1, 1)

            def prepare(_, i):
                u = units[i]
                if u["dve"] is not None:
                    e.wait_ge(s_pt, i + 1)
                    if u["act"] is not None:
                        e.wait_ge(*u["done"][0])
                    u["dve"](e, u["bank"]).then_inc(s_pv, 1)

            def normalise1(b, t):
                e.wait_ge(s_rs1, b + 1)
                e.wait_ge(s_mv1, 4 * b + 4)
                if ok(b - 3):
                    e.wait_ge(s_x2t, 4 * (b - 3) + t + 1)
                if ok(b - 1):
                    e.wait_ge(s_xt, 4 * (b - 1) + t + 1)
                e.tensor_scalar(xn[:, t, :], xb[:, b % NX, t, :], mv[:, b % 2, t, 0:1], rstd[:, b % 2, t:t + 1],
                                ALU.subtract, ALU.mult).then_inc(s_xn, 1)

            for i in range(N_FIRST):
                prepare(0, i)
                if units[i]["done"] == made[("v", 1)]:
                    for t in range(NT):
                        stats1(0, t)
                    moments1(0, 0)
                if units[i]["done"] == made[("v", 5)]:
                    e.wait_ge(s_pt, CTX_TURNED)
                    e.memset(k_diag[:, :, :], 0.0).then_inc(s_setv, 1)
                    for t in range(NT):
                        normalise1(0, t)
            first_units_over(e)

            def scale_bias(_, __):
                e.wait_ge(s_tanh, 2)
                e.wait_ge(*made["mix_bias"][0])
                e.tensor_scalar(mix_bias[:, :], mix_bias[:, :], tanh_g[:, 0:1], None, ALU.mult).then_inc(s_setv, 1)

            def x_lo(b, t):
                e.wait_ge(s_xhi, 4 * b + t + 1)
                tok = slice(t * P, (t + 1) * P)
                e.tensor_tensor(xnT_lo[:, :, tok], x_bank(t).rearrange("p (k s) -> p k s", k=NK),
                                xnT_hi[:, :, tok].bitcast(F32), ALU.subtract).then_inc(s_xlo, 1)

            def reciprocal(b, _):
                e.wait_ge(s_val, 4 * b + 4)
                e.wait_ge(s_rhi, b)
                e.wait_ge(s_rlo, b)
                e.reciprocal(rden[:, :], den_b).then_inc(s_rec, 1)

            def rden_low(b, _):
                e.wait_ge(s_rhi, b + 1)
                e.wait_ge(s_rec, b + 1)
                e.tensor_tensor(rden_lo[:, :], rden[:, :], rden_hi[:, :].bitcast(F32), ALU.subtract).then_inc(s_rlo, 1)

            def divide(b, g):
                e.wait_ge(s_bc, 4 * b + g + 1)
                e.tensor_tensor(attn[:, g, :], (den_b, num_b)[g % 2], attn[:, g, :], ALU.mult).then_inc(s_at, 1)

            def x1_tile(b, t):
                e.wait_ge(s_mix, 4 * b + t + 1)
                e.wait_ge(s_xbias, b + 1)
                row = xb[:, b % NX, t, :]
                e.tensor_tensor(row, pair_b[t % 2], row, ALU.add).then_inc(s_x1, 1)

            def stats2(b, t):
                e.wait_ge(s_x1, 4 * b + t + 1)
                e.wait_ge(s_mv2, 4 * b)
                e.bn_stats(bn_raw[:, 1, t, :], xb[:, b % NX, t, :]).then_inc(s_bn2, 1)

            def moments2(b, _):
                e.wait_ge(s_x2n, 4 * b)
                for t in range(NT):
                    e.wait_ge(s_bn2, 4 * b + t + 1)
                    e.bn_aggr(mv[:, 2, t, :], bn_raw[:, 1, t, :]).then_inc(s_mv2, 1)

            def normalise2(b, t):
                e.wait_ge(s_rs2, b + 1)
                e.wait_ge(s_mv2, 4 * b + 4)
                if ok(b - 1):
                    e.wait_ge(s_x2t, 4 * (b - 1) + t + 1)
                e.wait_ge(s_xt, 4 * min(b + 2, B - 1) + t + 1)
                e.tensor_scalar(xn[:, t, :], xb[:, b % NX, t, :], mv[:, 2, t, 0:1], rstd[:, 2, t:t + 1],
                                ALU.subtract, ALU.mult).then_inc(s_x2n, 1)

            def q_low(b, g):
                e.wait_ge(s_qhi, 4 * b + g + 1)
                e.scalar_tensor_tensor(out=q_lo[:, g, :], in0=pair_b[g % 2], scalar=bias_cols[:, g:g + 1],
                                       in1=q_hi[:, g, :], op0=ALU.add, op1=ALU.subtract).then_inc(s_qlo, 1)

            def maxima(b, g):
                e.wait_ge(s_ms, 4 * b + g + 1)
                e.wait_ge(s_mt, b)
                e.tensor_reduce(neg_max[:, :, g, :], quad[:, :, 0:HJ * SK].rearrange("p t (j s) -> p t j s", j=HJ),
                                AX.X, ALU.max, negate=True).then_inc(s_mx, 1)

            steps = [0]

            def link(ins):
                steps[0] += 1
                ins.then_inc(s_g, 1)
                e.wait_ge(s_g, steps[0])

            def wide(a):
                return a.unsqueeze(2).to_broadcast([P, NT, NE])

            def logit_gap(b, _):
                e.wait_ge(s_lg, b + 1)
                lg = num_b[:, 0:NT * NE].rearrange("p (t e) -> p t e", e=NE)
                link(e.tensor_reduce(l_max[:, :], lg, AX.X, ALU.max))
                e.tensor_tensor(l_sub[:, :, :], lg, wide(l_max[:, :]), ALU.subtract).then_inc(s_lsub, 1)

            def choose(b, _):
                e.wait_ge(s_lsub, b + 1)
                flat = "p t e -> p (t e)"
                link(e.scalar_tensor_tensor(out=ranked[:, :, :].rearrange(flat), in0=l_sub[:, :, :].rearrange(flat),
                                            scalar=0.0, in1=rank8[:, :, :].rearrange(flat),
                                            op0=ALU.is_equal, op1=ALU.mult))
                link(e.tensor_reduce(top_rank[:, :], ranked[:, :, :], AX.X, ALU.max))
                link(e.tensor_tensor(choice[:, :, :], ranked[:, :, :], wide(top_rank[:, :]), ALU.is_equal))
                for t in range(NT):
                    nxt = base_cnt[:, b % 2, t + 1, :] if t + 1 < NT else base_cnt[:, (b + 1) % 2, 0, :]
                    link(e.tensor_tensor(nxt, base_cnt[:, b % 2, t, :], choice[:, t, :], ALU.add))
                e.wait_ge(s_lexp, b + 1)
                link(e.tensor_reduce(l_sum[:, :], l_exp[:, :, :], AX.X, ALU.add))
                e.reciprocal(gate[:, :], l_sum[:, :]).then_inc(s_ch, 1)

            def read_places(b, _):
                e.wait_ge(s_pl, b + 1)
                e.wait_ge(s_ch, b + 1)
                pl = places_bank(b)[:, 0:NT * NE].rearrange("p (t e) -> p t e", e=NE)
                e.tensor_tensor(place_all[:, :, :], pl, choice[:, :, :], ALU.mult).then_inc(s_plr, 1)
                e.wait_ge(s_plr, b + 1)
                link(e.tensor_reduce(place[:, :], place_all[:, :, :], AX.X, ALU.add))

            def enter(b, _):
                e.wait_ge(s_ch, b + 1)
                e.wait_ge(s_tb, b)
                for t in range(NT):
                    e.tensor_scalar(place_hot[:, t, :], place_iota[:, :], place[:, t:t + 1], None, ALU.is_equal)
                link(e.tensor_scalar(token[:, :], token_iota[:, :], float(b * S), None, ALU.add))
                e.tensor_tensor(entry[:, :, 0, :], choice[:, :, :], wide(token[:, :]), ALU.mult)
                e.tensor_tensor(entry[:, :, 1, :], choice[:, :, :], wide(gate[:, :]), ALU.mult).then_inc(s_en, 1)

            def add_table(b, _):
                e.wait_ge(s_tb, b + 1)
                e.wait_ge(s_tab, b)
                flat = "p w e -> p (w e)"
                tab = table[:, :, :].rearrange(flat)
                e.tensor_tensor(tab, table_bank(b)[0:CAP, 0:2 * NE], tab, ALU.add).then_inc(s_tab, 1)

            late_unit = lambda i: (prepare, 1, N_FIRST + i)
            run([-1], [
                (x_lo, 1, 0), late_unit(0), (x_lo, 1, 1), (x_lo, 1, 2), (x_lo, 1, 3), late_unit(1), (scale_bias, 1, 0),
                (q_low, 1, 0), (q_low, 1, 1), (maxima, 1, 0), (stats1, 2, 0), (stats1, 2, 1), (q_low, 1, 2),
                (maxima, 1, 1), (q_low, 1, 3), (maxima, 1, 2), late_unit(2), (maxima, 1, 3),
                (stats1, 2, 2), (stats1, 2, 3), (moments1, 2, 0), late_unit(3), (normalise1, 2, 0), late_unit(4),
                (normalise1, 2, 1), (normalise1, 2, 2), (x_lo, 2, 0), (normalise1, 2, 3),
            ])
            run(range(0, B - 1), [
                (x_lo, 1, 1), (x_lo, 1, 2), (stats2, -1, 2), (stats2, -1, 3), (moments2, -1, 0), (enter, -3, 0),
                (x_lo, 1, 3), (normalise2, -1, 0), (normalise2, -1, 1), (normalise2, -1, 2),
                (normalise2, -1, 3), (choose, -2, 0), (stats1, 2, 0), (stats1, 2, 1), (stats1, 2, 2), (stats1, 2, 3),
                (moments1, 2, 0),
                (reciprocal, 0, 0), (add_table, -3, 0), (rden_low, 0, 0), (q_low, 1, 0), (logit_gap, -1, 0),
                (q_low, 1, 1), (divide, 0, 0), (divide, 0, 1), (maxima, 1, 0), (q_low, 1, 2), (divide, 0, 2),
                (divide, 0, 3), (maxima, 1, 1), (q_low, 1, 3),
                (maxima, 1, 2), (x1_tile, 0, 0), (read_places, -2, 0), (maxima, 1, 3), (x1_tile, 0, 1),
                (stats2, 0, 0), (stats2, 0, 1), (x1_tile, 0, 2), (normalise1, 2, 0),
                (normalise1, 2, 1), (normalise1, 2, 2), (x_lo, 2, 0), (x1_tile, 0, 3), (normalise1, 2, 3),
            ])

            def row_index(_, __):
                e.wait_ge(s_tab, B - 1)
                link(e.tensor_scalar(far[:, :], table[:, 0, :], 0.0, FAR, ALU.is_equal, ALU.mult))
                e.scalar_tensor_tensor(out=row_ix[:, :], in0=far[:, :], scalar=-1.0, in1=table[:, 0, :],
                                       op0=ALU.add, op1=ALU.add).then_inc(s_row, 1)
                e.tensor_scalar(coef[:, :], table[:, 1, :], tanh_g[0:CAP, 1:2], None, ALU.mult).then_inc(s_row, 1)

            def row_stats(_, n):
                for x_ in ROW_GROUPS[n]:
                    e.wait_ge(s_ga[x_], 16)
                    e.bn_stats(t_bn[:, x_, :], rows[:, x_, :]).then_inc(s_tbn, 1)
                for x_ in ROW_GROUPS[n]:
                    e.wait_ge(s_tbn, x_ + 1)
                    e.bn_aggr(t_mv[:, x_, :], t_bn[:, x_, :]).then_inc(s_tmv, 1)

            def row_norm(_, x_):
                n = 1 + [x_ in group for group in ROW_GROUPS].index(True)
                e.wait_ge(s_trs, n)
                e.wait_ge(s_tmv, ROW_GROUPS[n - 1][-1] + 1)
                if x_ >= 4:
                    e.wait_ge(s_tt, x_ - 3)
                e.tensor_scalar(row_n[:, x_ % 4, :], rows[:, x_, :], t_mv[:, x_, 0:1], t_rstd[:, x_:x_ + 1],
                                ALU.subtract, ALU.mult).then_inc(s_txn, 1)

            def row_lo(_, x_):
                e.wait_ge(s_thi, x_ + 1)
                if x_ >= 4:
                    e.wait_ge(s_tmm, x_ - 3)
                tok = slice((x_ % 4) * P, (x_ % 4) * P + CAP)
                bank = tail_bank("row", x_).rearrange("p (k s) -> p k s", k=NK)[:, :, 0:CAP]
                e.tensor_tensor(xnT_lo[:, :, tok], bank, xnT_hi[:, :, tok].bitcast(F32),
                                ALU.subtract).then_inc(s_tlo, 1)

            def row_base(_, x_):
                e.wait_ge(s_txn, x_ + 1)
                e.wait_ge(s_row, 2)
                e.wait_ge(s_tail, 16)
                e.scalar_tensor_tensor(out=rows[:, x_, :], in0=rden[0:CAP, :], scalar=coef[:, x_:x_ + 1],
                                       in1=rows[:, x_, :], op0=ALU.mult, op1=ALU.add).then_inc(s_tb1, 1)

            def row_out(_, x_):
                e.wait_ge(s_tmm, x_ + 1)
                e.wait_ge(s_tb1, x_ + 1)
                e.scalar_tensor_tensor(out=rows[:, x_, :], in0=quad[0:CAP, x_ % 4, :], scalar=coef[:, x_:x_ + 1],
                                       in1=rows[:, x_, :], op0=ALU.mult, op1=ALU.add).then_inc(s_to, 1)

            def x2_lo(_, t):
                e.wait_ge(s_x2h, t + 1)
                tok = slice(t * P, (t + 1) * P)
                e.tensor_tensor(mixT_lo[:, :, tok], tail_bank("x2", t).rearrange("p (k s) -> p k s", k=NK),
                                attn_hi[:, :, tok].bitcast(F32), ALU.subtract).then_inc(s_x2l, 1)

            def last_coefs(b, _):
                e.wait_ge(s_ch, b + 1)
                e.scalar_tensor_tensor(out=last_coef[:, :], in0=place[:, :], scalar=CAP + 0.5, in1=gate[:, :],
                                       op0=ALU.is_lt, op1=ALU.mult).then_inc(s_lc, 1)
                e.wait_ge(s_lc, 1)
                e.tensor_scalar(last_coef[:, :], last_coef[:, :], tanh_g[:, 1:2], None, ALU.mult).then_inc(s_lc, 1)

            def last_base(b, t):
                e.wait_ge(s_lc, 2)
                e.wait_ge(s_tail, 16)
                e.wait_ge(s_x2n, 4 * b + t + 1)
                row = xb[:, b % NX, t, :]
                e.scalar_tensor_tensor(out=row, in0=rden[:, :], scalar=last_coef[:, t:t + 1], in1=row,
                                       op0=ALU.mult, op1=ALU.add).then_inc(s_lb, 1)

            def last_out(b, t):
                e.wait_ge(s_lm, t + 1)
                e.wait_ge(s_lb, t + 1)
                row = xb[:, b % NX, t, :]
                e.scalar_tensor_tensor(out=row, in0=quad[:, t, :], scalar=last_coef[:, t:t + 1], in1=row,
                                       op0=ALU.mult, op1=ALU.add).then_inc(s_lo, 1)

            run([B - 1], [
                (stats2, -1, 2), (stats2, -1, 3), (moments2, -1, 0), (enter, -3, 0), (normalise2, -1, 0),
                (normalise2, -1, 1), (choose, -2, 0), (normalise2, -1, 2), (normalise2, -1, 3),
                (add_table, -3, 0), (read_places, -2, 0), (enter, -2, 0),
                (reciprocal, 0, 0), (add_table, -2, 0), (rden_low, 0, 0), (logit_gap, -1, 0), (divide, 0, 0),
                (divide, 0, 1), (divide, 0, 2), (divide, 0, 3), (choose, -1, 0), (x1_tile, 0, 0),
                (read_places, -1, 0), (enter, -1, 0), (x1_tile, 0, 1), (add_table, -1, 0), (row_index, 0, 0),
                (stats2, 0, 0), (stats2, 0, 1), (x1_tile, 0, 2), (stats2, 0, 2), (row_stats, 0, 0), (x1_tile, 0, 3),
                (stats2, 0, 3), (moments2, 0, 0),
                (row_norm, 0, 0), (row_norm, 0, 1), (normalise2, 0, 0), (row_lo, 0, 0), (normalise2, 0, 1),
                (row_lo, 0, 1), (normalise2, 0, 2), (normalise2, 0, 3), (row_stats, 0, 1), (row_norm, 0, 2),
                (row_base, 0, 0), (row_lo, 0, 2), (x2_lo, 0, 0), (row_out, 0, 0), (x2_lo, 0, 1),
                (row_norm, 0, 3), (row_norm, 0, 4), (row_stats, 0, 2), (row_base, 0, 1), (x2_lo, 0, 2), (x2_lo, 0, 3),
                (row_out, 0, 1), (row_base, 0, 2), (row_norm, 0, 5), (row_lo, 0, 3), (row_lo, 0, 4), (row_out, 0, 2),
                (logit_gap, 0, 0), (row_base, 0, 3), (row_lo, 0, 5), (row_norm, 0, 6), (row_out, 0, 3),
                (choose, 0, 0), (row_norm, 0, 7), (row_base, 0, 4), (row_lo, 0, 6), (row_out, 0, 4),
                (read_places, 0, 0), (last_coefs, 0, 0), (row_base, 0, 5), (row_lo, 0, 7), (row_out, 0, 5),
                (row_base, 0, 6), (last_base, 0, 0), (row_out, 0, 6), (row_base, 0, 7), (last_base, 0, 1),
                (row_out, 0, 7), (last_base, 0, 2), (last_base, 0, 3),
                (last_out, 0, 0), (last_out, 0, 1), (last_out, 0, 2), (last_out, 0, 3),
            ])

        @block.gpsimd
        def _(e):
            n = [0]

            def made_const(ins):
                n[0] += 1
                ins.then_inc(s_set, 1)

            made_const(e.memset(ident[:, :], 0.0))
            e.wait_ge(s_set, 1)
            made_const(e.affine_select(out=ident[:, :], in_=ident[:, :], compare_op=ALU.not_equal, fill=1.0,
                                       base=0, pattern=[[-1, P]], channel_multiplier=1))
            made_const(e.memset(neg_half[:, :], -0.5))
            made_const(e.memset(ones_col[:, :], 1.0))
            made_const(e.memset(tri[:, :], 1.0))
            e.wait_ge(s_set, 5)
            made_const(e.affine_select(out=tri[:, :], in_=tri[:, :], compare_op=ALU.is_ge, fill=0.0,
                                       base=0, pattern=[[1, P]], channel_multiplier=-1))
            made_const(e.memset(ones_bf[:, :], 1.0))
            made_const(e.iota(place_iota[:, :], pattern=[[1, CAP]], base=1, channel_multiplier=0,
                              allow_small_or_imprecise_dtypes=True))
            made_const(e.iota(token_iota[:, :], pattern=[[P, NT]], base=1, channel_multiplier=1,
                              allow_small_or_imprecise_dtypes=True))
            made_const(e.iota(rank8[:, :, :], pattern=[[0, NT], [-1, NE]], base=NE, channel_multiplier=0,
                              allow_small_or_imprecise_dtypes=True))
            made_const(e.memset(table[:, :, :], 0.0))
            made_const(e.memset(base_cnt[:, :, :, :], 0.0))
            made_const(e.memset(t_half[:, :], -0.5))
            assert n[0] == SET

            def rsqrt(done_mv, s_ve, s_rs, mean_var, tmp, dst, half_c):
                e.tensor_scalar(tmp, mean_var, EPS, None, ALU.add).then_inc(s_ve, 1)
                e.wait_ge(s_ve, done_mv)
                e.tensor_tensor(dst, tmp, half_c, ALU.pow).then_inc(s_rs, 1)

            def rstd1(b, _):
                e.wait_ge(s_mv1, 4 * b + 4)
                if b >= 2:
                    e.wait_ge(s_xn, 4 * (b - 1))
                rsqrt(b + 1, s_ve1, s_rs1, mv[:, b % 2, :, 1], veps[:, b % 2, :], rstd[:, b % 2, :], neg_half[:, :])

            def rstd2(b, _):
                e.wait_ge(s_mv2, 4 * b + 4)
                e.wait_ge(s_x2n, 4 * b)
                rsqrt(b + 1, s_ve2, s_rs2, mv[:, 2, :, 1], veps[:, 2, :], rstd[:, 2, :], neg_half[:, :])

            def sum_we(ex):
                e.wait_ge(*loaded(ex))
                if ex == 1:
                    e.wait_ge(*loaded(0))
                    first = slots[slot_of["we0"]]
                else:
                    e.wait_ge(s_ws, ex - 1)
                    first = w_sum[:, :, :]
                e.tensor_tensor(w_sum[:, :, :], first, slots[slot_of[f"we{ex}"]], ALU.add).then_inc(s_ws, 1)

            for ex in range(1, NE):
                sum_we(ex)
                if ex == 4:
                    rstd1(0, 0)
            first_units_over(e)
            e.wait_ge(s_ws, NE - 1)
            for i in range(2):
                made_const(e.memset(k_stack[3 * DK:STACK, i, :, :], SHIFT_UNIT))
                e.wait_ge(s_set, n[0])

            def attn_low(b, g):
                e.wait_ge(s_ahi, 4 * b + g + 1)
                e.wait_ge(s_mix, 4 * b)
                if ok(b - 1):
                    e.wait_ge(s_lp, b)
                e.tensor_tensor(attn_lo[:, g, :], attn[:, g, :], attn_hi[:, g, :].bitcast(F32),
                                ALU.subtract).then_inc(s_alo, 1)

            def add_bias(b, _):
                e.wait_ge(s_setv, SETV)
                e.wait_ge(s_xn, 4 * b + 4)
                for t in range(NT):
                    row = xb[:, b % NX, t, :]
                    ins = e.tensor_tensor(row, row, mix_bias[:, :], ALU.add)
                ins.then_inc(s_xbias, 1)

            def expert_low(b, _):
                e.wait_ge(s_wehi, 1)
                for k in range(NK):
                    e.tensor_tensor(wqT_lo[:, k, :], xb[:, B % NX, k, :], wqT_hi[:, k, :].bitcast(F32),
                                    ALU.subtract).then_inc(s_welo, 1)

            def clear_rows(b, _):
                e.wait_ge(s_val, 4 * B)
                e.memset(rows[:, :, :], 0.0).then_inc(s_clr, 1)

            attn_lows = [(attn_low, 0, g) for g in range(NK)]
            run(range(-1, B - 1), [(rstd2, -1, 0), (add_bias, 0, 0), (rstd1, 2, 0)] + attn_lows)
            run([B - 1], [(rstd2, -1, 0), (add_bias, 0, 0), (expert_low, 0, 0), (clear_rows, 0, 0)] + attn_lows)

            e.wait_ge(s_clr, 1)
            e.wait_ge(s_st, 16 * (B - 1))
            e.wait_ge(s_row, 1)

            def gather(x_):
                e.indirect_dma_start(
                    out=rows[:, x_, :], out_offset=None, in_=out_flat[0:(B - 1) * S, :],
                    in_offset=bass.IndirectOffsetOnAxis(ap=row_ix[:, x_:x_ + 1], axis=0),
                    bounds_check=(B - 1) * S - 1, oob_is_err=False).then_inc(s_ga[x_], 16)

            def row_rstd(n):
                group = slice(ROW_GROUPS[n][0], ROW_GROUPS[n][-1] + 1)
                e.wait_ge(s_tmv, group.stop)
                rsqrt(n + 1, s_tve, s_trs, t_mv[:, group, 1], t_ve[:, group], t_rstd[:, group], t_half[:, group])

            for x_ in range(4):
                gather(x_)
            row_rstd(0)
            gather(4)
            rstd2(B - 1, 0)
            for x_ in range(5, NE):
                gather(x_)
            row_rstd(1)
            row_rstd(2)
            for x_ in range(NE):
                e.wait_ge(s_to, x_ + 1)
                e.indirect_dma_start(
                    out=out_flat[0:(B - 1) * S, :],
                    out_offset=bass.IndirectOffsetOnAxis(ap=row_ix[:, x_:x_ + 1], axis=0),
                    in_=rows[:, x_, :], in_offset=None,
                    bounds_check=(B - 1) * S - 1, oob_is_err=False).then_inc(s_sca, 16)
            e.wait_ge(s_sca, 16 * NE)


_INS = ['x', 'ctx_1024', 'g_xattn', 'g_ffn', 'L0_xattn_Wq', 'L0_xattn_bq', 'L0_xattn_Wk', 'L0_xattn_bk',
        'L0_xattn_Wv', 'L0_xattn_bv', 'L0_xattn_We', 'L0_xattn_be', 'L0_xattn_Wo', 'L0_xattn_bo',
        'L0_ffn_w_gate', 'L0_ffn_w_expert', 'L0_ffn_b_expert']


def kernel(**inputs):
    import numpy as _np
    import concourse.bacc as _bacc
    from concourse import mybir as _mybir
    from concourse.bass_utils import run_bass_kernel_spmd as _run

    nc = _bacc.Bacc("TRN2", target_bir_lowering=False, num_devices=1)
    arrays, args = {}, []
    for name in _INS:
        a = _np.ascontiguousarray(inputs[name])
        arrays[f"in_{name}_dram"] = a
        args.append(nc.dram_tensor(f"in_{name}_dram", a.shape, _mybir.dt.from_np(a.dtype), kind="ExternalInput").ap())
    out = nc.dram_tensor("out_0_dram", (B, S, D), F32, kind="ExternalOutput").ap()
    build(nc, *args, out)
    r = _run(nc, [arrays], core_ids=[0])
    return r.results[0]["out_0_dram"]
```
